# Optimizing a Trainium2 kernel written in Bass

```python
import numpy as np
import jax
import jax.numpy as jnp

def _softmax(x, axis=-1):
    return jax.nn.softmax(x, axis=axis)

def _gelu(x):
    return jax.nn.gelu(x, approximate=True)

def _silu(x):
    return jax.nn.silu(x)

def _sigmoid(x):
    return jax.nn.sigmoid(x)

def _layernorm(x, axis=-1, eps=1e-05):
    m = jnp.mean(x, axis=axis, keepdims=True)
    v = jnp.var(x, axis=axis, keepdims=True)
    return (x - m) / jnp.sqrt(v + eps)

def _scatter_add(tgt, idx, src, axis=0):
    return tgt.at[idx].add(src)

def _segment_sum(src, seg, n):
    return jax.ops.segment_sum(src, seg, n)
kernel_name = 'mk_adaln_d1_jaxref_r8_81ff59'

def setup_inputs(seed: int=0):
    np.random.seed(seed)
    _w = jnp.asarray

    def _L0_attn_setup():
        import jax, jax.numpy as jnp
        import numpy as np
        DIM = 128
        NUM_HEADS = 16
        HEAD_DIM = DIM // NUM_HEADS
        key = jax.random.key(seed)
        k1, k2, k3 = jax.random.split(key, 3)
        B, T = (2, 256)
        x = jax.random.normal(k1, (B, T, DIM), dtype=jnp.float32)
        w_qkv = jax.random.normal(k2, (3 * DIM, DIM), dtype=jnp.float32) * (1.0 / np.sqrt(DIM))
        w_out = jax.random.normal(k3, (DIM, DIM), dtype=jnp.float32) * (1.0 / np.sqrt(DIM))
        return {'x': x, 'w_qkv': w_qkv, 'w_out': w_out}
    _L0_attn_in = _L0_attn_setup()

    def _L0_ffn_setup():
        import jax, jax.numpy as jnp
        import numpy as np
        DIM, HEADS, FFN, E = (128, 16, 512, 8)
        B, S = (2, 128)
        EPS = 1e-05

        def _ln(x, g, b):
            mu = jnp.mean(x, axis=-1, keepdims=True)
            var = jnp.mean((x - mu) ** 2, axis=-1, keepdims=True)
            return (x - mu) * jax.lax.rsqrt(var + EPS) * g + b
        key = jax.random.key(seed)
        ks = jax.random.split(key, 20)
        sd = 0.02
        d, f = (DIM, FFN)
        return {'x': jax.random.normal(ks[0], (B, S, d), jnp.float32), 'ln1_g': jnp.ones((d,), jnp.float32), 'ln1_b': jnp.zeros((d,), jnp.float32), 'Wqkv': jax.random.normal(ks[1], (d, 3 * d), jnp.float32) * sd, 'bqkv': jnp.zeros((3 * d,), jnp.float32), 'Wo': jax.random.normal(ks[2], (d, d), jnp.float32) * sd, 'bo': jnp.zeros((d,), jnp.float32), 'ln2_g': jnp.ones((d,), jnp.float32), 'ln2_b': jnp.zeros((d,), jnp.float32), 'gate_w': jax.random.normal(ks[3], (d, E), jnp.float32) * sd, 'W1': jax.random.normal(ks[4], (E, d, f), jnp.float32) * sd, 'b1': jnp.zeros((E, f), jnp.float32), 'W2': jax.random.normal(ks[5], (E, f, d), jnp.float32) * sd, 'b2': jnp.zeros((E, d), jnp.float32), 'rW1': jax.random.normal(ks[6], (d, f), jnp.float32) * sd, 'rb1': jnp.zeros((f,), jnp.float32), 'rW2': jax.random.normal(ks[7], (f, d), jnp.float32) * sd, 'rb2': jnp.zeros((d,), jnp.float32), 'coef_w': jax.random.normal(ks[8], (d, 2), jnp.float32) * sd, 'coef_b': jnp.zeros((2,), jnp.float32)}
    _L0_ffn_in = _L0_ffn_setup()
    _L0_c = _w((lambda *s: np.random.randn(*s).astype(np.float32) * 0.05)(8, 128))
    _L0_wmod = _w((lambda *s: np.random.randn(*s).astype(np.float32) * 0.05)(128, 6 * 128) * 128 ** (-0.5))
    _d = {'L0_attn_x': _L0_attn_in['x'], 'L0_attn_w_qkv': _L0_attn_in['w_qkv'], 'L0_attn_w_out': _L0_attn_in['w_out'], 'L0_ffn_ln1_g': _L0_ffn_in['ln1_g'], 'L0_ffn_ln1_b': _L0_ffn_in['ln1_b'], 'L0_ffn_Wqkv': _L0_ffn_in['Wqkv'], 'L0_ffn_bqkv': _L0_ffn_in['bqkv'], 'L0_ffn_Wo': _L0_ffn_in['Wo'], 'L0_ffn_bo': _L0_ffn_in['bo'], 'L0_ffn_ln2_g': _L0_ffn_in['ln2_g'], 'L0_ffn_ln2_b': _L0_ffn_in['ln2_b'], 'L0_ffn_gate_w': _L0_ffn_in['gate_w'], 'L0_ffn_W1': _L0_ffn_in['W1'], 'L0_ffn_b1': _L0_ffn_in['b1'], 'L0_ffn_W2': _L0_ffn_in['W2'], 'L0_ffn_b2': _L0_ffn_in['b2'], 'L0_ffn_rW1': _L0_ffn_in['rW1'], 'L0_ffn_rb1': _L0_ffn_in['rb1'], 'L0_ffn_rW2': _L0_ffn_in['rW2'], 'L0_ffn_rb2': _L0_ffn_in['rb2'], 'L0_ffn_coef_w': _L0_ffn_in['coef_w'], 'L0_ffn_coef_b': _L0_ffn_in['coef_b'], 'L0_c': _L0_c, 'L0_wmod': _L0_wmod}
    _x0 = _d['L0_attn_x']
    _d['L0_attn_x'] = jax.random.normal(jax.random.fold_in(jax.random.key(seed), 1), (8, 512, 128), dtype=_x0.dtype)
    del _x0
    return _d

def reference(L0_attn_x, L0_attn_w_qkv, L0_attn_w_out, L0_ffn_ln1_g, L0_ffn_ln1_b, L0_ffn_Wqkv, L0_ffn_bqkv, L0_ffn_Wo, L0_ffn_bo, L0_ffn_ln2_g, L0_ffn_ln2_b, L0_ffn_gate_w, L0_ffn_W1, L0_ffn_b1, L0_ffn_W2, L0_ffn_b2, L0_ffn_rW1, L0_ffn_rb1, L0_ffn_rW2, L0_ffn_rb2, L0_ffn_coef_w, L0_ffn_coef_b, L0_c, L0_wmod):

    def _L0_attn_ref(x, w_qkv, w_out):
        import jax, jax.numpy as jnp
        import numpy as np
        DIM = 128
        NUM_HEADS = 16
        HEAD_DIM = DIM // NUM_HEADS
        B, T, C = x.shape
        H, D = (NUM_HEADS, HEAD_DIM)
        qkv = jnp.einsum('btc,fc->btf', x, w_qkv)
        qkv = qkv.reshape(B, T, 3, H, D).transpose(2, 0, 3, 1, 4)
        q, k, v = (qkv[0], qkv[1], qkv[2])
        scale = 1.0 / np.sqrt(D)
        scores = jnp.einsum('bhtd,bhsd->bhts', q, k) * scale
        causal = jnp.tril(jnp.ones((T, T), dtype=bool))
        scores = jnp.where(causal, scores, -jnp.inf)
        attn = jax.nn.softmax(scores, axis=-1)
        out = jnp.einsum('bhts,bhsd->bhtd', attn, v)
        out = out.transpose(0, 2, 1, 3).reshape(B, T, C)
        return jnp.einsum('btc,oc->bto', out, w_out)

    def _L0_ffn_ref(x, ln1_g, ln1_b, Wqkv, bqkv, Wo, bo, ln2_g, ln2_b, gate_w, W1, b1, W2, b2, rW1, rb1, rW2, rb2, coef_w, coef_b):
        import jax, jax.numpy as jnp
        import numpy as np
        DIM, HEADS, FFN, E = (128, 16, 512, 8)
        B, S = (2, 128)
        EPS = 1e-05

        def _ln(x, g, b):
            mu = jnp.mean(x, axis=-1, keepdims=True)
            var = jnp.mean((x - mu) ** 2, axis=-1, keepdims=True)
            return (x - mu) * jax.lax.rsqrt(var + EPS) * g + b
        b, s, d = x.shape
        h, dh = (HEADS, d // HEADS)
        xn = _ln(x, ln1_g, ln1_b)
        qkv = xn @ Wqkv + bqkv
        q, k, v = jnp.split(qkv, 3, axis=-1)
        q = q.reshape(b, s, h, dh)
        k = k.reshape(b, s, h, dh)
        v = v.reshape(b, s, h, dh)
        scores = jnp.einsum('bqhd,bkhd->bhqk', q, k) / jnp.sqrt(jnp.float32(dh))
        attn = jax.nn.softmax(scores, axis=-1)
        ctx = jnp.einsum('bhqk,bkhd->bqhd', attn, v).reshape(b, s, d)
        x = x + ctx @ Wo + bo
        xn2 = _ln(x, ln2_g, ln2_b)
        xt = xn2.reshape(b * s, d)
        probs = jax.nn.softmax(xt @ gate_w, axis=-1)
        gate_val = jnp.max(probs, axis=-1, keepdims=True)
        expert_idx = jnp.argmax(probs, axis=-1)
        oh = jax.nn.one_hot(expert_idx, E, dtype=xt.dtype)
        xe = jnp.einsum('te,td->etd', oh, xt)
        he = jax.nn.gelu(jnp.einsum('etd,edf->etf', xe, W1) + b1[:, None, :], approximate=False)
        ye = jnp.einsum('etf,efd->etd', he, W2) + b2[:, None, :]
        moe_out = jnp.einsum('te,etd->td', oh, ye) * gate_val
        rm = jax.nn.gelu(xt @ rW1 + rb1, approximate=False) @ rW2 + rb2
        coef = jax.nn.softmax(xt @ coef_w + coef_b, axis=-1)
        ff = moe_out * coef[:, 0:1] + rm * coef[:, 1:2]
        return x + ff.reshape(b, s, d)
    x = L0_attn_x
    mod = (_silu(L0_c) @ L0_wmod).reshape(L0_c.shape[0], 6, 1, -1)
    sa, ca, ga, sb, cb, gb = (mod[:, 0], mod[:, 1], mod[:, 2], mod[:, 3], mod[:, 4], mod[:, 5])
    ga = (2 * (ga >= 0) - 1) * jnp.maximum(jnp.abs(ga), 0.25)
    gb = (2 * (gb >= 0) - 1) * jnp.maximum(jnp.abs(gb), 0.25)
    h = _layernorm(x, axis=-1) * (1 + ca) + sa
    x = x + ga * _L0_attn_ref(h, L0_attn_w_qkv, L0_attn_w_out)
    h = _layernorm(x, axis=-1) * (1 + cb) + sb
    x = x + gb * _L0_ffn_ref(h, L0_ffn_ln1_g, L0_ffn_ln1_b, L0_ffn_Wqkv, L0_ffn_bqkv, L0_ffn_Wo, L0_ffn_bo, L0_ffn_ln2_g, L0_ffn_ln2_b, L0_ffn_gate_w, L0_ffn_W1, L0_ffn_b1, L0_ffn_W2, L0_ffn_b2, L0_ffn_rW1, L0_ffn_rb1, L0_ffn_rW2, L0_ffn_rb2, L0_ffn_coef_w, L0_ffn_coef_b)
    return x

_drawn_inputs = setup_inputs


def setup_inputs(seed=0):
    import zlib

    import numpy as np

    out = dict(_drawn_inputs(seed))
    spreads = {'L0_ffn_ln1_g': (1.0, 0.6),
     'L0_ffn_ln1_b': (0.0, 0.8),
     'L0_ffn_bqkv': (0.0, 0.8),
     'L0_ffn_bo': (0.0, 0.33),
     'L0_ffn_ln2_g': (1.0, 0.6),
     'L0_ffn_ln2_b': (0.0, 0.8),
     'L0_ffn_b1': (0.0, 0.8),
     'L0_ffn_b2': (0.0, 0.8),
     'L0_ffn_rb1': (0.0, 0.8),
     'L0_ffn_rb2': (0.0, 0.702),
     'L0_ffn_coef_b': (0.0, 0.8)}
    factors = {'L0_ffn_Wqkv': 8.0,
     'L0_ffn_Wo': 8.0,
     'L0_ffn_gate_w': 8.0,
     'L0_ffn_W1': 8.0,
     'L0_ffn_W2': 8.0,
     'L0_ffn_rW1': 8.0,
     'L0_ffn_rW2': 7.684,
     'L0_ffn_coef_w': 8.0}
    for name, (base, spread) in spreads.items():
        noise = np.random.default_rng([zlib.crc32(name.encode()), seed]).standard_normal(out[name].shape)
        drawn = base * np.exp(spread * noise) if base else spread * noise
        out[name] = jnp.asarray(drawn.astype(out[name].dtype))
    for name, factor in factors.items():
        out[name] = (out[name] * factor).astype(out[name].dtype)
    return out
```

```python
from contextlib import ExitStack

import concourse.bass as bass
from concourse import mybir

F32 = mybir.dt.float32
BF16 = mybir.dt.bfloat16
I32 = mybir.dt.int32
ACT = mybir.ActivationFunctionType
ALU = mybir.AluOpType
AX = mybir.AxisListType

P = 128
B, T, C = 8, 512, 128
H, D = 16, 8
TB = T // P
NT = B * TB
E, F = 8, 512
FT = F // P
EPS = 1e-5
SCALE = float(D) ** -0.5
BIG = 3.0e38
NG = 4
HG = H // NG
UN = NG * TB
Q_PARTS = (0, 0, 0, 1, 1, 2)
K_PARTS = (0, 1, 2, 0, 1, 0)
NR = len(Q_PARTS)
KS_ROWS = NR * D
NX = NT + E
KT_ROWS = KS_ROWS + 3


class Tensors:
    pass


def head_of(g, i):
    par, p = i % 2, 2 * g + i // 2
    return par * (H // 2) + p


def load_and_tables(nc, k, a, banks):
    with ExitStack() as ctx:
        def sb(name, shape, dt=F32):
            return ctx.enter_context(nc.sbuf_tensor(name, shape, dt))

        def sem(name):
            return ctx.enter_context(nc.semaphore(name))

        wqk_nat = sb("wqk_nat", [P, 3, C])
        wout_nat = sb("wout_nat", [P, C])
        wout_perm = sb("wout_perm", [P, C])
        wqkv2 = sb("wqkv2", [P, 3 * C])
        b1_nat = sb("b1_nat", [E * FT, P])
        rb1_nat = sb("rb1_nat", [FT, P])
        bqk_nat = sb("bqk_nat", [2, C])
        bqk_perm = sb("bqk_perm", [2, C])
        ln1_nat = sb("ln1_nat", [2, C])
        c_nat = sb("c_nat", [B, C])
        c_exp = sb("c_exp", [B, C])
        c_one = sb("c_one", [B, C])
        c_rec = sb("c_rec", [B, C])
        c_silu = sb("c_silu", [B, C])
        siluT = sb("siluT", [P, B])
        silu_bc = sb("silu_bc", [P, B, P])
        wmod = sb("wmod", [P, 6 * C])
        gabs = sb("gabs", [P, B, C])
        gsgn = sb("gsgn", [P, B, C])
        gneg = sb("gneg", [P, B, C])

        x_in = sem("lt_x_in")
        c_in = sem("lt_c_in")
        w_in = sem("lt_w_in")
        consts0 = sem("lt_consts0")
        ident_ok = sem("lt_ident_ok")
        exp_ok = sem("lt_exp_ok")
        chain = sem("lt_chain")
        silu_ok = sem("lt_silu_ok")
        siluT_ps = sem("lt_siluT_ps")
        siluT_ok = sem("lt_siluT_ok")
        mod_ps = sem("lt_mod_ps")
        br_ps = sem("lt_br_ps")
        br_ok = sem("lt_br_ok")
        wt_ps = sem("lt_wt_ps")
        perm_ok = sem("lt_perm_ok")
        wt_free = sem("lt_wt_free")

        block = ctx.enter_context(nc.Block())

        @block.sync
        def _(sp):
            sp.dma_start(c_nat[:, :], a["L0_c"]).then_inc(c_in, 16)
            sp.dma_start(wmod[:, :], a["L0_wmod"]).then_inc(c_in, 16)
            xv = a["L0_attn_x"].rearrange("b (t p) c -> p (b t) c", p=P)
            for b in range(B):
                sp.dma_start(k.X[:, TB * b:TB * b + TB, :], xv[:, TB * b:TB * b + TB, :]).then_inc(x_in, 16)
            for part in range(2):
                wv = a["L0_attn_w_qkv"][part * C:part * C + C, :].rearrange(
                    "(par half p d) c -> half par d p c", par=2, half=2, d=D)
                for half in range(2):
                    for par in range(2):
                        r = (2 * half + par) * 32
                        sp.dma_start(wqk_nat[r:r + 32, part, :], wv[half, par]).then_inc(w_in, 16)
            sp.dma_start(wqk_nat[:, 2, :], a["L0_attn_w_qkv"][2 * C:3 * C, :]).then_inc(w_in, 16)
            sp.dma_start(wout_nat[:, :], a["L0_attn_w_out"]).then_inc(w_in, 16)
            sp.dma_start(wqkv2[:, :], a["L0_ffn_Wqkv"]).then_inc(w_in, 16)
            sp.dma_start(b1_nat[:, :], a["L0_ffn_b1"].rearrange("e (t f) -> (e t) f", f=P)).then_inc(w_in, 16)
            sp.dma_start(rb1_nat[:, :], a["L0_ffn_rb1"].rearrange("(t f) -> t f", f=P)).then_inc(w_in, 16)
            for g in range(NG):
                for i in range(HG):
                    h = head_of(g, i)
                    r = g * 32 + i * D
                    sp.dma_start(k.wo2[r:r + D, :], a["L0_ffn_Wo"][h * D:h * D + D, :]).then_inc(w_in, 16)
            sp.dma_start(bqk_nat[:, :], a["L0_ffn_bqkv"][0:2 * C].rearrange("(s c) -> s c", c=C)).then_inc(w_in, 16)
            for row, name in enumerate(("L0_ffn_ln1_g", "L0_ffn_ln1_b")):
                sp.dma_start(ln1_nat[row:row + 1, :], a[name].rearrange("(o c) -> o c", o=1)).then_inc(w_in, 16)
            sp.dma_start(k.bv2[:, :], a["L0_ffn_bqkv"][2 * C:3 * C].partition_broadcast(P)).then_inc(w_in, 16)
            for dst, name in ((k.bo_bc, "L0_ffn_bo"), (k.g2_bc, "L0_ffn_ln2_g"), (k.b2_bc, "L0_ffn_ln2_b"),
                              (k.rb2_bc, "L0_ffn_rb2")):
                sp.dma_start(dst[:, :], a[name].partition_broadcast(P)).then_inc(w_in, 16)
            n = 2 * 4 + 1 + 1 + 1 + 1 + 1 + H + 1 + 2 + 1 + 4
            sp.wait_ge(w_in, 16 * n)
            sp.wait_ge(x_in, 16 * B)

        N_W = 16 * (2 * 4 + 1 + 1 + 1 + 1 + 1 + H + 1 + 2 + 1 + 4)

        @block.gpsimd
        def _(pool):
            pool.memset(k.ident[:, :], 0.0).then_inc(consts0, 1)
            pool.memset(k.cmask[:, :], 0.0).then_inc(consts0, 1)
            pool.memset(k.zcol[:, :], 0.0).then_inc(ident_ok, 1)
            pool.wait_ge(consts0, 2)
            pool.affine_select(out=k.ident[:, :], in_=k.ident[:, :], compare_op=ALU.not_equal, fill=1.0,
                               base=0, pattern=[[-1, P]], channel_multiplier=1).then_inc(ident_ok, 1)
            dg = k.cmask[:, T - P:T]
            pool.affine_select(out=dg, in_=dg, compare_op=ALU.is_ge, fill=-BIG,
                               base=0, pattern=[[-1, P]], channel_multiplier=1).then_inc(ident_ok, 1)
            pool.wait_ge(ident_ok, 3)
            pool.tensor_copy(k.identb[:, :], k.ident[:, :]).then_inc(ident_ok, 1)

        @block.scalar
        def _(act):
            act.wait_ge(c_in, 32)
            act.activation(c_exp[:, :], c_nat[:, :], ACT.Exp, scale=-1.0).then_inc(exp_ok, 1)
            for b in range(B):
                act.wait_ge(br_ps, b + 1)
                act.activation(k.gb[:, b, :], banks[b][:, 3 * C:4 * C], ACT.Copy)
                act.activation(k.BR[:, b, :, :], banks[b][:, 0:3 * C].rearrange("p (j c) -> p j c", j=3),
                               ACT.Copy).then_inc(br_ok, 1)

        @block.vector
        def _(dve):
            dve.wait_ge(exp_ok, 1)
            nc.vector.tensor_scalar(c_one[:, :], c_exp[:, :], 1.0, None, ALU.add).then_inc(chain, 1)
            dve.wait_ge(chain, 1)
            nc.vector.reciprocal(c_rec[:, :], c_one[:, :]).then_inc(chain, 1)
            dve.wait_ge(chain, 2)
            nc.vector.tensor_tensor(c_silu[:, :], c_nat[:, :], c_rec[:, :], ALU.mult).then_inc(silu_ok, 1)
            dve.wait_ge(siluT_ps, 1)
            nc.vector.tensor_copy(siluT[:, :], banks[0][:, 0:B]).then_inc(chain, 1)
            dve.wait_ge(chain, 3)
            nc.vector.tensor_copy(silu_bc[:, :, :],
                                  siluT[:, :].unsqueeze(2).broadcast_to([P, B, P])).then_inc(siluT_ok, 1)
            dve.wait_ge(mod_ps, 1)
            nc.vector.tensor_copy(k.sac[:, :], banks[1][:, 0:B])
            nc.vector.tensor_scalar(k.cac[:, :], banks[1][:, B:2 * B], 1.0, None, ALU.add).then_inc(wt_free, 1)
            dve.wait_ge(br_ok, B)
            n = 3
            for g in (k.BR[:, :, 0, :], k.gb[:, :, :]):
                nc.vector.tensor_scalar(gsgn[:, :, :], g, 0.0, 2.0, ALU.is_ge, ALU.mult)
                nc.vector.scalar_tensor_tensor(out=gneg[:, :, :], in0=g, scalar=-1.0, in1=g,
                                               op0=ALU.mult, op1=ALU.max).then_inc(chain, 1)
                n += 1
                dve.wait_ge(chain, n)
                nc.vector.tensor_scalar(gabs[:, :, :], gneg[:, :, :], 0.25, None, ALU.max).then_inc(chain, 1)
                n += 1
                dve.wait_ge(chain, n)
                nc.vector.scalar_tensor_tensor(out=g, in0=gsgn[:, :, :], scalar=-1.0, in1=gabs[:, :, :],
                                               op0=ALU.add, op1=ALU.mult).then_inc(chain, 1)
                n += 1
                dve.wait_ge(chain, n)
            nc.vector.tensor_scalar(k.BR[:, :, 2, :], k.BR[:, :, 2, :], 1.0, None, ALU.add)
            dve.wait_ge(w_in, N_W)
            for g in range(NG):
                src = wout_nat[:, :].rearrange("o (par g pp d) -> o g pp par d", par=2, g=NG, d=D)[:, g]
                last = nc.vector.tensor_copy(
                    wout_perm[:, g * 32:g * 32 + 32].rearrange("o (pp par d) -> o pp par d", pp=2, par=2), src)
            src = bqk_nat[:, :].rearrange("s (par half p d) -> s half par d p", par=2, half=2, d=D)
            for half in range(2):
                for par in range(2):
                    r = (2 * half + par) * 32
                    last = nc.vector.tensor_copy(bqk_perm[:, r:r + 32].rearrange("s (d p) -> s d p", d=D),
                                                 src[:, half, par])
            last.then_inc(perm_ok, 1)
            for part, dst in ((0, k.wq2), (1, k.wk2)):
                src = wqkv2[:, part * C:part * C + C].rearrange("c (par half p d) -> c half par d p",
                                                               par=2, half=2, d=D)
                for half in range(2):
                    for par in range(2):
                        r = (2 * half + par) * 32
                        nc.vector.tensor_copy(dst[:, r:r + 32].rearrange("c (d p) -> c d p", d=D),
                                              src[:, half, par])
            nc.vector.tensor_copy(k.wv2[:, :], wqkv2[:, 2 * C:3 * C])
            for n, (dst, cols) in enumerate(((k.wq1, C), (k.wk1, C), (k.wv1, C), (k.wo1, C),
                                             (k.eb1T, E * FT), (k.rb1T, FT), (k.bqk2, 2), (k.ln1c, 2))):
                dve.wait_ge(wt_ps, n + 1)
                nc.vector.tensor_copy(dst[:, :], banks[(2 + n) % 8][:, 0:cols])

        @block.tensor
        def _(pe):
            pe.wait_ge(ident_ok, 4)
            pe.wait_ge(silu_ok, 1)
            pe.transpose(banks[0][:, 0:B], c_silu[:, :], k.ident[0:B, 0:B]).then_inc(siluT_ps, 1)
            pe.wait_ge(siluT_ok, 1)
            for j in range(2):
                mm = pe.matmul(banks[1][:, B * j:B * j + B], wmod[:, C * j:C * j + C], silu_bc[:, :, 0],
                               start=True, stop=True)
            mm.then_inc(mod_ps, 1)
            for b in range(B):
                if b == 1:
                    pe.wait_ge(wt_free, 1)
                pe.matmul(banks[b][:, :], silu_bc[:, b, :], wmod[:, 2 * C:6 * C],
                          start=True, stop=True).then_inc(br_ps, 1)
            pe.wait_ge(w_in, N_W)
            pe.wait_ge(br_ok, B)
            for n in range(3):
                pe.transpose(banks[2 + n][:, 0:C], wqk_nat[:, n, :], k.ident[:, :]).then_inc(wt_ps, 1)
            pe.wait_ge(perm_ok, 1)
            pe.transpose(banks[5][:, 0:C], wout_perm[:, :], k.ident[:, :]).then_inc(wt_ps, 1)
            pe.transpose(banks[6][:, 0:E * FT], b1_nat[:, :], k.ident[0:E * FT, 0:E * FT]).then_inc(wt_ps, 1)
            pe.transpose(banks[7][:, 0:FT], rb1_nat[:, :], k.ident[0:FT, 0:FT]).then_inc(wt_ps, 1)
            pe.transpose(banks[0][:, 0:2], bqk_perm[:, :], k.ident[0:2, 0:2]).then_inc(wt_ps, 1)
            pe.transpose(banks[1][:, 0:2], ln1_nat[:, :], k.ident[0:2, 0:2]).then_inc(wt_ps, 1)


def stats(nc, k, src, tag):
    with ExitStack() as ctx:
        def sem(name):
            return ctx.enter_context(nc.semaphore(f"{tag}_{name}"))

        st_ok, mv_ok, ve_ok, rs_ok = sem("st_ok"), sem("mv_ok"), sem("ve_ok"), sem("rs_ok")
        six = ctx.enter_context(nc.sbuf_tensor(f"{tag}_six", [P, NT, 6], F32))
        mv = ctx.enter_context(nc.sbuf_tensor(f"{tag}_mv", [P, NT, 2], F32))
        ve = ctx.enter_context(nc.sbuf_tensor(f"{tag}_ve", [P, NT], F32))
        block = ctx.enter_context(nc.Block())

        @block.vector
        def _(dve):
            with dve.Fori(0, NT - 7, 8) as t:
                for i in range(8):
                    last = nc.vector.bn_stats(six[:, bass.ds(t + i, 1), :], src[:, bass.ds(t + i, 1), :])
                last.then_inc(st_ok, 1)
            dve.wait_ge(st_ok, NT // 8)
            for i in range(NT):
                last = nc.vector.bn_aggr(mv[:, i, :], six[:, i, :])
            last.then_inc(mv_ok, 1)
            dve.wait_ge(mv_ok, 1)
            nc.vector.tensor_scalar(ve[:, :], mv[:, :, 1], EPS, None, ALU.add).then_inc(ve_ok, 1)
            dve.wait_ge(rs_ok, 1)
            nc.vector.scalar_tensor_tensor(out=k.nmr[:, :], in0=mv[:, :, 0], scalar=-1.0, in1=k.rstd[:, :],
                                           op0=ALU.mult, op1=ALU.mult)

        @block.gpsimd
        def _(pool):
            pool.memset(k.mhalf[:, :], -0.5).then_inc(ve_ok, 1)
            pool.wait_ge(ve_ok, 2)
            pool.tensor_tensor(k.rstd[:, :], ve[:, :], k.mhalf[:, :], ALU.pow).then_inc(rs_ok, 1)


def norm_and_project(nc, k, src, wq, wk, wv, bqk, bv, scale_of, shift_of, banks, tag):
    with ExitStack() as ctx:
        def sb(name, shape, dt=F32):
            return ctx.enter_context(nc.sbuf_tensor(f"{tag}_{name}", shape, dt))

        def sem(name):
            return ctx.enter_context(nc.semaphore(f"{tag}_{name}"))

        XN = sb("XN", [P, 2, TB, C])
        HT = sb("HT", [P, 2, T])
        RE = sb("RE", [P, 2, 2, T])
        xn_ok = sem("xn_ok")
        tr_ps = sem("tr_ps")
        ht_ok = sem("ht_ok")
        qk_ps = sem("qk_ps")
        v_ps = sem("v_ps")
        s1_ok = sem("s1_ok")
        re_ok = sem("re_ok")
        s2_ok = sem("s2_ok")
        s3_ok = sem("s3_ok")
        v_ok = sem("v_ok")
        block = ctx.enter_context(nc.Block())

        def bank(u, j):
            return banks[4 * u + j]

        @block.vector
        def _(dve):
            with dve.Fori(0, B - 1, 2) as b0:
                for u in range(2):
                    b = b0 + u
                    for t in range(TB):
                        tile = b * TB + t
                        last = nc.vector.tensor_scalar(
                            XN[:, u, t, :], src[:, bass.ds(tile, 1), :], k.rstd[:, bass.ds(tile, 1)],
                            k.nmr[:, bass.ds(tile, 1)], ALU.mult, ALU.add)
                    last.then_inc(xn_ok, 1)
                    for side in range(2):
                        dve.wait_ge(s1_ok, 2 * b + side + 1)
                        nc.vector.scalar_tensor_tensor(
                            out=RE[:, u, side, :], in0=bank(u, 1 + side)[:, :], scalar=bqk[:, side:side + 1],
                            in1=k.QKS[:, side, 0, bass.ds(b * T, T)], op0=ALU.add,
                            op1=ALU.subtract).then_inc(re_ok, 1)
                    for side in range(2):
                        dve.wait_ge(s2_ok, 2 * b + side + 1)
                        nc.vector.tensor_tensor(
                            k.QKS[:, side, 2, bass.ds(b * T, T)], RE[:, u, side, :],
                            k.QKS[:, side, 1, bass.ds(b * T, T)], ALU.subtract).then_inc(s3_ok, 1)
                    dve.wait_ge(v_ps, b + 1)
                    nc.vector.tensor_tensor(
                        k.V[:, bass.ds(b * TB, TB), :], bank(u, 3)[:, :].rearrange("p (t c) -> p t c", t=TB),
                        bv[:, :].unsqueeze(1).broadcast_to([P, TB, C]), ALU.add).then_inc(v_ok, 1)

        @block.tensor
        def _(pe):
            with pe.Fori(0, B - 1, 2) as b0:
                for u in range(2):
                    b = b0 + u
                    pe.wait_ge(xn_ok, b + 1)
                    for t in range(TB):
                        mm = pe.transpose(bank(u, 0)[:, t * P:t * P + P], XN[:, u, t, :], k.ident[:, :])
                    mm.then_inc(tr_ps, 1)
                    pe.wait_ge(ht_ok, b + 1)
                    pe.matmul(bank(u, 1)[:, :], wq[:, :], HT[:, u, :], start=True, stop=True).then_inc(qk_ps, 1)
                    pe.matmul(bank(u, 2)[:, :], wk[:, :], HT[:, u, :], start=True, stop=True).then_inc(qk_ps, 1)
                    for t in range(TB):
                        mm = pe.matmul(bank(u, 3)[:, t * P:t * P + P], HT[:, u, t * P:t * P + P], wv[:, :],
                                       start=True, stop=True)
                    mm.then_inc(v_ps, 1)

        @block.scalar
        def _(act):
            with act.Fori(0, B - 1, 2) as b0:
                for u in range(2):
                    b = b0 + u
                    act.wait_ge(tr_ps, b + 1)
                    act.activation(HT[:, u, :], bank(u, 0)[:, :], ACT.Identity, bias=shift_of(b),
                                   scale=scale_of(b)).then_inc(ht_ok, 1)
                    for side in range(2):
                        act.wait_ge(qk_ps, 2 * b + side + 1)
                        act.activation(k.QKS[:, side, 0, bass.ds(b * T, T)], bank(u, 1 + side)[:, :],
                                       ACT.Identity, bias=bqk[:, side:side + 1]).then_inc(s1_ok, 1)
                    for side in range(2):
                        act.wait_ge(re_ok, 2 * b + side + 1)
                        act.activation(k.QKS[:, side, 1, bass.ds(b * T, T)], RE[:, u, side, :],
                                       ACT.Copy).then_inc(s2_ok, 1)


def wait_apart(eng, sem, value, ready=None):
    value = value if type(value) is int else eng.to_reg(value)
    if ready is not None:
        eng.wait_ge(*ready)
    eng.wait_ge(sem, value)


def in_pairs(eng, body, count=B):
    body(0, 0)
    body(1, 1)
    with eng.Fori(2, count - 1, 2) as n:
        body(n, 0)
        body(n + 1, 1)


def later(n, first=2):
    return not (type(n) is int and n < first)


def attention(nc, k, causal, pairs_s, banks_t, bank_o, bank_m, tag):
    with ExitStack() as ctx:
        def sb(name, shape, dt=F32):
            return ctx.enter_context(nc.sbuf_tensor(f"{tag}_{name}", shape, dt))

        def sem(name):
            return ctx.enter_context(nc.semaphore(f"{tag}_{name}"))

        QS = [sb(f"QS{u}", [P, H // 2, T], BF16) for u in range(2)]
        KS = [sb(f"KS{u}", [P, H // 2, T], BF16) for u in range(2)]
        PT = sb("PT", [P, 2, HG, T])
        VA = sb("VA", [P, 2, TB, H, 32])
        MX = sb("MX", [P, 2, TB, 2, HG])
        MR = sb("MR", [P, 2, TB, 2, HG])
        M3 = sb("M3", [P, 2, TB, 2, 3, HG], BF16)
        MT = sb("MT", [6 * HG, 2, T], BF16)
        OT = (k.H2[:, 16:24, :].rearrange("p (g t) c -> p g (t c)", g=2) if causal else
              sb("OT", [P, 2, T]))
        RD = sb("RD", [P, 2, TB, HG])
        JK = k.H2[:, 0:16, :].rearrange("p (a b t) c -> p a b (t c)", a=2, b=2) if causal else None

        filled = sem("filled")
        stk = [[sem(f"stk{u}{h}") for h in range(2)] for u in range(2)]
        vau = sem("vau")
        s_ps = sem("s_ps")
        red = sem("red")
        spl = sem("spl")
        m_ps = sem("m_ps")
        m_ev = sem("m_ev")
        m_row = [sem(f"m_row{h}") for h in range(2)]
        t_ps = sem("t_ps")
        ex = sem("ex")
        msk = sem("msk")
        o_pe = sem("o_pe")
        o_ev = sem("o_ev")
        o_tr = sem("o_tr")
        o_rc = sem("o_rc")
        o_nm = sem("o_nm")
        block = ctx.enter_context(nc.Block())

        N_HALF = 2 * 2 * NR * 16
        STEPS = B + 1

        def width(kt):
            return T - kt * P if causal else T

        def steps(eng, step):
            step(0, 0)
            step(1, 1)
            with eng.Fori(2, B - 1, 2) as n:
                step(n, 0)
                step(n + 1, 1)
            step(B, B % 2)

        def stage(n):
            first, last = (type(n) is int and n == 0), (type(n) is int and n == B)
            second = type(n) is int and n == 1
            return not last, not first, not first and not second

        @block.sync
        def _(sp):
            def load(n, u, half):
                for par in range(2):
                    src = (2 * half + par) * 32
                    for j in range(NR):
                        dst = 64 * par + D * j
                        for side, stack, part in ((0, QS[u], Q_PARTS[j]), (1, KS[u], K_PARTS[j])):
                            sp.dma_start(stack[dst:dst + D, HG * half:HG * half + HG, :],
                                         k.QKS[src:src + 32, side, part, bass.ds(n * T, T)]).then_inc(stk[u][half], 16)

            def maxima_rows(n, u, half):
                sp.wait_ge(m_ev, 2 * n + half + 1)
                for par in range(2):
                    sp.dma_start(QS[u][64 * par + KS_ROWS:64 * par + KT_ROWS, HG * half:HG * half + HG, :],
                                 MT[3 * HG * par:3 * HG * par + 3 * HG, half, :]).then_inc(m_row[half], 16)

            def step(n, u):
                maxima, sums, _ = stage(n)
                if sums:
                    maxima_rows(n - 1, 1 - u, 1)
                more = not (type(n) is int and n >= B - 1)
                if maxima:
                    if more:
                        if sums:
                            sp.wait_ge(t_ps, (n - 1) * UN * HG + UN * HG // 2)
                        load(n + 1, 1 - u, 0)
                    maxima_rows(n, u, 0)
                    if more:
                        if sums:
                            sp.wait_ge(t_ps, n * UN * HG)
                        load(n + 1, 1 - u, 1)

            sp.wait_ge(filled, 4)
            load(0, 0, 0)
            load(0, 0, 1)
            step(0, 0)
            step(1, 1)
            with sp.Fori(2, B - 3, 2) as n:
                step(n, 0)
                step(n + 1, 1)
            step(B - 2, 0)
            step(B - 1, 1)
            step(B, 0)

        @block.tensor
        def _(pe):
            def scores_max(n, u, g, qt, pair):
                if not (type(n) is int and n == 0 and g == 0 and qt == TB - 1):
                    pe.wait_ge(red, (n * UN + g * TB + TB - 1 - qt) * 2 + pair - 1)
                w = (qt + 1) * P if causal else T
                p = 2 * g + pair
                for par in range(2):
                    r = 64 * par
                    mm = pe.matmul(pairs_s[pair][:, par, 0:w], QS[u][r:r + KS_ROWS, p, qt * P:qt * P + P],
                                   KS[u][r:r + KS_ROWS, p, 0:w], start=True, stop=True)
                mm.then_inc(s_ps, 1)

            def scores_exp(n, u, g, kt, pair):
                w = width(kt)
                p = 2 * g + pair
                for par in range(2):
                    at = (g * TB + kt) * HG + 2 * pair + par
                    if not (type(n) is int and n == 0 and at < 2):
                        pe.wait_ge(ex, n * UN * HG + at - 1)
                    r = 64 * par
                    pe.matmul(banks_t[par][:, 0:w], KS[u][r:r + KT_ROWS, p, kt * P:kt * P + P],
                              QS[u][r:r + KT_ROWS, p, T - w:T], start=True, stop=True).then_inc(t_ps, 1)

            def add_sums(n, u, g, kt):
                w = width(kt)
                unit = n * UN + g * TB + kt
                if causal:
                    pe.wait_ge(msk, unit + 1)
                else:
                    pe.wait_ge(ex, (unit + 1) * HG)
                if kt == 0:
                    if g == 0:
                        pe.wait_ge(vau, n + 1)
                    if not (type(n) is int and n == 0 and g == 0):
                        pe.wait_ge(o_ev, n * NG + g)
                for i in range(HG):
                    mm = pe.matmul(bank_o[32 * i:32 * i + 32, T - w:T], VA[:, u, kt, head_of(g, i), :],
                                   PT[:, kt % 2, i, 0:w], start=(kt == 0), stop=(kt == TB - 1))
                mm.then_inc(o_pe, 1)

            def turn_sums(n, g, halves):
                pe.wait_ge(o_ev, n * NG + g + 1)
                if not (type(n) is int and n == 0 and g == 0):
                    pe.wait_ge(o_nm, n * NG + g)
                pe.wait_ge(m_ev, halves)
                for qt in range(TB):
                    mm = pe.transpose(bank_m[:, qt * P:qt * P + P], OT[:, g % 2, qt * P:qt * P + P],
                                      k.ident[:, :])
                mm.then_inc(o_tr, 1)

            def turn_maxima(n, half, groups):
                pe.wait_ge(spl, (2 * n + half) * 4 + 4)
                if not (type(groups) is int and groups == 0):
                    pe.wait_ge(o_nm, groups)
                if not (type(n) is int and n == 0 and half == 0):
                    pe.wait_ge(m_ev, 2 * n + half)
                out = bank_m[0:6 * HG, :].bitcast(BF16)
                for qt in range(TB):
                    mm = pe.transpose(out[:, qt * P:qt * P + P],
                                      M3[:, half, qt].rearrange("p a s h -> p (a s h)"), k.identb[:, :])
                mm.then_inc(m_ps, 1)

            def step(n, u):
                maxima, sums, before = stage(n)
                for g in range(NG):
                    for kt in range(TB):
                        if maxima and g % 2 == 0 and kt == 0:
                            pe.wait_ge(stk[u][g // 2], n * (N_HALF // 2) + N_HALF - u * (N_HALF // 2))
                        if sums and g % 2 == 0 and kt == 0:
                            pe.wait_ge(m_row[g // 2], n * 32)
                        if sums:
                            scores_exp(n - 1, 1 - u, g, kt, 0)
                        if maxima:
                            scores_max(n, u, g, TB - 1 - kt, 0)
                        if sums and (g or kt):
                            add_sums(n - 1, 1 - u, g if kt else g - 1, (kt - 1) % TB)
                        elif before:
                            add_sums(n - 2, u, NG - 1, TB - 1)
                        if kt == 1 and sums:
                            if g:
                                turn_sums(n - 1, g - 1, 2 * n if g < 3 or not maxima else 2 * n + 1)
                            elif before:
                                turn_sums(n - 2, NG - 1, 2 * n - 1)
                        if kt == 2 and g == 0 and sums:
                            turn_maxima(n - 1, 1, (n - 1) * NG)
                        if kt == 2 and g == 2 and maxima:
                            turn_maxima(n, 0, (n - 1) * NG + 2 if sums else 0)
                        if sums:
                            scores_exp(n - 1, 1 - u, g, kt, 1)
                        if maxima:
                            scores_max(n, u, g, TB - 1 - kt, 1)

            steps(pe, step)
            add_sums(B - 1, (B - 1) % 2, NG - 1, TB - 1)
            turn_sums(B - 1, NG - 1, 2 * B)

        @block.scalar
        def _(act):
            def keep_sums(n, g):
                act.wait_ge(o_pe, (n * NG + g + 1) * TB)
                if g >= 2:
                    act.wait_ge(o_tr, n * NG + g - 1)
                elif later(n, 1):
                    act.wait_ge(o_tr, n * NG + g - 1)
                act.activation(OT[:, g % 2, :], bank_o[:, :], ACT.Copy).then_inc(o_ev, 1)

            def keep_maxima(n, half):
                act.wait_ge(m_ps, 2 * n + half + 1)
                if later(n, 1):
                    act.wait_ge(m_row[half], n * 32)
                act.activation(MT[:, half, :], bank_m[0:6 * HG, :].bitcast(BF16)[:, 0:T],
                               ACT.Copy).then_inc(m_ev, 1)

            def step(n, u):
                maxima, sums, before = stage(n)
                for g in range(NG):
                    for kt in range(TB):
                        if sums:
                            w = width(kt)
                            unit = (n - 1) * UN + g * TB + kt
                            for i in range(HG):
                                act.wait_ge(t_ps, unit * HG + i + 1)
                                if i == 0 and (before or g or kt >= 2):
                                    act.wait_ge(o_pe, unit - 1)
                                act.activation(PT[:, kt % 2, i, 0:w], banks_t[i % 2][:, 0:w], ACT.Exp,
                                               scale=SCALE).then_inc(ex, 1)
                            if kt == 0:
                                if g:
                                    keep_sums(n - 1, g - 1)
                                elif before:
                                    keep_sums(n - 2, NG - 1)
                        if kt == 2 and g == 0 and sums:
                            keep_maxima(n - 1, 1)
                        if kt == 2 and g == 2 and maxima:
                            keep_maxima(n, 0)

            steps(act, step)
            keep_sums(B - 1, NG - 1)

        @block.vector
        def _(dve):
            def output(n, g):
                dve.wait_ge(o_tr, n * NG + g + 1)
                t = bank_m[:, :].rearrange("p (q i c) -> p q i c", q=TB, i=HG)
                nc.vector.reciprocal(RD[:, g % 2], t[:, :, :, D]).then_inc(o_rc, 1)
                dve.wait_ge(o_rc, n * NG + g + 1)
                out = k.O[:, bass.ds(n * TB, TB), g * 32:g * 32 + 32].rearrange("p q (i d) -> p q i d", i=HG)
                nc.vector.tensor_tensor(out, t[:, :, :, 0:D],
                                        RD[:, g % 2].unsqueeze(3).broadcast_to([P, TB, HG, D]),
                                        ALU.mult).then_inc(o_nm, 1)

            def step(n, u):
                maxima, sums, before = stage(n)
                for g in range(NG):
                    for kt in range(TB):
                        qt = TB - 1 - kt
                        for pair in range(2):
                            if not maxima:
                                continue
                            if kt == 0 and pair == 0 and g % 2 == 0 and sums:
                                dve.wait_ge(spl, (2 * (n - 1) + g // 2) * 4 + 4)
                            at = (n * UN + g * TB + kt) * 2 + pair
                            wait_apart(dve, s_ps, at + 1, (filled, 4))
                            mx = MX[:, g // 2, qt, :, 2 * (g % 2) + pair]
                            if causal:
                                w = (qt + 1) * P
                                for par in range(2):
                                    last = nc.vector.tensor_tensor_reduce(
                                        out=JK[:, pair, par, 0:w], in0=pairs_s[pair][:, par, 0:w], in1=k.cmask[:, T - w:T],
                                        scale=1.0, scalar=-BIG, op0=ALU.add, op1=ALU.max,
                                        accum_out=mx[:, par:par + 1])
                            else:
                                last = nc.vector.tensor_reduce(mx, pairs_s[pair][:, :, :], AX.X, ALU.max)
                            last.then_inc(red, 1)
                        if kt == 1 and sums:
                            if g:
                                output(n - 1, g - 1)
                            elif before:
                                output(n - 2, NG - 1)

            steps(dve, step)
            output(B - 1, NG - 1)

        @block.gpsimd
        def _(pool):
            for u in range(2):
                pool.memset(KS[u][:, :, :], -1.0).then_inc(filled, 1)
            pool.memset(VA[:, :, :, :, :], 0.0).then_inc(filled, 1)
            pool.wait_ge(filled, 3)
            pool.memset(VA[:, :, :, :, D:D + 1], 1.0).then_inc(filled, 1)
            pool.wait_ge(filled, 4)

            def stage_v(n, u):
                if later(n):
                    wait_apart(pool, o_pe, (n - 1) * UN, (filled, 4))
                pool.tensor_copy(VA[:, u, :, :, 0:D].rearrange("p t h d -> p (t h) d"),
                                 k.V[:, bass.ds(n * TB, TB), :].rearrange("p t (h d) -> p (t h) d", d=D)
                                 ).then_inc(vau, 1)

            def split_maxima(n, half):
                wait_apart(pool, red, (2 * n + half + 1) * UN, (filled, 4))
                if later(n, 1):
                    wait_apart(pool, m_ps, 2 * n + half - 1, (filled, 4))
                at = (2 * n + half) * 4
                m, r = MX[:, half], MR[:, half]
                part = [M3[:, half, :, :, s, :] for s in range(3)]
                pool.tensor_copy(part[0], m).then_inc(spl, 1)
                wait_apart(pool, spl, at + 1, (filled, 4))
                pool.tensor_tensor(r, m, part[0], ALU.subtract).then_inc(spl, 1)
                wait_apart(pool, spl, at + 2, (filled, 4))
                pool.tensor_copy(part[1], r).then_inc(spl, 1)
                wait_apart(pool, spl, at + 3, (filled, 4))
                pool.tensor_tensor(part[2], r, part[1], ALU.subtract).then_inc(spl, 1)

            def step(n, u):
                maxima, sums, _ = stage(n)
                for g in range(NG):
                    for kt in range(TB):
                        if g == 2 and kt == 0 and maxima:
                            split_maxima(n, 0)
                        if causal and sums:
                            unit = (n - 1) * UN + g * TB + kt
                            wait_apart(pool, ex, (unit + 1) * HG, (filled, 4))
                            dg = PT[:, kt % 2, :, 0:P]
                            pool.affine_select(out=dg, in_=dg, compare_op=ALU.is_ge, fill=0.0, base=0,
                                               pattern=[[0, HG], [1, P]], channel_multiplier=-1).then_inc(msk, 1)
                        if g == 0 and kt == 2 and maxima:
                            stage_v(n, u)
                if maxima:
                    split_maxima(n, 1)

            steps(pool, step)


def out_project(nc, k, wo, banks, tag, add_rows, into, gate):
    with ExitStack() as ctx:
        def sb(name, shape, dt=F32):
            return ctx.enter_context(nc.sbuf_tensor(f"{tag}_{name}", shape, dt))

        def sem(name):
            return ctx.enter_context(nc.semaphore(f"{tag}_{name}"))

        OB = sb("OB", [P, 2, TB, C])
        OC = sb("OC", [P, 2, T])
        YG = sb("YG", [P, 2, TB, C])
        ob_ok = sem("ob_ok")
        tr_ps = sem("tr_ps")
        oc_ok = sem("oc_ok")
        y_ps = sem("y_ps")
        yg_ok = sem("yg_ok")
        in_ok = sem("in_ok")
        block = ctx.enter_context(nc.Block())

        @block.gpsimd
        def _(pool):
            def fill(b, u):
                if later(b):
                    wait_apart(pool, tr_ps, b - 1, (ob_ok, 2))
                pool.tensor_copy(OB[:, u, :, :], k.O[:, bass.ds(b * TB, TB), :]).then_inc(ob_ok, 1)

            in_pairs(pool, fill)

        @block.tensor
        def _(pe):
            def project(b, u):
                pe.wait_ge(ob_ok, b + 1)
                for t in range(TB):
                    mm = pe.transpose(banks[2 * u][:, t * P:t * P + P], OB[:, u, t, :], k.ident[:, :])
                mm.then_inc(tr_ps, 1)
                pe.wait_ge(oc_ok, b + 1)
                if later(b):
                    pe.wait_ge(yg_ok, b - 1)
                for t in range(TB):
                    mm = pe.matmul(banks[2 * u + 1][:, t * P:t * P + P], OC[:, u, t * P:t * P + P],
                                   wo[:, :], start=True, stop=True)
                mm.then_inc(y_ps, 1)

            in_pairs(pe, project)

        @block.scalar
        def _(act):
            with act.Fori(0, B - 1, 2) as b0:
                for u in range(2):
                    b = b0 + u
                    act.wait_ge(tr_ps, b + 1)
                    act.activation(OC[:, u, :], banks[2 * u][:, :], ACT.Copy).then_inc(oc_ok, 1)

        @block.vector
        def _(dve):
            with dve.Fori(0, B - 1, 2) as b0:
                for u in range(2):
                    b = b0 + u
                    dve.wait_ge(y_ps, b + 1)
                    y = banks[2 * u + 1][:, :].rearrange("p (t c) -> p t c", t=TB)
                    if gate is not None:
                        row, op = gate[:, bass.ds(b, 1), :], ALU.mult
                    else:
                        row, op = add_rows[:, :].unsqueeze(1), ALU.add
                    nc.vector.tensor_tensor(YG[:, u], y, row.broadcast_to([P, TB, C]), op).then_inc(yg_ok, 1)
                    dve.wait_ge(yg_ok, b + 1)
                    dst = into[:, bass.ds(b * TB, TB), :]
                    nc.vector.tensor_tensor(dst, dst, YG[:, u], ALU.add).then_inc(in_ok, 1)


def modulate(nc, k, src, dst, mult, add, tag):
    with ExitStack() as ctx:
        def sem(name):
            return ctx.enter_context(nc.semaphore(f"{tag}_{name}"))

        XN = ctx.enter_context(nc.sbuf_tensor(f"{tag}_XN", [P, 2, TB, C], F32))
        XM = ctx.enter_context(nc.sbuf_tensor(f"{tag}_XM", [P, 2, TB, C], F32))
        xn_ok, xm_ok, out_ok = sem("xn_ok"), sem("xm_ok"), sem("out_ok")
        block = ctx.enter_context(nc.Block())

        @block.vector
        def _(dve):
            def scale(b, u):
                if later(b):
                    dve.wait_ge(out_ok, b - 1)
                for t in range(TB):
                    tile = b * TB + t
                    last = nc.vector.tensor_scalar(
                        XN[:, u, t, :], src[:, bass.ds(tile, 1), :], k.rstd[:, bass.ds(tile, 1)],
                        k.nmr[:, bass.ds(tile, 1)], ALU.mult, ALU.add)
                last.then_inc(xn_ok, 1)
                dve.wait_ge(xn_ok, b + 1)
                nc.vector.tensor_tensor(XM[:, u], XN[:, u], mult(b).broadcast_to([P, TB, C]),
                                        ALU.mult).then_inc(xm_ok, 1)

            in_pairs(dve, scale)

        @block.gpsimd
        def _(pool):
            with pool.Fori(0, B - 1, 2) as b0:
                for u in range(2):
                    b = b0 + u
                    wait_apart(pool, xm_ok, b + 1)
                    pool.tensor_tensor(dst[:, bass.ds(b * TB, TB), :], XM[:, u],
                                       add(b).broadcast_to([P, TB, C]), ALU.add).then_inc(out_ok, 1)


def gate_and_residual(nc, k, a, banks):
    NL = E + 2
    with ExitStack() as ctx:
        def sb(name, shape, dt=F32):
            return ctx.enter_context(nc.sbuf_tensor(f"gr_{name}", shape, dt))

        def sem(name):
            return ctx.enter_context(nc.semaphore(f"gr_{name}"))

        gw = sb("gw", [P, NL])
        cb = sb("cb", [P, NL])
        rw1 = sb("rw1", [P, F])
        rw2 = sb("rw2", [P, FT, C])
        XN = sb("XN", [P, 2, TB, C])
        XM = sb("XM", [P, 2, TB, C])
        OB = sb("OB", [P, 2, TB, C])
        XC = sb("XC", [P, 2, T])
        GE = sb("GE", [P, 2, FT, T])
        zero = sb("zero", [P, 4 * C])
        w_in = sem("w_in")
        z_in = sem("z_in")
        z_ok = sem("z_ok")
        xn_ok = sem("xn_ok")
        xm_ok = sem("xm_ok")
        xt_ok = sem("xt_ok")
        ob_ok = sem("ob_ok")
        tr_ps = sem("tr_ps")
        xc_ok = sem("xc_ok")
        lg_ps = sem("lg_ps")
        lg_ok = sem("lg_ok")
        up_ps = sem("up_ps")
        ge_ok = sem("ge_ok")
        dn_ps = sem("dn_ps")
        rm_ok = sem("rm_ok")
        block = ctx.enter_context(nc.Block())

        @block.sync
        def _(sp):
            sp.wait_ge(z_ok, 2)
            sp.dma_start(gw[:, 0:E], a["L0_ffn_gate_w"]).then_inc(w_in, 16)
            sp.dma_start(gw[:, E:NL], a["L0_ffn_coef_w"]).then_inc(w_in, 16)
            sp.dma_start(cb[:, E:NL], a["L0_ffn_coef_b"].partition_broadcast(P)).then_inc(w_in, 16)
            sp.dma_start(rw1[:, :], a["L0_ffn_rW1"]).then_inc(w_in, 16)
            sp.dma_start(rw2[:, :, :], a["L0_ffn_rW2"].rearrange("(t f) d -> f t d", f=P)).then_inc(w_in, 16)
            for n in range(NX // 4):
                sp.dma_start(k.XS[4 * P * n:4 * P * n + 4 * P, :].rearrange("(t p) c -> p t c", p=P),
                             zero[:, :].rearrange("p (t c) -> p t c", t=4)).then_inc(z_in, 16)
            sp.wait_ge(z_in, 16 * (NX // 4))

        @block.gpsimd
        def _(pool):
            pool.memset(cb[:, :], 0.0).then_inc(z_ok, 1)
            pool.memset(zero[:, :], 0.0).then_inc(z_ok, 1)

            def fill(b, u):
                wait_apart(pool, xt_ok, b + 1)
                if later(b):
                    wait_apart(pool, tr_ps, b - 1, (z_ok, 2))
                else:
                    pool.wait_ge(z_ok, 2)
                pool.tensor_copy(OB[:, u], k.O[:, bass.ds(b * TB, TB), :]).then_inc(ob_ok, 1)

            in_pairs(pool, fill)

        @block.vector
        def _(dve):
            def residual(b, u):
                dve.wait_ge(dn_ps, b + 1)
                nc.vector.tensor_tensor(
                    k.RM[:, bass.ds(b * TB, TB), :], banks[4 + u].rearrange("p (t c) -> p t c", t=TB),
                    k.rb2_bc[:, :].unsqueeze(1).broadcast_to([P, TB, C]), ALU.add).then_inc(rm_ok, 1)

            def step(b, u):
                if later(b):
                    dve.wait_ge(xt_ok, b - 1)
                for t in range(TB):
                    tile = b * TB + t
                    last = nc.vector.tensor_scalar(
                        XN[:, u, t, :], k.H2[:, bass.ds(tile, 1), :], k.rstd[:, bass.ds(tile, 1)],
                        k.nmr[:, bass.ds(tile, 1)], ALU.mult, ALU.add)
                last.then_inc(xn_ok, 1)
                dve.wait_ge(xn_ok, b + 1)
                nc.vector.tensor_tensor(XM[:, u], XN[:, u], k.g2_bc[:, :].unsqueeze(1).broadcast_to([P, TB, C]),
                                        ALU.mult).then_inc(xm_ok, 1)
                dve.wait_ge(xm_ok, b + 1)
                nc.vector.tensor_tensor(k.O[:, bass.ds(b * TB, TB), :], XM[:, u],
                                        k.b2_bc[:, :].unsqueeze(1).broadcast_to([P, TB, C]),
                                        ALU.add).then_inc(xt_ok, 1)
                dve.wait_ge(lg_ps, b + 1)
                nc.vector.tensor_tensor(
                    k.LG[:, bass.ds(b * TB, TB), :], banks[6 + u][:, 0:TB * NL].rearrange("p (t e) -> p t e", t=TB),
                    cb[:, :].unsqueeze(1).broadcast_to([P, TB, NL]), ALU.add).then_inc(lg_ok, 1)
                if later(b, 1):
                    residual(b - 1, 1 - u)

            dve.wait_ge(w_in, 16 * 5)
            in_pairs(dve, step)
            residual(B - 1, (B - 1) % 2)

        @block.scalar
        def _(act):
            def step(b, u):
                act.wait_ge(tr_ps, b + 1)
                act.activation(XC[:, u, :], banks[u], ACT.Copy).then_inc(xc_ok, 1)
                for ft in range(FT):
                    act.wait_ge(up_ps, b * FT + ft + 1)
                    act.activation(GE[:, u, ft, :], banks[2 + ft % 2], ACT.Gelu,
                                   bias=k.rb1T[:, ft:ft + 1]).then_inc(ge_ok, 1)

            with act.Fori(0, B - 1, 2) as b0:
                step(b0, 0)
                step(b0 + 1, 1)

        @block.tensor
        def _(pe):
            def down(b, u):
                pe.wait_ge(ge_ok, b * FT + FT)
                if later(b):
                    pe.wait_ge(rm_ok, b - 1)
                for t in range(TB):
                    for ft in range(FT):
                        mm = pe.matmul(banks[4 + u][:, t * P:t * P + P], GE[:, u, ft, t * P:t * P + P],
                                       rw2[:, ft, :], start=(ft == 0), stop=(ft == FT - 1))
                mm.then_inc(dn_ps, 1)

            def step(b, u):
                pe.wait_ge(ob_ok, b + 1)
                for t in range(TB):
                    mm = pe.transpose(banks[u][:, t * P:t * P + P], OB[:, u, t, :], k.ident[:, :])
                mm.then_inc(tr_ps, 1)
                pe.wait_ge(xc_ok, b + 1)
                if later(b):
                    pe.wait_ge(lg_ok, b - 1)
                for t in range(TB):
                    mm = pe.matmul(banks[6 + u][:, t * NL:t * NL + NL], XC[:, u, t * P:t * P + P], gw[:, :],
                                   start=True, stop=True)
                mm.then_inc(lg_ps, 1)
                for ft in range(FT):
                    if later(b, 1) or ft >= 2:
                        pe.wait_ge(ge_ok, b * FT + ft - 1)
                    pe.matmul(banks[2 + ft % 2], rw1[:, ft * P:ft * P + P], XC[:, u, :],
                              start=True, stop=True).then_inc(up_ps, 1)
                if later(b, 1):
                    down(b - 1, 1 - u)

            pe.wait_ge(w_in, 16 * 5)
            in_pairs(pe, step)
            down(B - 1, (B - 1) % 2)


def route(nc, k, banks):
    with ExitStack() as ctx:
        def sb(name, shape, dt=F32):
            return ctx.enter_context(nc.sbuf_tensor(f"rt_{name}", shape, dt))

        def sem(name):
            return ctx.enter_context(nc.semaphore(f"rt_{name}"))

        LM = sb("LM", [P, NT])
        DF = sb("DF", [P, NT, E])
        EX = sb("EX", [P, NT, E])
        SE = sb("SE", [P, NT])
        GV = sb("GV", [P, NT])
        CM = sb("CM", [P, NT])
        CD = sb("CD", [P, NT, 2])
        CE = sb("CE", [P, NT, 2])
        CS = sb("CS", [P, NT])
        CR = sb("CR", [P, NT])
        GC = sb("GC", [P, NT])
        EQ = sb("EQ", [P, NT, E])
        RV = sb("RV", [P, NT, E])
        RW = sb("RW", [P, NT, E])
        RM_ = sb("RM", [P, NT])
        OH = sb("OH", [P, NT, E])
        OHB = sb("OHB", [P, NT, E], BF16)
        tri = sb("tri", [P, P], BF16)
        ones = sb("ones", [P, P], BF16)
        one_row = sb("one_row", [P, NT])
        TT = sb("TT", [P, E, NT])
        TI = sb("TI", [P, E, NT])
        TX = sb("TX", [P, E, NT])
        NE = sb("NE", [P, E])
        NI = sb("NI", [P, E], I32)
        NS = sb("NS", [P, E], I32)
        NP = sb("NP", [P, E])
        EN = sb("EN", [P, E])
        OF = sb("OF", [P, E])
        BS = sb("BS", [P, E, NT])
        WB = sb("WB", [P, NT, E])
        WO = sb("WO", [P, NT, E])
        DS = sb("DS", [P, NT])
        JV = sb("JV", [P, NX])
        TE0 = sb("TE0", [P, NX])
        TE1 = sb("TE1", [P, NX])
        c_ok = sem("c_ok")
        dv = sem("dv")
        d_ok = sem("d_ok")
        e_ok = sem("e_ok")
        oh_ok = sem("oh_ok")
        cn_ps = sem("cn_ps")
        di_ok = sem("di_ok")
        sc_in = sem("sc_in")
        block = ctx.enter_context(nc.Block())

        @block.gpsimd
        def _(pool):
            pool.memset(tri[:, :], 1.0).then_inc(c_ok, 1)
            pool.memset(ones[:, :], 1.0).then_inc(c_ok, 1)
            pool.memset(one_row[:, :], 1.0).then_inc(c_ok, 1)
            pool.memset(TE0[:, :], 0.0).then_inc(c_ok, 1)
            pool.wait_ge(c_ok, 4)
            pool.affine_select(out=tri[:, :], in_=tri[:, :], compare_op=ALU.is_gt, fill=0.0, base=0,
                               pattern=[[1, P]], channel_multiplier=-1).then_inc(c_ok, 1)
            pool.iota(RV[:, :, :], pattern=[[0, NT], [-1, E]], base=E, channel_multiplier=0,
                      allow_small_or_imprecise_dtypes=True).then_inc(c_ok, 1)
            pool.iota(JV[:, :], pattern=[[P, NX]], base=0, channel_multiplier=0,
                      allow_small_or_imprecise_dtypes=True).then_inc(c_ok, 1)
            pool.wait_ge(di_ok, 1)
            for t in range(NT):
                pool.indirect_dma_start(out=k.XS, out_offset=bass.IndirectOffsetOnAxis(ap=k.DI[:, t:t + 1], axis=0),
                                        in_=k.O[:, t, :], in_offset=None).then_inc(sc_in, 16)
            pool.wait_ge(sc_in, 16 * NT)

        @block.scalar
        def _(act):
            act.wait_ge(d_ok, 2)
            act.activation(EX[:, :, :], DF[:, :, :], ACT.Exp)
            act.activation(CE[:, :, :], CD[:, :, :], ACT.Exp).then_inc(e_ok, 1)

        @block.tensor
        def _(pe):
            pe.wait_ge(c_ok, 7)
            pe.wait_ge(oh_ok, 1)
            oh = OHB[:, :, :].rearrange("p t e -> p (t e)")
            pe.matmul(banks[0][:, 0:NT * E], tri[:, :], oh, start=True, stop=True)
            pe.matmul(banks[1][:, 0:NT * E], ones[:, :], oh, start=True, stop=True).then_inc(cn_ps, 1)

        @block.vector
        def _(dve):
            v = nc.vector
            steps = [0]

            def link(ins):
                ins.then_inc(dv, 1)
                steps[0] += 1
                dve.wait_ge(dv, steps[0])

            def over(x, n):
                return x.unsqueeze(2).broadcast_to([P, NT, n])

            dve.wait_ge(c_ok, 7)
            lg, lc = k.LG[:, :, 0:E], k.LG[:, :, E:E + 2]
            v.tensor_reduce(CM[:, :], lc, AX.X, ALU.max)
            link(v.tensor_reduce(LM[:, :], lg, AX.X, ALU.max))
            v.tensor_tensor(DF[:, :, :], lg, over(LM[:, :], E), ALU.subtract).then_inc(d_ok, 1)
            v.tensor_tensor(CD[:, :, :], lc, over(CM[:, :], 2), ALU.subtract).then_inc(d_ok, 1)
            link(v.tensor_tensor(EQ[:, :, :], lg, over(LM[:, :], E), ALU.is_equal))
            link(v.tensor_tensor(RW[:, :, :], EQ[:, :, :], RV[:, :, :], ALU.mult))
            link(v.tensor_reduce(RM_[:, :], RW[:, :, :], AX.X, ALU.max))
            v.tensor_tensor(OHB[:, :, :], RW[:, :, :], over(RM_[:, :], E), ALU.is_equal).then_inc(oh_ok, 1)
            v.tensor_tensor(OH[:, :, :], RW[:, :, :], over(RM_[:, :], E), ALU.is_equal)
            dve.wait_ge(e_ok, 1)
            v.tensor_reduce(CS[:, :], CE[:, :, :], AX.X, ALU.add)
            link(v.tensor_reduce(SE[:, :], EX[:, :, :], AX.X, ALU.add))
            v.reciprocal(CR[:, :], CS[:, :])
            link(v.reciprocal(GV[:, :], SE[:, :]))
            v.tensor_tensor(k.G1[:, :], CE[:, :, 1], CR[:, :], ALU.mult)
            link(v.tensor_tensor(GC[:, :], CE[:, :, 0], CR[:, :], ALU.mult))
            v.tensor_tensor(k.G0[:, :], GC[:, :], GV[:, :], ALU.mult)
            dve.wait_ge(cn_ps, 1)
            link(v.tensor_copy(TT[:, :, :], banks[1][:, 0:NT * E].rearrange("p (t e) -> p e t", e=E)))
            for e in range(E):
                ins = v.tensor_tensor_scan(TI[:, e, :], one_row[:, :], TT[:, e, :], 0.0, ALU.mult, ALU.add)
            link(ins)
            v.tensor_tensor(TX[:, :, :], TI[:, :, :], TT[:, :, :], ALU.subtract)
            link(v.tensor_scalar(NE[:, :], TI[:, :, NT - 1], float(P - 1), None, ALU.add))
            link(v.tensor_copy(NI[:, :], NE[:, :]))
            link(v.tensor_scalar(NS[:, :], NI[:, :], 7, 7, ALU.logical_shift_right, ALU.logical_shift_left))
            link(v.tensor_copy(NP[:, :], NS[:, :]))
            link(v.tensor_tensor_scan(EN[:, :], one_row[:, 0:E], NP[:, :], 0.0, ALU.mult, ALU.add))
            link(v.tensor_tensor(OF[:, :], EN[:, :], NP[:, :], ALU.subtract))
            link(v.tensor_tensor(BS[:, :, :], TX[:, :, :],
                                 OF[:, :].unsqueeze(2).broadcast_to([P, E, NT]), ALU.add))
            link(v.tensor_tensor(WB[:, :, :], banks[0][:, 0:NT * E].rearrange("p (t e) -> p t e", e=E),
                                 BS[:, :, :].rearrange("p e t -> p t e"), ALU.add))
            link(v.tensor_tensor(WO[:, :, :], WB[:, :, :], OH[:, :, :], ALU.mult))
            link(v.tensor_reduce(DS[:, :], WO[:, :, :], AX.X, ALU.add))
            v.tensor_copy(k.DI[:, :], DS[:, :]).then_inc(di_ok, 1)
            t0, t1 = TE0, TE1
            for e in range(E - 1):
                link(v.scalar_tensor_tensor(out=t1[:, :], in0=JV[:, :], scalar=EN[:, e:e + 1], in1=t0[:, :],
                                            op0=ALU.is_ge, op1=ALU.add))
                t0, t1 = t1, t0
            v.tensor_copy(k.TE[:, :], t0[:, :])


def experts(nc, k, a, banks):
    with ExitStack() as ctx:
        def sb(name, shape, dt=F32):
            return ctx.enter_context(nc.sbuf_tensor(f"ex_{name}", shape, dt))

        def sem(name):
            return ctx.enter_context(nc.semaphore(f"ex_{name}"))

        EB2 = sb("EB2", [P, E, C])
        W1 = sb("W1", [P, 2, F])
        W2 = sb("W2", [P, 2, FT, C])
        XT = sb("XT", [P, 2, C])
        XC = sb("XC", [P, 2, P])
        HB = sb("HB", [P, 2, FT, P])
        GE = sb("GE", [P, 2, FT, P])
        YT = sb("YT", [P, 2, C])
        b_in = sem("b_in")
        in_ = [sem(f"in{u}") for u in range(2)]
        tr_ps = sem("tr_ps")
        xc_ok = sem("xc_ok")
        up_ps = sem("up_ps")
        hb_ok = sem("hb_ok")
        ge_ok = sem("ge_ok")
        dn_ps = sem("dn_ps")
        y_ok = sem("y_ok")
        y_out = [sem(f"y_out{u}") for u in range(2)]
        block = ctx.enter_context(nc.Block())

        def expert_of(eng, j):
            return eng.value_load(k.TE[0:1, bass.ds(j, 1)], min_val=0, max_val=E - 1)

        @block.sync
        def _(sp):
            sp.dma_start(EB2[:, :, :], a["L0_ffn_b2"].partition_broadcast(P)).then_inc(b_in, 16)

            def load(j, u):
                e = expert_of(sp, j)
                if later(j):
                    sp.wait_ge(dn_ps, j - 1)
                sp.dma_start(XT[:, u, :], k.XS[bass.ds(j * P, P), :]).then_inc(in_[u], 16)
                sp.dma_start(W1[:, u, :], a["L0_ffn_W1"][bass.ds(e, 1), :, :].rearrange("o c f -> c (o f)")
                             ).then_inc(in_[u], 16)
                sp.dma_start(W2[:, u, :, :], a["L0_ffn_W2"][bass.ds(e, 1), :, :].rearrange(
                    "o (t f) d -> f (o t) d", f=P)).then_inc(in_[u], 16)

            in_pairs(sp, load, NX)

        @block.tensor
        def _(pe):
            def turn(j, u):
                pe.wait_ge(in_[u], j * 24 + 48 - 24 * u)
                pe.transpose(banks[u][:, 0:P], XT[:, u, :], k.ident[:, :]).then_inc(tr_ps, 1)

            def down(j, u):
                pe.wait_ge(ge_ok, j + 1)
                if later(j):
                    pe.wait_ge(y_ok, j - 1)
                for ft in range(FT):
                    mm = pe.matmul(banks[4 + u][:, 0:C], GE[:, u, ft, :], W2[:, u, ft, :],
                                   start=(ft == 0), stop=(ft == FT - 1))
                mm.then_inc(dn_ps, 1)

            def step(j, u, turn_next=True):
                pe.wait_ge(xc_ok, j + 1)
                if later(j):
                    pe.wait_ge(hb_ok, j - 1)
                for ft in range(FT):
                    mm = pe.matmul(banks[2 + u][:, ft * P:ft * P + P], W1[:, u, ft * P:ft * P + P], XC[:, u, :],
                                   start=True, stop=True)
                mm.then_inc(up_ps, 1)
                if later(j, 1):
                    down(j - 1, 1 - u)
                if turn_next:
                    turn(j + 1, 1 - u)

            turn(0, 0)
            step(0, 0)
            step(1, 1)
            with pe.Fori(2, NX - 3, 2) as j:
                step(j, 0)
                step(j + 1, 1)
            step(NX - 2, 0)
            step(NX - 1, 1, False)
            down(NX - 1, 1)

        @block.scalar
        def _(act):
            def turned(j, u):
                act.wait_ge(tr_ps, j + 1)
                act.activation(XC[:, u, :], banks[u][:, 0:P], ACT.Copy).then_inc(xc_ok, 1)

            def step(j, u, turn_next=True):
                act.wait_ge(hb_ok, j + 1)
                act.activation(GE[:, u], HB[:, u], ACT.Gelu).then_inc(ge_ok, 1)
                if turn_next:
                    turned(j + 1, 1 - u)

            turned(0, 0)
            with act.Fori(0, NX - 3, 2) as j:
                step(j, 0)
                step(j + 1, 1)
            step(NX - 2, 0)
            step(NX - 1, 1, False)

        @block.vector
        def _(dve):
            def output(j, u):
                e = expert_of(dve, j)
                dve.wait_ge(dn_ps, j + 1)
                if later(j):
                    dve.wait_ge(y_out[u], j * 8 - 8 * u)
                nc.vector.tensor_tensor(YT[:, u, :], banks[4 + u][:, 0:C],
                                        EB2[:, bass.ds(e, 1), :].rearrange("p o c -> p (o c)"),
                                        ALU.add).then_inc(y_ok, 1)

            def step(j, u):
                e = expert_of(dve, j)
                dve.wait_ge(up_ps, j + 1)
                nc.vector.tensor_tensor(HB[:, u], banks[2 + u].rearrange("p (t n) -> p t n", t=FT),
                                        k.eb1T[:, bass.ds(e * FT, FT)].unsqueeze(2).broadcast_to([P, FT, P]),
                                        ALU.add).then_inc(hb_ok, 1)
                if later(j, 1):
                    output(j - 1, 1 - u)

            dve.wait_ge(b_in, 16)
            in_pairs(dve, step, NX)
            output(NX - 1, 1)

        @block.gpsimd
        def _(pool):
            with pool.Fori(0, NX - 1, 2) as j0:
                for u in range(2):
                    j = j0 + u
                    pool.wait_ge(y_ok, j + 1)
                    pool.dma_start(k.YS[bass.ds(j * P, P), :], YT[:, u, :]).then_inc(y_out[u], 16)
            for u in range(2):
                pool.wait_ge(y_out[u], 16 * NX // 2)


def combine(nc, k, out):
    with ExitStack() as ctx:
        def sb(name, shape, dt=F32):
            return ctx.enter_context(nc.sbuf_tensor(f"cb_{name}", shape, dt))

        def sem(name):
            return ctx.enter_context(nc.semaphore(f"cb_{name}"))

        Y = sb("Y", [P, B, TB, C])
        A1 = sb("A1", [P, 2, TB, C])
        A2 = sb("A2", [P, 2, TB, C])
        A3 = sb("A3", [P, 2, TB, C])
        R = sb("R", [P, B, TB, C])
        y_in = [sem(f"y_in{b}") for b in range(B)]
        a1_ok, a2_ok, a3_ok, r_ok, r_out = sem("a1_ok"), sem("a2_ok"), sem("a3_ok"), sem("r_ok"), sem("r_out")
        block = ctx.enter_context(nc.Block())

        @block.gpsimd
        def _(pool):
            for t in range(NT):
                pool.indirect_dma_start(out=Y[:, t // TB, t % TB, :], out_offset=None, in_=k.YS,
                                        in_offset=bass.IndirectOffsetOnAxis(ap=k.DI[:, t:t + 1], axis=0)
                                        ).then_inc(y_in[t // TB], 16)

        @block.vector
        def _(dve):
            v = nc.vector
            for b in range(B):
                u = b % 2
                if b >= 2:
                    dve.wait_ge(r_ok, b - 1)
                for t in range(TB):
                    n = b * TB + t
                    ins = v.scalar_tensor_tensor(out=A1[:, u, t, :], in0=k.RM[:, n, :], scalar=k.G1[:, n:n + 1],
                                                 in1=k.H2[:, n, :], op0=ALU.mult, op1=ALU.add)
                ins.then_inc(a1_ok, 1)
                dve.wait_ge(y_in[b], 16 * TB)
                dve.wait_ge(a1_ok, b + 1)
                for t in range(TB):
                    n = b * TB + t
                    ins = v.scalar_tensor_tensor(out=A2[:, u, t, :], in0=Y[:, b, t, :], scalar=k.G0[:, n:n + 1],
                                                 in1=A1[:, u, t, :], op0=ALU.mult, op1=ALU.add)
                ins.then_inc(a2_ok, 1)
                dve.wait_ge(a2_ok, b + 1)
                v.tensor_tensor(A3[:, u], A2[:, u], k.gb[:, b:b + 1, :].broadcast_to([P, TB, C]),
                                ALU.mult).then_inc(a3_ok, 1)
                dve.wait_ge(a3_ok, b + 1)
                v.tensor_tensor(R[:, b], A3[:, u], k.X[:, b * TB:b * TB + TB, :], ALU.add).then_inc(r_ok, 1)

        @block.sync
        def _(sp):
            o = out.rearrange("b (t p) c -> b p t c", p=P)
            for b in range(B):
                sp.wait_ge(r_ok, b + 1)
                sp.dma_start(o[b], R[:, b]).then_inc(r_out, 16)
            sp.wait_ge(r_out, 16 * B)


def build(nc, a, out):
    k = Tensors()
    k.XS = nc.dram_tensor("sorted_tokens", [NX * P, C], F32).ap()
    k.YS = nc.dram_tensor("sorted_outputs", [NX * P, C], F32).ap()
    with ExitStack() as ctx:
        def sb(name, shape, dt=F32):
            return ctx.enter_context(nc.sbuf_tensor(name, shape, dt))

        pairs_s = [ctx.enter_context(nc.psum_tensor(f"pair_s{i}", [P, 2, T], F32)) for i in range(2)]
        singles = [ctx.enter_context(nc.psum_tensor(f"bank{i}", [P, T], F32)) for i in range(4)]
        banks = [pairs_s[0][:, 0, :], pairs_s[0][:, 1, :], pairs_s[1][:, 0, :], pairs_s[1][:, 1, :]] + \
                [s[:, :] for s in singles]

        k.X = sb("X", [P, NT, C])
        k.O = sb("O", [P, NT, C])
        k.H2 = sb("H2", [P, NT, C])
        k.gb = sb("gb", [P, B, C])
        k.ident = sb("ident", [P, P])
        k.identb = sb("identb", [P, P], BF16)
        k.cmask = sb("cmask", [P, T])
        k.sac = sb("sac", [P, B])
        k.cac = sb("cac", [P, B])
        k.wq1 = sb("wq1", [P, C])
        k.wk1 = sb("wk1", [P, C])
        k.wv1 = sb("wv1", [P, C])
        k.wo1 = sb("wo1", [P, C])
        k.wq2 = sb("wq2", [P, C])
        k.wk2 = sb("wk2", [P, C])
        k.wv2 = sb("wv2", [P, C])
        k.wo2 = sb("wo2", [P, C])
        k.bv2 = sb("bv2", [P, C])
        k.bo_bc = sb("bo_bc", [P, C])
        k.g2_bc = sb("g2_bc", [P, C])
        k.b2_bc = sb("b2_bc", [P, C])
        k.rb2_bc = sb("rb2_bc", [P, C])
        k.bqk2 = sb("bqk2", [P, 2])
        k.zcol = sb("zcol", [P, 2])
        k.ln1c = sb("ln1c", [P, 2])
        k.eb1T = sb("eb1T", [P, E * FT])
        k.rb1T = sb("rb1T", [P, FT])
        k.rstd = sb("rstd", [P, NT])
        k.nmr = sb("nmr", [P, NT])
        k.mhalf = sb("mhalf", [P, NT])

        with ExitStack() as first:
            k.BR = first.enter_context(nc.sbuf_tensor("BR", [P, B, 3, C], F32))
            load_and_tables(nc, k, a, banks)
            stats(nc, k, k.X, "st1")
            with ExitStack() as attn:
                k.QKS = attn.enter_context(nc.sbuf_tensor("QKS", [P, 2, 3, B * T], BF16))
                k.V = attn.enter_context(nc.sbuf_tensor("V", [P, NT, C], F32))
                norm_and_project(nc, k, k.X, k.wq1, k.wk1, k.wv1, k.zcol, k.zcol[:, 0:1].broadcast_to([P, C]),
                                 lambda b: k.cac[:, bass.ds(b, 1)], lambda b: k.sac[:, bass.ds(b, 1)],
                                 banks, "np1")
                attention(nc, k, True, pairs_s, banks[4:6], banks[6], banks[7], "at1")
            out_project(nc, k, k.wo1, banks, "op1", None, k.X, k.BR[:, :, 0, :])
            stats(nc, k, k.X, "st2")
            modulate(nc, k, k.X, k.H2, lambda b: k.BR[:, bass.ds(b, 1), 2, :],
                     lambda b: k.BR[:, bass.ds(b, 1), 1, :], "mo2")
        stats(nc, k, k.H2, "st3")
        with ExitStack() as attn:
            k.QKS = attn.enter_context(nc.sbuf_tensor("QKS2", [P, 2, 3, B * T], BF16))
            k.V = attn.enter_context(nc.sbuf_tensor("V2", [P, NT, C], F32))
            norm_and_project(nc, k, k.H2, k.wq2, k.wk2, k.wv2, k.bqk2, k.bv2,
                             lambda b: k.ln1c[:, 0:1], lambda b: k.ln1c[:, 1:2], banks, "np2")
            attention(nc, k, False, pairs_s, banks[4:6], banks[6], banks[7], "at2")
        out_project(nc, k, k.wo2, banks, "op2", k.bo_bc, k.H2, None)
        stats(nc, k, k.H2, "st4")
        k.RM = sb("RM", [P, NT, C])
        k.LG = sb("LG", [P, NT, E + 2])
        k.G0 = sb("G0", [P, NT])
        k.G1 = sb("G1", [P, NT])
        k.DI = sb("DI", [P, NT], mybir.dt.uint32)
        k.TE = sb("TE", [P, NX], I32)
        gate_and_residual(nc, k, a, banks)
        route(nc, k, banks)
        experts(nc, k, a, banks)
        combine(nc, k, out)


_OUTS = [((B, T, C), "float32")]


def kernel(**inputs):
    import numpy as _np
    import concourse.bacc as _bacc
    from concourse import mybir as _mybir
    from concourse.bass_utils import run_bass_kernel_spmd as _run

    nc = _bacc.Bacc("TRN2", target_bir_lowering=False, num_devices=1)
    arrays, args = {}, {}
    for name in inputs:
        arr = _np.ascontiguousarray(inputs[name])
        arrays[f"in_{name}"] = arr
        args[name] = nc.dram_tensor(f"in_{name}", arr.shape, _mybir.dt.from_np(arr.dtype),
                                    kind="ExternalInput").ap()
    shape, dtype = _OUTS[0]
    out = nc.dram_tensor("out_0", shape, _mybir.dt.from_np(_np.dtype(dtype)), kind="ExternalOutput").ap()
    build(nc, args, out)
    r = _run(nc, [arrays], core_ids=[0])
    return r.results[0]["out_0"]
```

```python
from contextlib import ExitStack

import concourse.bass as bass
from concourse import mybir

F32 = mybir.dt.float32
BF16 = mybir.dt.bfloat16
I32 = mybir.dt.int32
ACT = mybir.ActivationFunctionType
ALU = mybir.AluOpType
AX = mybir.AxisListType

P = 128
B, T, C = 8, 512, 128
H, D = 16, 8
TB = T // P
NT = B * TB
E, F = 8, 512
FT = F // P
EPS = 1e-5
SCALE = float(D) ** -0.5
BIG = 3.0e38
NG = 4
HG = H // NG
UN = NG * TB
Q_PARTS = (0, 0, 0, 1, 1, 2)
K_PARTS = (0, 1, 2, 0, 1, 0)
NR = len(Q_PARTS)
KS_ROWS = NR * D
NX = NT + E
KT_ROWS = KS_ROWS + 3
N_HALF = 16 * 2 * NR


class Tensors:
    pass


def head_of(g, i):
    par, p = i % 2, 2 * g + i // 2
    return par * (H // 2) + p


def in_pairs(eng, body, count=B):
    body(0, 0)
    body(1, 1)
    with eng.Fori(2, count - 1, 2) as n:
        body(n, 0)
        body(n + 1, 1)


def in_turns(eng, body, count=B):
    body(0, 0)
    body(1, 1)
    with eng.Fori(2, count - 3, 2) as n:
        body(n, 0)
        body(n + 1, 1)
    body(count - 2, 0)
    body(count - 1, 1)


def later(n, first=2):
    return not (type(n) is int and n < first)


def load_score_rows(sp, k, n, u, half):
    for par in range(2):
        src = (2 * half + par) * 32
        for j in range(NR):
            dst = 64 * par + D * j
            q_slot, k_slot = Q_PARTS[j], 3 + K_PARTS[j]
            sp.dma_start(k.ST[u][dst:dst + D, HG * half:HG * half + HG, :, :],
                         k.QKS[src:src + 32, q_slot:k_slot + 1:k_slot - q_slot, bass.ds(n * T, T)]
                         ).then_inc(k.stk[u][half], 16)


def load_and_tables(nc, k, a, banks):
    with ExitStack() as ctx:
        def sb(name, shape, dt=F32):
            return ctx.enter_context(nc.sbuf_tensor(name, shape, dt))

        def sem(name):
            return ctx.enter_context(nc.semaphore(name))

        wqk_nat = sb("wqk_nat", [P, 3, C])
        wout_nat = sb("wout_nat", [P, C])
        wout_perm = sb("wout_perm", [P, C])
        wqkv2 = sb("wqkv2", [P, 3 * C])
        b1_nat = sb("b1_nat", [E * FT, P])
        rb1_nat = sb("rb1_nat", [FT, P])
        bqk_nat = sb("bqk_nat", [2, C])
        bqk_perm = sb("bqk_perm", [2, C])
        ln1_nat = sb("ln1_nat", [2, C])
        c_nat = sb("c_nat", [B, C])
        c_exp = sb("c_exp", [B, C])
        c_one = sb("c_one", [B, C])
        c_rec = sb("c_rec", [B, C])
        c_silu = sb("c_silu", [B, C])
        siluT = sb("siluT", [P, B])
        wmod = sb("wmod", [P, 6 * C])
        silu_bc, gabs, gsgn, gneg = (k.O[:, B * i:B * i + B, :] for i in range(4))

        x_in = sem("lt_x_in")
        c_in = sem("lt_c_in")
        w_in = sem("lt_w_in")
        consts0 = sem("lt_consts0")
        ident_ok = sem("lt_ident_ok")
        exp_ok = sem("lt_exp_ok")
        chain = sem("lt_chain")
        silu_ok = sem("lt_silu_ok")
        siluT_ps = sem("lt_siluT_ps")
        siluT_ok = sem("lt_siluT_ok")
        mod_ps = sem("lt_mod_ps")
        br_ps = sem("lt_br_ps")
        br_ok = sem("lt_br_ok")
        wt_ps = sem("lt_wt_ps")
        perm_ok = sem("lt_perm_ok")
        wt_free = sem("lt_wt_free")
        filled = sem("lt_filled")

        block = ctx.enter_context(nc.Block())

        @block.sync
        def _(sp):
            sp.dma_start(c_nat[:, :], a["L0_c"]).then_inc(c_in, 16)
            sp.dma_start(wmod[:, :], a["L0_wmod"]).then_inc(c_in, 16)
            xv = a["L0_attn_x"].rearrange("b (t p) c -> p (b t) c", p=P)
            for b in range(B):
                sp.dma_start(k.X[:, TB * b:TB * b + TB, :], xv[:, TB * b:TB * b + TB, :]).then_inc(x_in, 16)
            for part in range(2):
                wv = a["L0_attn_w_qkv"][part * C:part * C + C, :].rearrange(
                    "(par half p d) c -> half par d p c", par=2, half=2, d=D)
                for half in range(2):
                    for par in range(2):
                        r = (2 * half + par) * 32
                        sp.dma_start(wqk_nat[r:r + 32, part, :], wv[half, par]).then_inc(w_in, 16)
            sp.dma_start(wqk_nat[:, 2, :], a["L0_attn_w_qkv"][2 * C:3 * C, :]).then_inc(w_in, 16)
            sp.dma_start(wout_nat[:, :], a["L0_attn_w_out"]).then_inc(w_in, 16)
            sp.dma_start(wqkv2[:, :], a["L0_ffn_Wqkv"]).then_inc(w_in, 16)
            sp.dma_start(b1_nat[:, :], a["L0_ffn_b1"].rearrange("e (t f) -> (e t) f", f=P)).then_inc(w_in, 16)
            sp.dma_start(rb1_nat[:, :], a["L0_ffn_rb1"].rearrange("(t f) -> t f", f=P)).then_inc(w_in, 16)
            for g in range(NG):
                for i in range(HG):
                    h = head_of(g, i)
                    r = g * 32 + i * D
                    sp.dma_start(k.wo2[r:r + D, :], a["L0_ffn_Wo"][h * D:h * D + D, :]).then_inc(w_in, 16)
            sp.dma_start(bqk_nat[:, :], a["L0_ffn_bqkv"][0:2 * C].rearrange("(s c) -> s c", c=C)).then_inc(w_in, 16)
            for row, name in enumerate(("L0_ffn_ln1_g", "L0_ffn_ln1_b")):
                sp.dma_start(ln1_nat[row:row + 1, :], a[name].rearrange("(o c) -> o c", o=1)).then_inc(w_in, 16)
            sp.dma_start(k.bv2[:, :], a["L0_ffn_bqkv"][2 * C:3 * C].partition_broadcast(P)).then_inc(w_in, 16)
            for dst, name in ((k.bo_bc, "L0_ffn_bo"), (k.g2_bc, "L0_ffn_ln2_g"), (k.b2_bc, "L0_ffn_ln2_b"),
                              (k.rb2_bc, "L0_ffn_rb2")):
                sp.dma_start(dst[:, :], a[name].partition_broadcast(P)).then_inc(w_in, 16)
            n = 2 * 4 + 1 + 1 + 1 + 1 + 1 + H + 1 + 2 + 1 + 4
            sp.wait_ge(w_in, 16 * n)
            sp.wait_ge(x_in, 16 * B)

        N_W = 16 * (2 * 4 + 1 + 1 + 1 + 1 + 1 + H + 1 + 2 + 1 + 4)

        @block.gpsimd
        def _(pool):
            pool.memset(k.ident[:, :], 0.0).then_inc(consts0, 1)
            pool.memset(k.cmask[:, :], 0.0).then_inc(consts0, 1)
            pool.memset(k.zcol[:, :], 0.0).then_inc(ident_ok, 1)
            pool.wait_ge(consts0, 2)
            pool.affine_select(out=k.ident[:, :], in_=k.ident[:, :], compare_op=ALU.not_equal, fill=1.0,
                               base=0, pattern=[[-1, P]], channel_multiplier=1).then_inc(ident_ok, 1)
            dg = k.cmask[:, T - P:T]
            pool.affine_select(out=dg, in_=dg, compare_op=ALU.is_ge, fill=-BIG,
                               base=0, pattern=[[-1, P]], channel_multiplier=1).then_inc(ident_ok, 1)
            pool.wait_ge(ident_ok, 3)
            pool.tensor_copy(k.identb[:, :], k.ident[:, :]).then_inc(ident_ok, 1)
            for u in range(2):
                pool.memset(k.ST[u][:, :, 1, :], -1.0)
            pool.memset(k.VA[:, :, :, :, :], 0.0).then_inc(filled, 1)
            pool.wait_ge(filled, 1)
            pool.memset(k.VA[:, :, :, :, D:D + 1], 1.0)

        @block.scalar
        def _(act):
            act.wait_ge(c_in, 32)
            act.activation(c_exp[:, :], c_nat[:, :], ACT.Exp, scale=-1.0).then_inc(exp_ok, 1)
            for b in range(B):
                act.wait_ge(br_ps, b + 1)
                act.activation(k.gb[:, b, :], banks[b][:, 3 * C:4 * C], ACT.Copy)
                act.activation(k.BR[:, b, :, :], banks[b][:, 0:3 * C].rearrange("p (j c) -> p j c", j=3),
                               ACT.Copy).then_inc(br_ok, 1)

        @block.vector
        def _(dve):
            dve.wait_ge(exp_ok, 1)
            nc.vector.tensor_scalar(c_one[:, :], c_exp[:, :], 1.0, None, ALU.add).then_inc(chain, 1)
            dve.wait_ge(chain, 1)
            nc.vector.reciprocal(c_rec[:, :], c_one[:, :]).then_inc(chain, 1)
            dve.wait_ge(chain, 2)
            nc.vector.tensor_tensor(c_silu[:, :], c_nat[:, :], c_rec[:, :], ALU.mult).then_inc(silu_ok, 1)
            dve.wait_ge(siluT_ps, 1)
            nc.vector.tensor_copy(siluT[:, :], banks[0][:, 0:B]).then_inc(chain, 1)
            dve.wait_ge(chain, 3)
            nc.vector.tensor_copy(silu_bc[:, :, :],
                                  siluT[:, :].unsqueeze(2).broadcast_to([P, B, P])).then_inc(siluT_ok, 1)
            dve.wait_ge(mod_ps, 1)
            nc.vector.tensor_copy(k.sac[:, :], banks[1][:, 0:B])
            nc.vector.tensor_scalar(k.cac[:, :], banks[1][:, B:2 * B], 1.0, None, ALU.add).then_inc(wt_free, 1)
            dve.wait_ge(br_ok, B)
            n = 3
            for g in (k.BR[:, :, 0, :], k.gb[:, :, :]):
                nc.vector.tensor_scalar(gsgn[:, :, :], g, 0.0, 2.0, ALU.is_ge, ALU.mult)
                nc.vector.scalar_tensor_tensor(out=gneg[:, :, :], in0=g, scalar=-1.0, in1=g,
                                               op0=ALU.mult, op1=ALU.max).then_inc(chain, 1)
                n += 1
                dve.wait_ge(chain, n)
                nc.vector.tensor_scalar(gabs[:, :, :], gneg[:, :, :], 0.25, None, ALU.max).then_inc(chain, 1)
                n += 1
                dve.wait_ge(chain, n)
                nc.vector.scalar_tensor_tensor(out=g, in0=gsgn[:, :, :], scalar=-1.0, in1=gabs[:, :, :],
                                               op0=ALU.add, op1=ALU.mult).then_inc(chain, 1)
                n += 1
                dve.wait_ge(chain, n)
            nc.vector.tensor_scalar(k.BR[:, :, 2, :], k.BR[:, :, 2, :], 1.0, None, ALU.add)
            dve.wait_ge(w_in, N_W)
            for g in range(NG):
                src = wout_nat[:, :].rearrange("o (par g pp d) -> o g pp par d", par=2, g=NG, d=D)[:, g]
                last = nc.vector.tensor_copy(
                    wout_perm[:, g * 32:g * 32 + 32].rearrange("o (pp par d) -> o pp par d", pp=2, par=2), src)
            src = bqk_nat[:, :].rearrange("s (par half p d) -> s half par d p", par=2, half=2, d=D)
            for half in range(2):
                for par in range(2):
                    r = (2 * half + par) * 32
                    last = nc.vector.tensor_copy(bqk_perm[:, r:r + 32].rearrange("s (d p) -> s d p", d=D),
                                                 src[:, half, par])
            last.then_inc(perm_ok, 1)
            for part, dst in ((0, k.wq2), (1, k.wk2)):
                src = wqkv2[:, part * C:part * C + C].rearrange("c (par half p d) -> c half par d p",
                                                               par=2, half=2, d=D)
                for half in range(2):
                    for par in range(2):
                        r = (2 * half + par) * 32
                        nc.vector.tensor_copy(dst[:, r:r + 32].rearrange("c (d p) -> c d p", d=D),
                                              src[:, half, par])
            nc.vector.tensor_copy(k.wv2[:, :], wqkv2[:, 2 * C:3 * C])
            for n, (dst, cols) in enumerate(((k.wq1, C), (k.wk1, C), (k.wv1, C), (k.wo1, C),
                                             (k.eb1T, E * FT), (k.rb1T, FT), (k.bqk2, 2), (k.ln1c, 2))):
                dve.wait_ge(wt_ps, n + 1)
                nc.vector.tensor_copy(dst[:, :], banks[(2 + n) % 8][:, 0:cols])

        @block.tensor
        def _(pe):
            pe.wait_ge(ident_ok, 4)
            pe.wait_ge(silu_ok, 1)
            pe.transpose(banks[0][:, 0:B], c_silu[:, :], k.ident[0:B, 0:B]).then_inc(siluT_ps, 1)
            pe.wait_ge(siluT_ok, 1)
            for j in range(2):
                mm = pe.matmul(banks[1][:, B * j:B * j + B], wmod[:, C * j:C * j + C], silu_bc[:, :, 0],
                               start=True, stop=True)
            mm.then_inc(mod_ps, 1)
            for b in range(B):
                if b == 1:
                    pe.wait_ge(wt_free, 1)
                pe.matmul(banks[b][:, :], silu_bc[:, b, :], wmod[:, 2 * C:6 * C],
                          start=True, stop=True).then_inc(br_ps, 1)
            pe.wait_ge(w_in, N_W)
            pe.wait_ge(br_ok, B)
            for n in range(3):
                pe.transpose(banks[2 + n][:, 0:C], wqk_nat[:, n, :], k.ident[:, :]).then_inc(wt_ps, 1)
            pe.wait_ge(perm_ok, 1)
            pe.transpose(banks[5][:, 0:C], wout_perm[:, :], k.ident[:, :]).then_inc(wt_ps, 1)
            pe.transpose(banks[6][:, 0:E * FT], b1_nat[:, :], k.ident[0:E * FT, 0:E * FT]).then_inc(wt_ps, 1)
            pe.transpose(banks[7][:, 0:FT], rb1_nat[:, :], k.ident[0:FT, 0:FT]).then_inc(wt_ps, 1)
            pe.transpose(banks[0][:, 0:2], bqk_perm[:, :], k.ident[0:2, 0:2]).then_inc(wt_ps, 1)
            pe.transpose(banks[1][:, 0:2], ln1_nat[:, :], k.ident[0:2, 0:2]).then_inc(wt_ps, 1)


def stats(nc, k, src, tag):
    with ExitStack() as ctx:
        def sem(name):
            return ctx.enter_context(nc.semaphore(f"{tag}_{name}"))

        st_ok, mv_ok, ve_ok, rs_ok = sem("st_ok"), sem("mv_ok"), sem("ve_ok"), sem("rs_ok")
        six = ctx.enter_context(nc.sbuf_tensor(f"{tag}_six", [P, NT, 6], F32))
        mv = ctx.enter_context(nc.sbuf_tensor(f"{tag}_mv", [P, NT, 2], F32))
        ve = ctx.enter_context(nc.sbuf_tensor(f"{tag}_ve", [P, NT], F32))
        block = ctx.enter_context(nc.Block())

        @block.vector
        def _(dve):
            with dve.Fori(0, NT - 7, 8) as t:
                for i in range(8):
                    last = nc.vector.bn_stats(six[:, bass.ds(t + i, 1), :], src[:, bass.ds(t + i, 1), :])
                last.then_inc(st_ok, 1)
            dve.wait_ge(st_ok, NT // 8)
            for i in range(NT):
                last = nc.vector.bn_aggr(mv[:, i, :], six[:, i, :])
            last.then_inc(mv_ok, 1)
            dve.wait_ge(mv_ok, 1)
            nc.vector.tensor_scalar(ve[:, :], mv[:, :, 1], EPS, None, ALU.add).then_inc(ve_ok, 1)
            dve.wait_ge(rs_ok, 1)
            nc.vector.scalar_tensor_tensor(out=k.nmr[:, :], in0=mv[:, :, 0], scalar=-1.0, in1=k.rstd[:, :],
                                           op0=ALU.mult, op1=ALU.mult)

        @block.gpsimd
        def _(pool):
            pool.memset(k.mhalf[:, :], -0.5).then_inc(ve_ok, 1)
            pool.wait_ge(ve_ok, 2)
            pool.tensor_tensor(k.rstd[:, :], ve[:, :], k.mhalf[:, :], ALU.pow).then_inc(rs_ok, 1)


def norm_and_project(nc, k, src, wq, wk, wv, bqk, bv, scale_of, shift_of, banks, tag):
    with ExitStack() as ctx:
        def sb(name, shape, dt=F32):
            return ctx.enter_context(nc.sbuf_tensor(f"{tag}_{name}", shape, dt))

        def sem(name):
            return ctx.enter_context(nc.semaphore(f"{tag}_{name}"))

        XN = sb("XN", [P, 2, TB, C])
        HT = sb("HT", [P, 2, T])
        RE = sb("RE", [P, 2, 2, T])
        xn_ok = sem("xn_ok")
        tr_ps = sem("tr_ps")
        ht_ok = sem("ht_ok")
        qk_ps = sem("qk_ps")
        v_ps = sem("v_ps")
        s1_ok = sem("s1_ok")
        re_ok = sem("re_ok")
        s2_ok = sem("s2_ok")
        s3_ok = sem("s3_ok")
        v_ok = sem("v_ok")
        block = ctx.enter_context(nc.Block())

        def bank(u, j):
            return banks[4 * u + j]

        def is_last(b):
            return type(b) is int and b == B - 1

        @block.sync
        def _(sp):
            for b in range(2):
                sp.wait_ge(s3_ok, 2 * b + 2)
                for half in range(2):
                    load_score_rows(sp, k, b, b, half)

        @block.vector
        def _(dve):
            def normalise(b, u):
                if later(b):
                    dve.wait_ge(tr_ps, b - 1)
                for t in range(TB):
                    tile = b * TB + t
                    last = nc.vector.tensor_scalar(
                        XN[:, u, t, :], src[:, bass.ds(tile, 1), :], k.rstd[:, bass.ds(tile, 1)],
                        k.nmr[:, bass.ds(tile, 1)], ALU.mult, ALU.add)
                last.then_inc(xn_ok, 1)

            def step(b, u):
                if not is_last(b):
                    normalise(b + 1, 1 - u)
                for side in range(2):
                    dve.wait_ge(s1_ok, 2 * b + side + 1)
                    nc.vector.scalar_tensor_tensor(
                        out=RE[:, u, side, :], in0=bank(u, 1 + side)[:, :], scalar=bqk[:, side:side + 1],
                        in1=k.QKS[:, 3 * side, bass.ds(b * T, T)], op0=ALU.add,
                        op1=ALU.subtract).then_inc(re_ok, 1)
                dve.wait_ge(v_ps, b + 1)
                nc.vector.tensor_tensor(
                    k.V[:, bass.ds(b * TB, TB), :], bank(u, 3)[:, :].rearrange("p (t c) -> p t c", t=TB),
                    bv[:, :].unsqueeze(1).broadcast_to([P, TB, C]), ALU.add).then_inc(v_ok, 1)
                for side in range(2):
                    dve.wait_ge(s2_ok, 2 * b + side + 1)
                    nc.vector.tensor_tensor(
                        k.QKS[:, 3 * side + 2, bass.ds(b * T, T)], RE[:, u, side, :],
                        k.QKS[:, 3 * side + 1, bass.ds(b * T, T)], ALU.subtract).then_inc(s3_ok, 1)

            normalise(0, 0)
            in_turns(dve, step)

        @block.tensor
        def _(pe):
            def turn(b, u):
                pe.wait_ge(xn_ok, b + 1)
                if later(b):
                    pe.wait_ge(ht_ok, b - 1)
                for t in range(TB):
                    mm = pe.transpose(bank(u, 0)[:, t * P:t * P + P], XN[:, u, t, :], k.ident[:, :])
                mm.then_inc(tr_ps, 1)

            def step(b, u):
                pe.wait_ge(ht_ok, b + 1)
                if later(b):
                    pe.wait_ge(re_ok, 2 * (b - 1))
                pe.matmul(bank(u, 1)[:, :], wq[:, :], HT[:, u, :], start=True, stop=True).then_inc(qk_ps, 1)
                pe.matmul(bank(u, 2)[:, :], wk[:, :], HT[:, u, :], start=True, stop=True).then_inc(qk_ps, 1)
                if not is_last(b):
                    turn(b + 1, 1 - u)
                if later(b):
                    pe.wait_ge(v_ok, b - 1)
                for t in range(TB):
                    mm = pe.matmul(bank(u, 3)[:, t * P:t * P + P], HT[:, u, t * P:t * P + P], wv[:, :],
                                   start=True, stop=True)
                mm.then_inc(v_ps, 1)

            turn(0, 0)
            in_turns(pe, step)

        @block.scalar
        def _(act):
            def turned(b, u):
                act.wait_ge(tr_ps, b + 1)
                if later(b):
                    act.wait_ge(v_ps, b - 1)
                act.activation(HT[:, u, :], bank(u, 0)[:, :], ACT.Identity, bias=shift_of(b),
                               scale=scale_of(b)).then_inc(ht_ok, 1)

            def step(b, u):
                for side in range(2):
                    act.wait_ge(qk_ps, 2 * b + side + 1)
                    act.activation(k.QKS[:, 3 * side, bass.ds(b * T, T)], bank(u, 1 + side)[:, :],
                                   ACT.Identity, bias=bqk[:, side:side + 1]).then_inc(s1_ok, 1)
                if not is_last(b):
                    turned(b + 1, 1 - u)
                for side in range(2):
                    act.wait_ge(re_ok, 2 * b + side + 1)
                    act.activation(k.QKS[:, 3 * side + 1, bass.ds(b * T, T)], RE[:, u, side, :],
                                   ACT.Copy).then_inc(s2_ok, 1)

            turned(0, 0)
            in_turns(act, step)


def wait_apart(eng, sem, value, ready=None):
    value = value if type(value) is int else eng.to_reg(value)
    if ready is not None:
        eng.wait_ge(*ready)
    eng.wait_ge(sem, value)


def attention(nc, k, causal, pairs_s, banks_t, bank_o, bank_m, spare, tag):
    sems = []
    with ExitStack() as ctx:
        def sb(name, shape, dt=F32):
            return ctx.enter_context(nc.sbuf_tensor(f"{tag}_{name}", shape, dt))

        def sem(name):
            sems.append(nc.alloc_semaphore(name=f"{tag}_{name}"))
            return sems[-1]

        ST, VA = k.ST, k.VA
        PT = ([spare[:, 16:32, :].rearrange("p (h t) c -> p h (t c)", h=HG)] +
              [sb(f"PT{kt}", [P, HG, T - kt * P]) for kt in range(1, TB)] if causal else
              [sb(f"PT{j}", [P, HG, T]) for j in range(2)])
        NB = len(PT)
        LAG = NB // 2
        MX = sb("MX", [P, 2, TB, 2, HG])
        MR = sb("MR", [P, 2, TB, 2, HG])
        M3 = sb("M3", [P, 2, TB, 2, 3, HG], BF16)
        MT = sb("MT", [6 * HG, 2, T], BF16)
        OT = spare[:, 0:8, :].rearrange("p (g t) c -> p g (t c)", g=2)
        RD = sb("RD", [P, 2, TB, HG])
        JK = (spare[:, 8:16, :].rearrange("p t c -> p (t c)").bitcast(BF16).rearrange(
            "p (a b t) -> p a b t", a=2, b=2) if causal else None)

        vau = sem("vau")
        s_ps = sem("s_ps")
        red = sem("red")
        spl = sem("spl")
        m_ps = sem("m_ps")
        m_ev = sem("m_ev")
        m_row = [sem(f"m_row{h}") for h in range(2)]
        t_ps = sem("t_ps")
        ex = sem("ex")
        msk = sem("msk")
        o_pe = sem("o_pe")
        o_ev = sem("o_ev")
        o_tr = sem("o_tr")
        o_rc = sem("o_rc")
        o_nm = sem("o_nm")
        block = ctx.enter_context(nc.Block())

        STEPS = B + 1

        def width(kt):
            return T - kt * P if causal else T

        def steps(eng, step):
            step(0, 0)
            step(1, 1)
            with eng.Fori(2, B - 1, 2) as n:
                step(n, 0)
                step(n + 1, 1)
            step(B, B % 2)

        def stage(n):
            first, last = (type(n) is int and n == 0), (type(n) is int and n == B)
            second = type(n) is int and n == 1
            return not last, not first, not first and not second

        @block.sync
        def _(sp):
            def maxima_rows(n, u, half):
                sp.wait_ge(m_ev, 2 * n + half + 1)
                for par in range(2):
                    sp.dma_start(ST[u][64 * par + KS_ROWS:64 * par + KT_ROWS, HG * half:HG * half + HG, 0, :],
                                 MT[3 * HG * par:3 * HG * par + 3 * HG, half, :]).then_inc(m_row[half], 16)

            def step(n, u):
                maxima, sums, _ = stage(n)
                if sums:
                    maxima_rows(n - 1, 1 - u, 1)
                more = not (type(n) is int and n >= B - 1)
                if maxima:
                    if more and sums:
                        sp.wait_ge(t_ps, (n - 1) * UN * HG + UN * HG // 2)
                        load_score_rows(sp, k, n + 1, 1 - u, 0)
                    maxima_rows(n, u, 0)
                    if more and sums:
                        sp.wait_ge(t_ps, n * UN * HG)
                        load_score_rows(sp, k, n + 1, 1 - u, 1)

            step(0, 0)
            step(1, 1)
            with sp.Fori(2, B - 3, 2) as n:
                step(n, 0)
                step(n + 1, 1)
            step(B - 2, 0)
            step(B - 1, 1)
            step(B, 0)

        @block.tensor
        def _(pe):
            def scores_max(n, u, g, qt, pair):
                if not (type(n) is int and n == 0 and g == 0 and qt == TB - 1):
                    pe.wait_ge(red, (n * UN + g * TB + TB - 1 - qt) * 2 + pair - 1)
                w = (qt + 1) * P if causal else T
                p = 2 * g + pair
                for par in range(2):
                    r = 64 * par
                    mm = pe.matmul(pairs_s[pair][:, par, 0:w], ST[u][r:r + KS_ROWS, p, 0, qt * P:qt * P + P],
                                   ST[u][r:r + KS_ROWS, p, 1, 0:w], start=True, stop=True)
                mm.then_inc(s_ps, 1)

            def scores_exp(n, u, g, kt, pair):
                w = width(kt)
                p = 2 * g + pair
                for par in range(2):
                    at = (g * TB + kt) * HG + 2 * pair + par
                    if not (type(n) is int and n == 0 and at < 2):
                        pe.wait_ge(ex, n * UN * HG + at - 1)
                    r = 64 * par
                    pe.matmul(banks_t[par][:, 0:w], ST[u][r:r + KT_ROWS, p, 1, kt * P:kt * P + P],
                              ST[u][r:r + KT_ROWS, p, 0, T - w:T], start=True, stop=True).then_inc(t_ps, 1)

            def add_sums(n, u, g, kt):
                w = width(kt)
                unit = n * UN + g * TB + kt
                if causal:
                    pe.wait_ge(msk, unit + 1)
                else:
                    pe.wait_ge(ex, (unit + 1) * HG)
                if kt == 0:
                    if g == 0:
                        pe.wait_ge(vau, n + 1)
                    if not (type(n) is int and n == 0 and g == 0):
                        pe.wait_ge(o_ev, n * NG + g)
                for i in range(HG):
                    mm = pe.matmul(bank_o[32 * i:32 * i + 32, T - w:T], VA[:, u, kt, head_of(g, i), :],
                                   PT[kt % NB][:, i, 0:w], start=(kt == 0), stop=(kt == TB - 1))
                mm.then_inc(o_pe, 1)

            def turn_sums(n, g, halves):
                pe.wait_ge(o_ev, n * NG + g + 1)
                if not (type(n) is int and n == 0 and g == 0):
                    pe.wait_ge(o_nm, n * NG + g)
                pe.wait_ge(m_ev, halves)
                for qt in range(TB):
                    mm = pe.transpose(bank_m[:, qt * P:qt * P + P], OT[:, g % 2, qt * P:qt * P + P],
                                      k.ident[:, :])
                mm.then_inc(o_tr, 1)

            def turn_maxima(n, half, groups):
                pe.wait_ge(spl, (2 * n + half) * 4 + 4)
                if not (type(groups) is int and groups == 0):
                    pe.wait_ge(o_nm, groups)
                if not (type(n) is int and n == 0 and half == 0):
                    pe.wait_ge(m_ev, 2 * n + half)
                out = bank_m[0:6 * HG, :].bitcast(BF16)
                for qt in range(TB):
                    mm = pe.transpose(out[:, qt * P:qt * P + P],
                                      M3[:, half, qt].rearrange("p a s h -> p (a s h)"), k.identb[:, :])
                mm.then_inc(m_ps, 1)

            def step(n, u):
                maxima, sums, before = stage(n)
                for g in range(NG):
                    for kt in range(TB):
                        if maxima and g % 2 == 0 and kt == 0:
                            pe.wait_ge(k.stk[u][g // 2], n * (N_HALF // 2) + N_HALF - u * (N_HALF // 2))
                        if sums and g % 2 == 0 and kt == 0:
                            pe.wait_ge(m_row[g // 2], n * 32)
                        if sums:
                            scores_exp(n - 1, 1 - u, g, kt, 0)
                        q = g * TB + kt - LAG
                        if sums and q >= 0:
                            add_sums(n - 1, 1 - u, q // TB, q % TB)
                        elif before and q < 0:
                            add_sums(n - 2, u, NG - 1, TB + q)
                        if kt == LAG and sums:
                            if g:
                                turn_sums(n - 1, g - 1, 2 * n if g < 3 or not maxima else 2 * n + 1)
                            elif before:
                                turn_sums(n - 2, NG - 1, 2 * n - 1)
                        if sums:
                            scores_exp(n - 1, 1 - u, g, kt, 1)
                        if kt == LAG + 1 and g == 0 and sums:
                            turn_maxima(n - 1, 1, (n - 1) * NG)
                        if kt == LAG + 1 and g == 2 and maxima:
                            turn_maxima(n, 0, (n - 1) * NG + 2 if sums else 0)
                        if maxima:
                            scores_max(n, u, g, TB - 1 - kt, 0)
                            scores_max(n, u, g, TB - 1 - kt, 1)

            steps(pe, step)
            for kt in range(TB - LAG, TB):
                add_sums(B - 1, (B - 1) % 2, NG - 1, kt)
            turn_sums(B - 1, NG - 1, 2 * B)

        @block.scalar
        def _(act):
            def keep_sums(n, g):
                act.wait_ge(o_pe, (n * NG + g + 1) * TB)
                if g >= 2:
                    act.wait_ge(o_tr, n * NG + g - 1)
                elif later(n, 1):
                    act.wait_ge(o_tr, n * NG + g - 1)
                act.activation(OT[:, g % 2, :], bank_o[:, :], ACT.Copy).then_inc(o_ev, 1)

            def keep_maxima(n, half):
                act.wait_ge(m_ps, 2 * n + half + 1)
                if later(n, 1):
                    act.wait_ge(m_row[half], n * 32)
                act.activation(MT[:, half, :], bank_m[0:6 * HG, :].bitcast(BF16)[:, 0:T],
                               ACT.Copy).then_inc(m_ev, 1)

            def step(n, u):
                maxima, sums, before = stage(n)
                for g in range(NG):
                    for kt in range(TB):
                        if sums:
                            w = width(kt)
                            unit = (n - 1) * UN + g * TB + kt
                            for i in range(HG):
                                act.wait_ge(t_ps, unit * HG + i + 1)
                                if i == 0 and (before or g * TB + kt >= NB):
                                    act.wait_ge(o_pe, unit - NB + 1)
                                act.activation(PT[kt % NB][:, i, 0:w], banks_t[i % 2][:, 0:w], ACT.Exp,
                                               scale=SCALE).then_inc(ex, 1)
                            if kt == LAG - 1:
                                if g:
                                    keep_sums(n - 1, g - 1)
                                elif before:
                                    keep_sums(n - 2, NG - 1)
                        if kt == LAG + 1 and g == 0 and sums:
                            keep_maxima(n - 1, 1)
                        if kt == LAG + 1 and g == 2 and maxima:
                            keep_maxima(n, 0)

            steps(act, step)
            keep_sums(B - 1, NG - 1)

        @block.vector
        def _(dve):
            def output(n, g):
                dve.wait_ge(o_tr, n * NG + g + 1)
                t = bank_m[:, :].rearrange("p (q i c) -> p q i c", q=TB, i=HG)
                nc.vector.reciprocal(RD[:, g % 2], t[:, :, :, D]).then_inc(o_rc, 1)
                dve.wait_ge(o_rc, n * NG + g + 1)
                out = k.O[:, bass.ds(n * TB, TB), g * 32:g * 32 + 32].rearrange("p q (i d) -> p q i d", i=HG)
                nc.vector.tensor_tensor(out, t[:, :, :, 0:D],
                                        RD[:, g % 2].unsqueeze(3).broadcast_to([P, TB, HG, D]),
                                        ALU.mult).then_inc(o_nm, 1)

            def step(n, u):
                maxima, sums, before = stage(n)
                for g in range(NG):
                    for kt in range(TB):
                        qt = TB - 1 - kt
                        for pair in range(2):
                            if not maxima:
                                continue
                            if kt == 0 and pair == 0 and g % 2 == 0 and sums:
                                dve.wait_ge(spl, (2 * (n - 1) + g // 2) * 4 + 4)
                            at = (n * UN + g * TB + kt) * 2 + pair
                            wait_apart(dve, s_ps, at + 1, (s_ps, 1))
                            mx = MX[:, g // 2, qt, :, 2 * (g % 2) + pair]
                            if causal:
                                w = (qt + 1) * P
                                for par in range(2):
                                    last = nc.vector.tensor_tensor_reduce(
                                        out=JK[:, pair, par, 0:w], in0=pairs_s[pair][:, par, 0:w], in1=k.cmask[:, T - w:T],
                                        scale=1.0, scalar=-BIG, op0=ALU.add, op1=ALU.max,
                                        accum_out=mx[:, par:par + 1])
                            else:
                                last = nc.vector.tensor_reduce(mx, pairs_s[pair][:, :, :], AX.X, ALU.max)
                            last.then_inc(red, 1)
                        if kt == LAG and sums:
                            if g:
                                output(n - 1, g - 1)
                            elif before:
                                output(n - 2, NG - 1)

            steps(dve, step)
            output(B - 1, NG - 1)

        @block.gpsimd
        def _(pool):
            def stage_v(n, u):
                if later(n):
                    wait_apart(pool, o_pe, (n - 1) * UN, (vau, 1))
                pool.tensor_copy(VA[:, u, :, :, 0:D].rearrange("p t h d -> p (t h) d"),
                                 k.V[:, bass.ds(n * TB, TB), :].rearrange("p t (h d) -> p (t h) d", d=D)
                                 ).then_inc(vau, 1)

            def split_maxima(n, half):
                wait_apart(pool, red, (2 * n + half + 1) * UN, (vau, 1))
                if later(n, 1):
                    wait_apart(pool, m_ps, 2 * n + half - 1, (vau, 1))
                at = (2 * n + half) * 4
                m, r = MX[:, half], MR[:, half]
                part = [M3[:, half, :, :, s, :] for s in range(3)]
                pool.tensor_copy(part[0], m).then_inc(spl, 1)
                wait_apart(pool, spl, at + 1, (vau, 1))
                pool.tensor_tensor(r, m, part[0], ALU.subtract).then_inc(spl, 1)
                wait_apart(pool, spl, at + 2, (vau, 1))
                pool.tensor_copy(part[1], r).then_inc(spl, 1)
                wait_apart(pool, spl, at + 3, (vau, 1))
                pool.tensor_tensor(part[2], r, part[1], ALU.subtract).then_inc(spl, 1)

            def step(n, u):
                maxima, sums, _ = stage(n)
                for g in range(NG):
                    for kt in range(TB):
                        if g == 2 and kt == 0 and maxima:
                            split_maxima(n, 0)
                        if causal and sums:
                            unit = (n - 1) * UN + g * TB + kt
                            wait_apart(pool, ex, (unit + 1) * HG, (vau, 1))
                            dg = PT[kt % NB][:, :, 0:P]
                            pool.affine_select(out=dg, in_=dg, compare_op=ALU.is_ge, fill=0.0, base=0,
                                               pattern=[[0, HG], [1, P]], channel_multiplier=-1).then_inc(msk, 1)
                        if g == 0 and kt == 2 and maxima:
                            stage_v(n, u)
                if maxima:
                    split_maxima(n, 1)

            steps(pool, step)
    nc.clear_and_free_semaphores(sems)
    nc.all_engine_barrier()


def out_project(nc, k, wo, banks, tag, add_rows, into, gate):
    with ExitStack() as ctx:
        def sb(name, shape, dt=F32):
            return ctx.enter_context(nc.sbuf_tensor(f"{tag}_{name}", shape, dt))

        def sem(name):
            return ctx.enter_context(nc.semaphore(f"{tag}_{name}"))

        OB = sb("OB", [P, 2, TB, C])
        OC = sb("OC", [P, 2, T])
        YG = sb("YG", [P, 2, TB, C])
        ob_ok = sem("ob_ok")
        tr_ps = sem("tr_ps")
        oc_ok = sem("oc_ok")
        y_ps = sem("y_ps")
        yg_ok = sem("yg_ok")
        in_ok = sem("in_ok")
        block = ctx.enter_context(nc.Block())

        @block.gpsimd
        def _(pool):
            def fill(b, u):
                if later(b):
                    wait_apart(pool, tr_ps, b - 1, (ob_ok, 2))
                pool.tensor_copy(OB[:, u, :, :], k.O[:, bass.ds(b * TB, TB), :]).then_inc(ob_ok, 1)

            in_pairs(pool, fill)

        @block.tensor
        def _(pe):
            def project(b, u):
                pe.wait_ge(ob_ok, b + 1)
                for t in range(TB):
                    mm = pe.transpose(banks[2 * u][:, t * P:t * P + P], OB[:, u, t, :], k.ident[:, :])
                mm.then_inc(tr_ps, 1)
                pe.wait_ge(oc_ok, b + 1)
                if later(b):
                    pe.wait_ge(yg_ok, b - 1)
                for t in range(TB):
                    mm = pe.matmul(banks[2 * u + 1][:, t * P:t * P + P], OC[:, u, t * P:t * P + P],
                                   wo[:, :], start=True, stop=True)
                mm.then_inc(y_ps, 1)

            in_pairs(pe, project)

        @block.scalar
        def _(act):
            with act.Fori(0, B - 1, 2) as b0:
                for u in range(2):
                    b = b0 + u
                    act.wait_ge(tr_ps, b + 1)
                    act.activation(OC[:, u, :], banks[2 * u][:, :], ACT.Copy).then_inc(oc_ok, 1)

        @block.vector
        def _(dve):
            with dve.Fori(0, B - 1, 2) as b0:
                for u in range(2):
                    b = b0 + u
                    dve.wait_ge(y_ps, b + 1)
                    y = banks[2 * u + 1][:, :].rearrange("p (t c) -> p t c", t=TB)
                    if gate is not None:
                        row, op = gate[:, bass.ds(b, 1), :], ALU.mult
                    else:
                        row, op = add_rows[:, :].unsqueeze(1), ALU.add
                    nc.vector.tensor_tensor(YG[:, u], y, row.broadcast_to([P, TB, C]), op).then_inc(yg_ok, 1)
                    dve.wait_ge(yg_ok, b + 1)
                    dst = into[:, bass.ds(b * TB, TB), :]
                    nc.vector.tensor_tensor(dst, dst, YG[:, u], ALU.add).then_inc(in_ok, 1)


def modulate(nc, k, src, dst, mult, add, tag):
    with ExitStack() as ctx:
        def sem(name):
            return ctx.enter_context(nc.semaphore(f"{tag}_{name}"))

        XN = ctx.enter_context(nc.sbuf_tensor(f"{tag}_XN", [P, 2, TB, C], F32))
        XM = ctx.enter_context(nc.sbuf_tensor(f"{tag}_XM", [P, 2, TB, C], F32))
        xn_ok, xm_ok, out_ok = sem("xn_ok"), sem("xm_ok"), sem("out_ok")
        block = ctx.enter_context(nc.Block())

        @block.vector
        def _(dve):
            def scale(b, u):
                if later(b):
                    dve.wait_ge(out_ok, b - 1)
                for t in range(TB):
                    tile = b * TB + t
                    last = nc.vector.tensor_scalar(
                        XN[:, u, t, :], src[:, bass.ds(tile, 1), :], k.rstd[:, bass.ds(tile, 1)],
                        k.nmr[:, bass.ds(tile, 1)], ALU.mult, ALU.add)
                last.then_inc(xn_ok, 1)
                dve.wait_ge(xn_ok, b + 1)
                nc.vector.tensor_tensor(XM[:, u], XN[:, u], mult(b).broadcast_to([P, TB, C]),
                                        ALU.mult).then_inc(xm_ok, 1)

            in_pairs(dve, scale)

        @block.gpsimd
        def _(pool):
            with pool.Fori(0, B - 1, 2) as b0:
                for u in range(2):
                    b = b0 + u
                    wait_apart(pool, xm_ok, b + 1)
                    pool.tensor_tensor(dst[:, bass.ds(b * TB, TB), :], XM[:, u],
                                       add(b).broadcast_to([P, TB, C]), ALU.add).then_inc(out_ok, 1)


def gate_and_residual(nc, k, a, banks):
    NL = E + 2
    with ExitStack() as ctx:
        def sb(name, shape, dt=F32):
            return ctx.enter_context(nc.sbuf_tensor(f"gr_{name}", shape, dt))

        def sem(name):
            return ctx.enter_context(nc.semaphore(f"gr_{name}"))

        gw = sb("gw", [P, NL])
        cb = sb("cb", [P, NL])
        rw1 = sb("rw1", [P, F])
        rw2 = sb("rw2", [P, FT, C])
        XN = sb("XN", [P, 2, TB, C])
        XM = sb("XM", [P, 2, TB, C])
        OB = sb("OB", [P, 2, TB, C])
        XC = sb("XC", [P, 2, T])
        GE = sb("GE", [P, 2, FT, T])
        zero = sb("zero", [P, 4 * C])
        w_in = sem("w_in")
        z_in = sem("z_in")
        z_ok = sem("z_ok")
        xn_ok = sem("xn_ok")
        xm_ok = sem("xm_ok")
        xt_ok = sem("xt_ok")
        kept = sem("kept")
        tr_ps = sem("tr_ps")
        xc_ok = sem("xc_ok")
        lg_ps = sem("lg_ps")
        lg_ok = sem("lg_ok")
        up_ps = sem("up_ps")
        ge_ok = sem("ge_ok")
        dn_ps = sem("dn_ps")
        rm_ok = sem("rm_ok")
        block = ctx.enter_context(nc.Block())

        @block.sync
        def _(sp):
            sp.wait_ge(z_ok, 2)
            sp.dma_start(gw[:, 0:E], a["L0_ffn_gate_w"]).then_inc(w_in, 16)
            sp.dma_start(gw[:, E:NL], a["L0_ffn_coef_w"]).then_inc(w_in, 16)
            sp.dma_start(cb[:, E:NL], a["L0_ffn_coef_b"].partition_broadcast(P)).then_inc(w_in, 16)
            sp.dma_start(rw1[:, :], a["L0_ffn_rW1"]).then_inc(w_in, 16)
            sp.dma_start(rw2[:, :, :], a["L0_ffn_rW2"].rearrange("(t f) d -> f t d", f=P)).then_inc(w_in, 16)
            sp.wait_ge(tr_ps, 2)
            for e in range(E):
                sp.dma_start(k.W1[:, e, :], a["L0_ffn_W1"][e]).then_inc(z_in, 16)
                sp.dma_start(k.W2[:, e, :, :], a["L0_ffn_W2"][e].rearrange("(t f) d -> f t d", f=P)
                             ).then_inc(z_in, 16)
            for n in range(NX // 4):
                sp.dma_start(k.XS[4 * P * n:4 * P * n + 4 * P, :].rearrange("(t p) c -> p t c", p=P),
                             zero[:, :].rearrange("p (t c) -> p t c", t=4)).then_inc(z_in, 16)
            sp.wait_ge(z_in, 16 * (2 * E + NX // 4))

        @block.gpsimd
        def _(pool):
            pool.memset(cb[:, :], 0.0).then_inc(z_ok, 1)
            pool.memset(zero[:, :], 0.0).then_inc(z_ok, 1)
            pool.wait_ge(z_ok, 2)
            with pool.Fori(0, B - 1, 2) as b0:
                for u in range(2):
                    b = b0 + u
                    wait_apart(pool, xt_ok, b + 1, (z_ok, 2))
                    pool.tensor_copy(k.O[:, bass.ds(b * TB, TB), :], OB[:, u]).then_inc(kept, 1)

        @block.vector
        def _(dve):
            def normalise(b, u):
                for t in range(TB):
                    tile = b * TB + t
                    last = nc.vector.tensor_scalar(
                        XN[:, u, t, :], k.H2[:, bass.ds(tile, 1), :], k.rstd[:, bass.ds(tile, 1)],
                        k.nmr[:, bass.ds(tile, 1)], ALU.mult, ALU.add)
                last.then_inc(xn_ok, 1)
                dve.wait_ge(xn_ok, b + 1)
                nc.vector.tensor_tensor(XM[:, u], XN[:, u], k.g2_bc[:, :].unsqueeze(1).broadcast_to([P, TB, C]),
                                        ALU.mult).then_inc(xm_ok, 1)
                dve.wait_ge(xm_ok, b + 1)
                if later(b):
                    dve.wait_ge(tr_ps, b - 1)
                    dve.wait_ge(kept, b - 1)
                nc.vector.tensor_tensor(OB[:, u], XM[:, u],
                                        k.b2_bc[:, :].unsqueeze(1).broadcast_to([P, TB, C]),
                                        ALU.add).then_inc(xt_ok, 1)

            def logits(b, u):
                dve.wait_ge(lg_ps, b + 1)
                nc.vector.tensor_tensor(
                    k.LG[:, bass.ds(b * TB, TB), :], banks[6 + u][:, 0:TB * NL].rearrange("p (t e) -> p t e", t=TB),
                    cb[:, :].unsqueeze(1).broadcast_to([P, TB, NL]), ALU.add).then_inc(lg_ok, 1)

            def residual(b, u):
                dve.wait_ge(dn_ps, b + 1)
                nc.vector.tensor_tensor(
                    k.RM[:, bass.ds(b * TB, TB), :], banks[4 + u].rearrange("p (t c) -> p t c", t=TB),
                    k.rb2_bc[:, :].unsqueeze(1).broadcast_to([P, TB, C]), ALU.add).then_inc(rm_ok, 1)

            def step(b, u):
                if not (type(b) is int and b == B - 1):
                    normalise(b + 1, 1 - u)
                logits(b, u)
                if later(b, 1):
                    residual(b - 1, 1 - u)

            normalise(0, 0)
            dve.wait_ge(w_in, 16 * 5)
            in_turns(dve, step)
            residual(B - 1, (B - 1) % 2)

        @block.scalar
        def _(act):
            def turned(b, u):
                act.wait_ge(tr_ps, b + 1)
                act.activation(XC[:, u, :], banks[u], ACT.Copy).then_inc(xc_ok, 1)

            def step(b, u):
                for ft in range(FT):
                    act.wait_ge(up_ps, b * FT + ft + 1)
                    act.activation(GE[:, u, ft, :], banks[2 + ft % 2], ACT.Gelu,
                                   bias=k.rb1T[:, ft:ft + 1]).then_inc(ge_ok, 1)
                if not (type(b) is int and b == B - 1):
                    turned(b + 1, 1 - u)

            turned(0, 0)
            in_turns(act, step)

        @block.tensor
        def _(pe):
            def turn(b, u):
                pe.wait_ge(xt_ok, b + 1)
                for t in range(TB):
                    mm = pe.transpose(banks[u][:, t * P:t * P + P], OB[:, u, t, :], k.ident[:, :])
                mm.then_inc(tr_ps, 1)

            def down(b, u):
                pe.wait_ge(ge_ok, b * FT + FT)
                if later(b):
                    pe.wait_ge(rm_ok, b - 1)
                for t in range(TB):
                    for ft in range(FT):
                        mm = pe.matmul(banks[4 + u][:, t * P:t * P + P], GE[:, u, ft, t * P:t * P + P],
                                       rw2[:, ft, :], start=(ft == 0), stop=(ft == FT - 1))
                mm.then_inc(dn_ps, 1)

            def step(b, u):
                pe.wait_ge(xc_ok, b + 1)
                if later(b):
                    pe.wait_ge(lg_ok, b - 1)
                for t in range(TB):
                    mm = pe.matmul(banks[6 + u][:, t * NL:t * NL + NL], XC[:, u, t * P:t * P + P], gw[:, :],
                                   start=True, stop=True)
                mm.then_inc(lg_ps, 1)
                for ft in range(FT):
                    if later(b, 1) or ft >= 2:
                        pe.wait_ge(ge_ok, b * FT + ft - 1)
                    pe.matmul(banks[2 + ft % 2], rw1[:, ft * P:ft * P + P], XC[:, u, :],
                              start=True, stop=True).then_inc(up_ps, 1)
                if not (type(b) is int and b == B - 1):
                    turn(b + 1, 1 - u)
                if later(b, 1):
                    down(b - 1, 1 - u)

            pe.wait_ge(w_in, 16 * 5)
            turn(0, 0)
            in_turns(pe, step)
            down(B - 1, (B - 1) % 2)


def route(nc, k, banks):
    with ExitStack() as ctx:
        def sb(name, shape, dt=F32):
            return ctx.enter_context(nc.sbuf_tensor(f"rt_{name}", shape, dt))

        def sem(name):
            return ctx.enter_context(nc.semaphore(f"rt_{name}"))

        LM = sb("LM", [P, NT])
        DF = sb("DF", [P, NT, E])
        EX = sb("EX", [P, NT, E])
        SE = sb("SE", [P, NT])
        GV = sb("GV", [P, NT])
        CM = sb("CM", [P, NT])
        CD = sb("CD", [P, NT, 2])
        CE = sb("CE", [P, NT, 2])
        CS = sb("CS", [P, NT])
        CR = sb("CR", [P, NT])
        GC = sb("GC", [P, NT])
        EQ = sb("EQ", [P, NT, E])
        RV = sb("RV", [P, NT, E])
        RW = sb("RW", [P, NT, E])
        RM_ = sb("RM", [P, NT])
        OH = sb("OH", [P, NT, E])
        OHB = sb("OHB", [P, NT, E], BF16)
        tri = sb("tri", [P, P], BF16)
        ones = sb("ones", [P, P], BF16)
        one_row = sb("one_row", [P, NT])
        TT = sb("TT", [P, E, NT])
        TI = sb("TI", [P, E, NT])
        TX = sb("TX", [P, E, NT])
        NE = sb("NE", [P, E])
        NI = sb("NI", [P, E], I32)
        NS = sb("NS", [P, E], I32)
        NP = sb("NP", [P, E])
        EN = sb("EN", [P, E])
        OF = sb("OF", [P, E])
        BS = sb("BS", [P, E, NT])
        WB = sb("WB", [P, NT, E])
        WO = sb("WO", [P, NT, E])
        DS = sb("DS", [P, NT])
        JV = sb("JV", [P, NX])
        TE0 = sb("TE0", [P, NX])
        TE1 = sb("TE1", [P, NX])
        c_ok = sem("c_ok")
        dv = sem("dv")
        d_ok = sem("d_ok")
        e_ok = sem("e_ok")
        oh_ok = sem("oh_ok")
        cn_ps = sem("cn_ps")
        di_ok = sem("di_ok")
        sc_in = sem("sc_in")
        block = ctx.enter_context(nc.Block())

        @block.gpsimd
        def _(pool):
            pool.memset(tri[:, :], 1.0).then_inc(c_ok, 1)
            pool.memset(ones[:, :], 1.0).then_inc(c_ok, 1)
            pool.memset(one_row[:, :], 1.0).then_inc(c_ok, 1)
            pool.memset(TE0[:, :], 0.0).then_inc(c_ok, 1)
            pool.wait_ge(c_ok, 4)
            pool.affine_select(out=tri[:, :], in_=tri[:, :], compare_op=ALU.is_gt, fill=0.0, base=0,
                               pattern=[[1, P]], channel_multiplier=-1).then_inc(c_ok, 1)
            pool.iota(RV[:, :, :], pattern=[[0, NT], [-1, E]], base=E, channel_multiplier=0,
                      allow_small_or_imprecise_dtypes=True).then_inc(c_ok, 1)
            pool.iota(JV[:, :], pattern=[[P, NX]], base=0, channel_multiplier=0,
                      allow_small_or_imprecise_dtypes=True).then_inc(c_ok, 1)
            pool.wait_ge(di_ok, 1)
            for t in range(NT):
                pool.indirect_dma_start(out=k.XS, out_offset=bass.IndirectOffsetOnAxis(ap=k.DI[:, t:t + 1], axis=0),
                                        in_=k.O[:, t, :], in_offset=None).then_inc(sc_in, 16)
            pool.wait_ge(sc_in, 16 * NT)

        @block.scalar
        def _(act):
            act.wait_ge(d_ok, 2)
            act.activation(EX[:, :, :], DF[:, :, :], ACT.Exp)
            act.activation(CE[:, :, :], CD[:, :, :], ACT.Exp).then_inc(e_ok, 1)

        @block.tensor
        def _(pe):
            pe.wait_ge(c_ok, 7)
            pe.wait_ge(oh_ok, 1)
            oh = OHB[:, :, :].rearrange("p t e -> p (t e)")
            pe.matmul(banks[0][:, 0:NT * E], tri[:, :], oh, start=True, stop=True)
            pe.matmul(banks[1][:, 0:NT * E], ones[:, :], oh, start=True, stop=True).then_inc(cn_ps, 1)

        @block.vector
        def _(dve):
            v = nc.vector
            steps = [0]

            def link(ins):
                ins.then_inc(dv, 1)
                steps[0] += 1
                dve.wait_ge(dv, steps[0])

            def over(x, n):
                return x.unsqueeze(2).broadcast_to([P, NT, n])

            dve.wait_ge(c_ok, 7)
            lg, lc = k.LG[:, :, 0:E], k.LG[:, :, E:E + 2]
            v.tensor_reduce(CM[:, :], lc, AX.X, ALU.max)
            link(v.tensor_reduce(LM[:, :], lg, AX.X, ALU.max))
            v.tensor_tensor(DF[:, :, :], lg, over(LM[:, :], E), ALU.subtract).then_inc(d_ok, 1)
            v.tensor_tensor(CD[:, :, :], lc, over(CM[:, :], 2), ALU.subtract).then_inc(d_ok, 1)
            link(v.tensor_tensor(EQ[:, :, :], lg, over(LM[:, :], E), ALU.is_equal))
            link(v.tensor_tensor(RW[:, :, :], EQ[:, :, :], RV[:, :, :], ALU.mult))
            link(v.tensor_reduce(RM_[:, :], RW[:, :, :], AX.X, ALU.max))
            v.tensor_tensor(OHB[:, :, :], RW[:, :, :], over(RM_[:, :], E), ALU.is_equal).then_inc(oh_ok, 1)
            v.tensor_tensor(OH[:, :, :], RW[:, :, :], over(RM_[:, :], E), ALU.is_equal)
            dve.wait_ge(e_ok, 1)
            v.tensor_reduce(CS[:, :], CE[:, :, :], AX.X, ALU.add)
            link(v.tensor_reduce(SE[:, :], EX[:, :, :], AX.X, ALU.add))
            v.reciprocal(CR[:, :], CS[:, :])
            link(v.reciprocal(GV[:, :], SE[:, :]))
            v.tensor_tensor(k.G1[:, :], CE[:, :, 1], CR[:, :], ALU.mult)
            link(v.tensor_tensor(GC[:, :], CE[:, :, 0], CR[:, :], ALU.mult))
            v.tensor_tensor(k.G0[:, :], GC[:, :], GV[:, :], ALU.mult)
            dve.wait_ge(cn_ps, 1)
            link(v.tensor_copy(TT[:, :, :], banks[1][:, 0:NT * E].rearrange("p (t e) -> p e t", e=E)))
            for e in range(E):
                ins = v.tensor_tensor_scan(TI[:, e, :], one_row[:, :], TT[:, e, :], 0.0, ALU.mult, ALU.add)
            link(ins)
            v.tensor_tensor(TX[:, :, :], TI[:, :, :], TT[:, :, :], ALU.subtract)
            link(v.tensor_scalar(NE[:, :], TI[:, :, NT - 1], float(P - 1), None, ALU.add))
            link(v.tensor_copy(NI[:, :], NE[:, :]))
            link(v.tensor_scalar(NS[:, :], NI[:, :], 7, 7, ALU.logical_shift_right, ALU.logical_shift_left))
            link(v.tensor_copy(NP[:, :], NS[:, :]))
            link(v.tensor_tensor_scan(EN[:, :], one_row[:, 0:E], NP[:, :], 0.0, ALU.mult, ALU.add))
            link(v.tensor_tensor(OF[:, :], EN[:, :], NP[:, :], ALU.subtract))
            link(v.tensor_tensor(BS[:, :, :], TX[:, :, :],
                                 OF[:, :].unsqueeze(2).broadcast_to([P, E, NT]), ALU.add))
            link(v.tensor_tensor(WB[:, :, :], banks[0][:, 0:NT * E].rearrange("p (t e) -> p t e", e=E),
                                 BS[:, :, :].rearrange("p e t -> p t e"), ALU.add))
            link(v.tensor_tensor(WO[:, :, :], WB[:, :, :], OH[:, :, :], ALU.mult))
            link(v.tensor_reduce(DS[:, :], WO[:, :, :], AX.X, ALU.add))
            v.tensor_copy(k.DI[:, :], DS[:, :]).then_inc(di_ok, 1)
            t0, t1 = TE0, TE1
            for e in range(E - 1):
                link(v.scalar_tensor_tensor(out=t1[:, :], in0=JV[:, :], scalar=EN[:, e:e + 1], in1=t0[:, :],
                                            op0=ALU.is_ge, op1=ALU.add))
                t0, t1 = t1, t0
            v.tensor_copy(k.TE[:, :], t0[:, :])


def experts(nc, k, a, banks):
    U = 4
    with ExitStack() as ctx:
        def sb(name, shape, dt=F32):
            return ctx.enter_context(nc.sbuf_tensor(f"ex_{name}", shape, dt))

        def sem(name):
            return ctx.enter_context(nc.semaphore(f"ex_{name}"))

        EB2 = sb("EB2", [P, E, C])
        WS = sb("WS", [P, 2, F])
        XT = sb("XT", [P, U, C])
        XC = sb("XC", [P, 2, P])
        HB = sb("HB", [P, 2, FT, P])
        GE = sb("GE", [P, 2, FT, P])
        YT = sb("YT", [P, U, C])
        b_in = sem("b_in")
        x_in = [sem(f"x_in{i}") for i in range(U)]
        tr_ps = sem("tr_ps")
        xc_ok = sem("xc_ok")
        up_ps = sem("up_ps")
        hb_ok = sem("hb_ok")
        ge_ok = sem("ge_ok")
        dn_ps = sem("dn_ps")
        y_ok = sem("y_ok")
        y_out = [sem(f"y_out{i}") for i in range(U)]
        block = ctx.enter_context(nc.Block())

        def expert_of(eng, j):
            return eng.value_load(k.TE[0:1, bass.ds(j, 1)], min_val=0, max_val=E - 1)

        def in_fours(eng, body):
            for j in range(U):
                body(j, j)
            with eng.Fori(U, NX - 2 * U + 1, U) as j0:
                for i in range(U):
                    body(j0 + i, i)
            for j in range(NX - U, NX):
                body(j, j % U)

        def is_last(j):
            return type(j) is int and j == NX - 1

        @block.sync
        def _(sp):
            sp.dma_start(EB2[:, :, :], a["L0_ffn_b2"].partition_broadcast(P)).then_inc(b_in, 16)

            def load(j, i):
                if later(j, U):
                    sp.wait_ge(tr_ps, j - U + 1)
                sp.dma_start(XT[:, i, :], k.XS[bass.ds(j * P, P), :]).then_inc(x_in[i], 16)

            in_fours(sp, load)

        @block.tensor
        def _(pe):
            def turn(j, i):
                pe.wait_ge(x_in[i], j * (16 // U) + 16 - i * (16 // U))
                pe.transpose(banks[i % 2][:, 0:P], XT[:, i, :], k.ident[:, :]).then_inc(tr_ps, 1)

            def down(j, u):
                e = expert_of(pe, j)
                pe.wait_ge(ge_ok, j + 1)
                if later(j):
                    pe.wait_ge(y_ok, j - 1)
                for ft in range(FT):
                    mm = pe.matmul(banks[4 + u][:, 0:C], GE[:, u, ft, :],
                                   k.W2[:, bass.ds(e, 1), ft, :].rearrange("p o c -> p (o c)"),
                                   start=(ft == 0), stop=(ft == FT - 1))
                mm.then_inc(dn_ps, 1)

            def step(j, i):
                u = i % 2
                pe.wait_ge(xc_ok, j + 1)
                if later(j):
                    pe.wait_ge(hb_ok, j - 1)
                for ft in range(FT):
                    mm = pe.matmul(banks[2 + u][:, ft * P:ft * P + P], WS[:, u, ft * P:ft * P + P], XC[:, u, :],
                                   start=True, stop=True)
                mm.then_inc(up_ps, 1)
                if not is_last(j):
                    turn(j + 1, (i + 1) % U)
                if later(j, 1):
                    down(j - 1, 1 - u)

            turn(0, 0)
            in_fours(pe, step)
            down(NX - 1, (NX - 1) % 2)

        @block.scalar
        def _(act):
            def staged(j, u):
                e = expert_of(act, j)
                if later(j):
                    act.wait_ge(up_ps, j - 1)
                act.activation(WS[:, u, :], k.W1[:, bass.ds(e, 1), :].rearrange("p o f -> p (o f)"), ACT.Copy)
                act.wait_ge(tr_ps, j + 1)
                act.activation(XC[:, u, :], banks[u][:, 0:P], ACT.Copy).then_inc(xc_ok, 1)

            def step(j, i):
                u = i % 2
                if not is_last(j):
                    staged(j + 1, 1 - u)
                act.wait_ge(hb_ok, j + 1)
                act.activation(GE[:, u], HB[:, u], ACT.Gelu).then_inc(ge_ok, 1)

            staged(0, 0)
            in_fours(act, step)

        @block.vector
        def _(dve):
            def output(j, i):
                e = expert_of(dve, j)
                dve.wait_ge(dn_ps, j + 1)
                if later(j, U):
                    dve.wait_ge(y_out[i], j * (16 // U) - i * (16 // U))
                nc.vector.tensor_tensor(YT[:, i, :], banks[4 + i % 2][:, 0:C],
                                        EB2[:, bass.ds(e, 1), :].rearrange("p o c -> p (o c)"),
                                        ALU.add).then_inc(y_ok, 1)

            def step(j, i):
                e = expert_of(dve, j)
                dve.wait_ge(up_ps, j + 1)
                nc.vector.tensor_tensor(HB[:, i % 2], banks[2 + i % 2].rearrange("p (t n) -> p t n", t=FT),
                                        k.eb1T[:, bass.ds(e * FT, FT)].unsqueeze(2).broadcast_to([P, FT, P]),
                                        ALU.add).then_inc(hb_ok, 1)
                if later(j, 1):
                    output(j - 1, (i - 1) % U)

            dve.wait_ge(b_in, 16)
            in_fours(dve, step)
            output(NX - 1, (NX - 1) % U)

        @block.gpsimd
        def _(pool):
            with pool.Fori(0, NX - U + 1, U) as j0:
                for i in range(U):
                    j = j0 + i
                    pool.wait_ge(y_ok, j + 1)
                    pool.dma_start(k.YS[bass.ds(j * P, P), :], YT[:, i, :]).then_inc(y_out[i], 16)
            for i in range(U):
                pool.wait_ge(y_out[i], 16 * NX // U)


def combine(nc, k, out):
    with ExitStack() as ctx:
        def sb(name, shape, dt=F32):
            return ctx.enter_context(nc.sbuf_tensor(f"cb_{name}", shape, dt))

        def sem(name):
            return ctx.enter_context(nc.semaphore(f"cb_{name}"))

        Y = sb("Y", [P, B, TB, C])
        A1 = sb("A1", [P, 2, TB, C])
        A2 = sb("A2", [P, 2, TB, C])
        A3 = sb("A3", [P, 2, TB, C])
        y_in = [sem(f"y_in{b}") for b in range(B)]
        a1_ok, a2_ok, a3_ok, r_ok, r_out = sem("a1_ok"), sem("a2_ok"), sem("a3_ok"), sem("r_ok"), sem("r_out")
        block = ctx.enter_context(nc.Block())

        @block.gpsimd
        def _(pool):
            for t in range(NT):
                pool.indirect_dma_start(out=Y[:, t // TB, t % TB, :], out_offset=None, in_=k.YS,
                                        in_offset=bass.IndirectOffsetOnAxis(ap=k.DI[:, t:t + 1], axis=0)
                                        ).then_inc(y_in[t // TB], 16)

        @block.vector
        def _(dve):
            v = nc.vector
            for b in range(B):
                u = b % 2
                if b >= 2:
                    dve.wait_ge(r_ok, b - 1)
                for t in range(TB):
                    n = b * TB + t
                    ins = v.scalar_tensor_tensor(out=A1[:, u, t, :], in0=k.RM[:, n, :], scalar=k.G1[:, n:n + 1],
                                                 in1=k.H2[:, n, :], op0=ALU.mult, op1=ALU.add)
                ins.then_inc(a1_ok, 1)
                dve.wait_ge(y_in[b], 16 * TB)
                dve.wait_ge(a1_ok, b + 1)
                for t in range(TB):
                    n = b * TB + t
                    ins = v.scalar_tensor_tensor(out=A2[:, u, t, :], in0=Y[:, b, t, :], scalar=k.G0[:, n:n + 1],
                                                 in1=A1[:, u, t, :], op0=ALU.mult, op1=ALU.add)
                ins.then_inc(a2_ok, 1)
                dve.wait_ge(a2_ok, b + 1)
                v.tensor_tensor(A3[:, u], A2[:, u], k.gb[:, b:b + 1, :].broadcast_to([P, TB, C]),
                                ALU.mult).then_inc(a3_ok, 1)
                dve.wait_ge(a3_ok, b + 1)
                x = k.X[:, b * TB:b * TB + TB, :]
                v.tensor_tensor(x, A3[:, u], x, ALU.add).then_inc(r_ok, 1)

        @block.sync
        def _(sp):
            o = out.rearrange("b (t p) c -> b p t c", p=P)
            for b in range(B):
                sp.wait_ge(r_ok, b + 1)
                sp.dma_start(o[b], k.X[:, b * TB:b * TB + TB, :]).then_inc(r_out, 16)
            sp.wait_ge(r_out, 16 * B)


def build(nc, a, out):
    k = Tensors()
    k.XS = nc.dram_tensor("sorted_tokens", [NX * P, C], F32).ap()
    k.YS = nc.dram_tensor("sorted_outputs", [NX * P, C], F32).ap()
    with ExitStack() as ctx:
        def sb(name, shape, dt=F32):
            return ctx.enter_context(nc.sbuf_tensor(name, shape, dt))

        pairs_s = [ctx.enter_context(nc.psum_tensor(f"pair_s{i}", [P, 2, T], F32)) for i in range(2)]
        singles = [ctx.enter_context(nc.psum_tensor(f"bank{i}", [P, T], F32)) for i in range(4)]
        banks = [pairs_s[0][:, 0, :], pairs_s[0][:, 1, :], pairs_s[1][:, 0, :], pairs_s[1][:, 1, :]] + \
                [s[:, :] for s in singles]

        k.X = sb("X", [P, NT, C])
        k.O = sb("O", [P, NT, C])
        k.H2 = sb("H2", [P, NT, C])
        k.gb = sb("gb", [P, B, C])
        k.ident = sb("ident", [P, P])
        k.identb = sb("identb", [P, P], BF16)
        k.cmask = sb("cmask", [P, T])
        k.sac = sb("sac", [P, B])
        k.cac = sb("cac", [P, B])
        k.wq1 = sb("wq1", [P, C])
        k.wk1 = sb("wk1", [P, C])
        k.wv1 = sb("wv1", [P, C])
        k.wo1 = sb("wo1", [P, C])
        k.wq2 = sb("wq2", [P, C])
        k.wk2 = sb("wk2", [P, C])
        k.wv2 = sb("wv2", [P, C])
        k.wo2 = sb("wo2", [P, C])
        k.bv2 = sb("bv2", [P, C])
        k.bo_bc = sb("bo_bc", [P, C])
        k.g2_bc = sb("g2_bc", [P, C])
        k.b2_bc = sb("b2_bc", [P, C])
        k.rb2_bc = sb("rb2_bc", [P, C])
        k.bqk2 = sb("bqk2", [P, 2])
        k.zcol = sb("zcol", [P, 2])
        k.ln1c = sb("ln1c", [P, 2])
        k.eb1T = sb("eb1T", [P, E * FT])
        k.rb1T = sb("rb1T", [P, FT])
        k.rstd = sb("rstd", [P, NT])
        k.nmr = sb("nmr", [P, NT])
        k.mhalf = sb("mhalf", [P, NT])

        with ExitStack() as first:
            def first_sb(name, shape, dt=F32):
                return first.enter_context(nc.sbuf_tensor(name, shape, dt))

            k.BR = first_sb("BR", [P, B, 3, C])
            k.QKS = first_sb("QKS", [P, 6, B * T], BF16)
            k.V = first_sb("V", [P, NT, C])
            k.ST = [first_sb(f"ST{u}", [P, H // 2, 2, T], BF16) for u in range(2)]
            k.VA = first_sb("VA", [P, 2, TB, H, 32])

            load_and_tables(nc, k, a, banks)
            stats(nc, k, k.X, "st1")
            k.stk = [[nc.alloc_semaphore(name=f"rows1_{u}{h}") for h in range(2)] for u in range(2)]
            norm_and_project(nc, k, k.X, k.wq1, k.wk1, k.wv1, k.zcol, k.zcol[:, 0:1].broadcast_to([P, C]),
                             lambda b: k.cac[:, bass.ds(b, 1)], lambda b: k.sac[:, bass.ds(b, 1)],
                             banks, "np1")
            attention(nc, k, True, pairs_s, banks[4:6], banks[6], banks[7], k.H2, "at1")
            out_project(nc, k, k.wo1, banks, "op1", None, k.X, k.BR[:, :, 0, :])
            stats(nc, k, k.X, "st2")
            modulate(nc, k, k.X, k.H2, lambda b: k.BR[:, bass.ds(b, 1), 2, :],
                     lambda b: k.BR[:, bass.ds(b, 1), 1, :], "mo2")
            stats(nc, k, k.H2, "st3")
            k.stk = [[nc.alloc_semaphore(name=f"rows2_{u}{h}") for h in range(2)] for u in range(2)]
            norm_and_project(nc, k, k.H2, k.wq2, k.wk2, k.wv2, k.bqk2, k.bv2,
                             lambda b: k.ln1c[:, 0:1], lambda b: k.ln1c[:, 1:2], banks, "np2")
            attention(nc, k, False, pairs_s, banks[4:6], banks[6], banks[7],
                      k.BR.rearrange("p b j c -> p (b j) c"), "at2")
        out_project(nc, k, k.wo2, banks, "op2", k.bo_bc, k.H2, None)
        stats(nc, k, k.H2, "st4")
        k.RM = sb("RM", [P, NT, C])
        k.LG = sb("LG", [P, NT, E + 2])
        k.G0 = sb("G0", [P, NT])
        k.G1 = sb("G1", [P, NT])
        k.W1 = sb("W1", [P, E, F])
        k.W2 = sb("W2", [P, E, FT, C])
        k.DI = sb("DI", [P, NT], mybir.dt.uint32)
        k.TE = sb("TE", [P, NX], I32)
        gate_and_residual(nc, k, a, banks)
        route(nc, k, banks)
        experts(nc, k, a, banks)
        combine(nc, k, out)


_OUTS = [((B, T, C), "float32")]


def kernel(**inputs):
    import numpy as _np
    import concourse.bacc as _bacc
    from concourse import mybir as _mybir
    from concourse.bass_utils import run_bass_kernel_spmd as _run

    nc = _bacc.Bacc("TRN2", target_bir_lowering=False, num_devices=1)
    arrays, args = {}, {}
    for name in inputs:
        arr = _np.ascontiguousarray(inputs[name])
        arrays[f"in_{name}"] = arr
        args[name] = nc.dram_tensor(f"in_{name}", arr.shape, _mybir.dt.from_np(arr.dtype),
                                    kind="ExternalInput").ap()
    shape, dtype = _OUTS[0]
    out = nc.dram_tensor("out_0", shape, _mybir.dt.from_np(_np.dtype(dtype)), kind="ExternalOutput").ap()
    build(nc, args, out)
    r = _run(nc, [arrays], core_ids=[0])
    return r.results[0]["out_0"]
```

```python
from contextlib import ExitStack

import concourse.bass as bass
from concourse import mybir

F32 = mybir.dt.float32
BF16 = mybir.dt.bfloat16
I32 = mybir.dt.int32
ACT = mybir.ActivationFunctionType
ALU = mybir.AluOpType
AX = mybir.AxisListType

P = 128
B, T, C = 8, 512, 128
H, D = 16, 8
TB = T // P
NT = B * TB
E, F = 8, 512
FT = F // P
EPS = 1e-5
SCALE = float(D) ** -0.5
BIG = 3.0e38
NG = 4
HG = H // NG
UN = NG * TB
Q_PARTS = (0, 0, 0, 1, 1, 2)
K_PARTS = (0, 1, 2, 0, 1, 0)
NR = len(Q_PARTS)
M_ROW = 61
RES_BESIDE_ROUTE = B - 2
NX = NT + E
KT_ROWS = M_ROW + 3
N_HALF = 16 * 2 * NR


class Tensors:
    pass


def head_of(g, i):
    par, p = i % 2, 2 * g + i // 2
    return par * (H // 2) + p


def in_pairs(eng, body, count=B):
    body(0, 0)
    body(1, 1)
    if count > 2:
        with eng.Fori(2, count - 1, 2) as n:
            body(n, 0)
            body(n + 1, 1)


def in_turns(eng, body, count=B):
    body(0, 0)
    body(1, 1)
    with eng.Fori(2, count - 3, 2) as n:
        body(n, 0)
        body(n + 1, 1)
    body(count - 2, 0)
    body(count - 1, 1)


def later(n, first=2):
    return not (type(n) is int and n < first)


def load_score_rows(sp, k, n, u, half):
    for par in range(2):
        src = (2 * half + par) * 32
        for j in range(NR):
            dst = 64 * par + D * j
            q_slot, k_slot = Q_PARTS[j], 3 + K_PARTS[j]
            sp.dma_start(k.ST[u][dst:dst + D, HG * half:HG * half + HG, :, :],
                         k.QKS[src:src + 32, q_slot:k_slot + 1:k_slot - q_slot, bass.ds(n * T, T)]
                         ).then_inc(k.stk[u][half], 16)


def load_and_tables(nc, k, a, banks):
    with ExitStack() as ctx:
        def sb(name, shape, dt=F32):
            return ctx.enter_context(nc.sbuf_tensor(name, shape, dt))

        def sem(name):
            return ctx.enter_context(nc.semaphore(name))

        wqk_nat = sb("wqk_nat", [P, 3, C])
        wout_nat = sb("wout_nat", [P, C])
        wout_perm = sb("wout_perm", [P, C])
        wqkv2 = sb("wqkv2", [P, 3 * C])
        b1_nat = sb("b1_nat", [E * FT, P])
        rb1_nat = sb("rb1_nat", [FT, P])
        bqk_nat = sb("bqk_nat", [2, C])
        bqk_perm = sb("bqk_perm", [2, C])
        ln1_nat = sb("ln1_nat", [2, C])
        c_nat = sb("c_nat", [B, C])
        c_exp = sb("c_exp", [B, C])
        c_one = sb("c_one", [B, C])
        c_rec = sb("c_rec", [B, C])
        c_silu = sb("c_silu", [B, C])
        siluT = sb("siluT", [P, B])
        wmod = sb("wmod", [P, 6 * C])
        silu_bc = k.O[:, 0:B, :]

        x_in = sem("lt_x_in")
        c_in = sem("lt_c_in")
        w_in = sem("lt_w_in")
        consts0 = sem("lt_consts0")
        ident_ok = sem("lt_ident_ok")
        exp_ok = sem("lt_exp_ok")
        chain = sem("lt_chain")
        silu_ok = sem("lt_silu_ok")
        siluT_ps = sem("lt_siluT_ps")
        siluT_ok = sem("lt_siluT_ok")
        mod_ps = sem("lt_mod_ps")
        br_ps = sem("lt_br_ps")
        br_ok = sem("lt_br_ok")
        wt_ps = sem("lt_wt_ps")
        perm_ok = sem("lt_perm_ok")
        wt_free = sem("lt_wt_free")
        filled = sem("lt_filled")

        x_stats = Stats(nc, k, k.X, lambda name: sem(f"lt_{name}"))
        block = ctx.enter_context(nc.Block())

        N_W = 16 * (2 * 4 + 1 + 1 + 1 + 1 + 1 + H // 2 + 1 + 2 + 1 + 4 + 3)

        @block.sync
        def _(sp):
            sp.dma_start(c_nat[:, :], a["L0_c"]).then_inc(c_in, 16)
            sp.dma_start(wmod[:, :], a["L0_wmod"]).then_inc(c_in, 16)
            xv = a["L0_attn_x"].rearrange("b (t p) c -> p (b t) c", p=P)
            for b in range(B):
                sp.dma_start(k.X[:, TB * b:TB * b + TB, :], xv[:, TB * b:TB * b + TB, :]).then_inc(x_in, 16)
            for part in range(2):
                wv = a["L0_attn_w_qkv"][part * C:part * C + C, :].rearrange(
                    "(par half p d) c -> half par d p c", par=2, half=2, d=D)
                for half in range(2):
                    for par in range(2):
                        r = (2 * half + par) * 32
                        sp.dma_start(wqk_nat[r:r + 32, part, :], wv[half, par]).then_inc(w_in, 16)
            sp.dma_start(wqk_nat[:, 2, :], a["L0_attn_w_qkv"][2 * C:3 * C, :]).then_inc(w_in, 16)
            sp.dma_start(wout_nat[:, :], a["L0_attn_w_out"]).then_inc(w_in, 16)
            sp.dma_start(wqkv2[:, :], a["L0_ffn_Wqkv"]).then_inc(w_in, 16)
            sp.dma_start(b1_nat[:, :], a["L0_ffn_b1"].rearrange("e (t f) -> (e t) f", f=P)).then_inc(w_in, 16)
            sp.dma_start(rb1_nat[:, :], a["L0_ffn_rb1"].rearrange("(t f) -> t f", f=P)).then_inc(w_in, 16)
            wo = a["L0_ffn_Wo"].rearrange("(par gp d) c -> gp par d c", par=2, d=D)
            for gp in range(H // 2):
                sp.dma_start(k.wo2[2 * D * gp:2 * D * gp + 2 * D, :], wo[gp]).then_inc(w_in, 16)
            sp.dma_start(bqk_nat[:, :], a["L0_ffn_bqkv"][0:2 * C].rearrange("(s c) -> s c", c=C)).then_inc(w_in, 16)
            for row, name in enumerate(("L0_ffn_ln1_g", "L0_ffn_ln1_b")):
                sp.dma_start(ln1_nat[row:row + 1, :], a[name].rearrange("(o c) -> o c", o=1)).then_inc(w_in, 16)
            sp.dma_start(k.bv2[:, :], a["L0_ffn_bqkv"][2 * C:3 * C].partition_broadcast(P)).then_inc(w_in, 16)
            for dst, name in ((k.bo_bc, "L0_ffn_bo"), (k.g2_bc, "L0_ffn_ln2_g"), (k.b2_bc, "L0_ffn_ln2_b"),
                              (k.rb2_bc, "L0_ffn_rb2")):
                sp.dma_start(dst[:, :], a[name].partition_broadcast(P)).then_inc(w_in, 16)
            sp.dma_start(k.gw[:, 0:E], a["L0_ffn_gate_w"]).then_inc(w_in, 16)
            sp.dma_start(k.gw[:, E:E + 2], a["L0_ffn_coef_w"]).then_inc(w_in, 16)
            sp.wait_ge(consts0, 3)
            sp.dma_start(k.cb[:, E:E + 2], a["L0_ffn_coef_b"].partition_broadcast(P)).then_inc(w_in, 16)
            sp.wait_ge(w_in, N_W)
            sp.wait_ge(x_in, 16 * B)

        @block.gpsimd
        def _(pool):
            pool.memset(k.ident[:, :], 0.0).then_inc(consts0, 1)
            pool.memset(k.cmask[:, :], 0.0).then_inc(consts0, 1)
            pool.memset(k.zcol[:, :], 0.0).then_inc(ident_ok, 1)
            pool.memset(k.cb[:, :], 0.0).then_inc(consts0, 1)
            pool.wait_ge(consts0, 3)
            pool.affine_select(out=k.ident[:, :], in_=k.ident[:, :], compare_op=ALU.not_equal, fill=1.0,
                               base=0, pattern=[[-1, P]], channel_multiplier=1).then_inc(ident_ok, 1)
            dg = k.cmask[:, T - P:T]
            pool.affine_select(out=dg, in_=dg, compare_op=ALU.is_ge, fill=-BIG,
                               base=0, pattern=[[-1, P]], channel_multiplier=1).then_inc(ident_ok, 1)
            pool.wait_ge(ident_ok, 3)
            pool.tensor_copy(k.identb[:, :], k.ident[:, :]).then_inc(ident_ok, 1)
            for u in range(2):
                pool.memset(k.ST[u][:, :, 0, :], 0.0)
                pool.memset(k.ST[u][:, :, 1, :], -1.0)
            pool.memset(k.VA[:, :, :, :, :], 0.0).then_inc(filled, 1)
            pool.wait_ge(filled, 1)
            pool.memset(k.VA[:, :, :, :, D:D + 1], 1.0)

        @block.scalar
        def _(act):
            act.wait_ge(c_in, 32)
            act.activation(c_exp[:, :], c_nat[:, :], ACT.Exp, scale=-1.0).then_inc(exp_ok, 1)
            for b in range(B):
                act.wait_ge(br_ps, b + 1)
                act.activation(k.gb[:, b, :], banks[b][:, 3 * C:4 * C], ACT.Copy)
                act.activation(k.BR[:, b, :, :], banks[b][:, 0:3 * C].rearrange("p (j c) -> p j c", j=3),
                               ACT.Copy).then_inc(br_ok, 1)

        @block.vector
        def _(dve):
            dve.wait_ge(exp_ok, 1)
            nc.vector.tensor_scalar(c_one[:, :], c_exp[:, :], 1.0, None, ALU.add).then_inc(chain, 1)
            dve.wait_ge(chain, 1)
            nc.vector.reciprocal(c_rec[:, :], c_one[:, :]).then_inc(chain, 1)
            dve.wait_ge(chain, 2)
            nc.vector.tensor_tensor(c_silu[:, :], c_nat[:, :], c_rec[:, :], ALU.mult).then_inc(silu_ok, 1)
            dve.wait_ge(siluT_ps, 1)
            nc.vector.tensor_copy(siluT[:, :], banks[0][:, 0:B]).then_inc(chain, 1)
            dve.wait_ge(chain, 3)
            nc.vector.tensor_copy(silu_bc[:, :, :],
                                  siluT[:, :].unsqueeze(2).broadcast_to([P, B, P])).then_inc(siluT_ok, 1)
            dve.wait_ge(mod_ps, 1)
            nc.vector.tensor_copy(k.sac[:, :], banks[1][:, 0:B])
            nc.vector.tensor_scalar(k.cac[:, :], banks[1][:, B:2 * B], 1.0, None, ALU.add).then_inc(wt_free, 1)
            dve.wait_ge(x_in, 16 * B)
            for b in range(B):
                x_stats.rows(dve, b)
            x_stats.finish(dve)
            dve.wait_ge(w_in, N_W)
            for g in range(NG):
                src = wout_nat[:, :].rearrange("o (par g pp d) -> o g pp par d", par=2, g=NG, d=D)[:, g]
                last = nc.vector.tensor_copy(
                    wout_perm[:, g * 32:g * 32 + 32].rearrange("o (pp par d) -> o pp par d", pp=2, par=2), src)
            src = bqk_nat[:, :].rearrange("s (par half p d) -> s half par d p", par=2, half=2, d=D)
            for half in range(2):
                for par in range(2):
                    r = (2 * half + par) * 32
                    last = nc.vector.tensor_copy(bqk_perm[:, r:r + 32].rearrange("s (d p) -> s d p", d=D),
                                                 src[:, half, par])
            last.then_inc(perm_ok, 1)
            for part, dst in ((0, k.wq2), (1, k.wk2)):
                src = wqkv2[:, part * C:part * C + C].rearrange("c (par half p d) -> c half par d p",
                                                               par=2, half=2, d=D)
                for half in range(2):
                    for par in range(2):
                        r = (2 * half + par) * 32
                        nc.vector.tensor_copy(dst[:, r:r + 32].rearrange("c (d p) -> c d p", d=D),
                                              src[:, half, par])
            nc.vector.tensor_copy(k.wv2[:, :], wqkv2[:, 2 * C:3 * C])
            for n, (dst, cols) in enumerate(((k.wq1, C), (k.wk1, C), (k.wv1, C), (k.wo1, C),
                                             (k.eb1T, E * FT), (k.rb1T, FT), (k.bqk2, 2), (k.ln1c, 2))):
                dve.wait_ge(wt_ps, n + 1)
                nc.vector.tensor_copy(dst[:, :], banks[(2 + n) % 8][:, 0:cols])

        @block.tensor
        def _(pe):
            pe.wait_ge(ident_ok, 4)
            pe.wait_ge(silu_ok, 1)
            pe.transpose(banks[0][:, 0:B], c_silu[:, :], k.ident[0:B, 0:B]).then_inc(siluT_ps, 1)
            pe.wait_ge(siluT_ok, 1)
            for j in range(2):
                mm = pe.matmul(banks[1][:, B * j:B * j + B], wmod[:, C * j:C * j + C], silu_bc[:, :, 0],
                               start=True, stop=True)
            mm.then_inc(mod_ps, 1)
            for b in range(B):
                if b == 1:
                    pe.wait_ge(wt_free, 1)
                pe.matmul(banks[b][:, :], silu_bc[:, b, :], wmod[:, 2 * C:6 * C],
                          start=True, stop=True).then_inc(br_ps, 1)
            pe.wait_ge(w_in, N_W)
            pe.wait_ge(br_ok, B)
            for n in range(3):
                pe.transpose(banks[2 + n][:, 0:C], wqk_nat[:, n, :], k.ident[:, :]).then_inc(wt_ps, 1)
            pe.wait_ge(perm_ok, 1)
            pe.transpose(banks[5][:, 0:C], wout_perm[:, :], k.ident[:, :]).then_inc(wt_ps, 1)
            pe.transpose(banks[6][:, 0:E * FT], b1_nat[:, :], k.ident[0:E * FT, 0:E * FT]).then_inc(wt_ps, 1)
            pe.transpose(banks[7][:, 0:FT], rb1_nat[:, :], k.ident[0:FT, 0:FT]).then_inc(wt_ps, 1)
            pe.transpose(banks[0][:, 0:2], bqk_perm[:, :], k.ident[0:2, 0:2]).then_inc(wt_ps, 1)
            pe.transpose(banks[1][:, 0:2], ln1_nat[:, :], k.ident[0:2, 0:2]).then_inc(wt_ps, 1)


class Stats:

    def __init__(self, nc, k, src, sem):
        self.nc, self.k, self.src = nc, k, src
        self.st_ok = sem("st_ok")
        self.mv_ok = sem("mv_ok")
        self.rs_ok = sem("rs_ok")

    def rows(self, dve, b):
        k = self.k
        for t in range(TB):
            tile = b * TB + t
            last = self.nc.vector.bn_stats(k.six[:, bass.ds(tile, 1), :], self.src[:, bass.ds(tile, 1), :])
        last.then_inc(self.st_ok, 1)

    def finish(self, dve):
        k = self.k
        dve.wait_ge(self.st_ok, B)
        for tile in range(NT):
            last = self.nc.vector.bn_aggr(k.mv[:, tile, :], k.six[:, tile, :])
        last.then_inc(self.mv_ok, 1)
        dve.wait_ge(self.mv_ok, 1)
        v = self.nc.vector
        steps = [0]

        def link(ins):
            ins.then_inc(self.rs_ok, 1)
            steps[0] += 1
            dve.wait_ge(self.rs_ok, steps[0])

        link(v.tensor_scalar(k.ve[:, :], k.mv[:, :, 1], EPS, None, ALU.add))
        link(v.tensor_scalar(k.rs[0][:, :].bitcast(I32), k.ve[:, :].bitcast(I32), -0.5, float(0x5F3759DF),
                             ALU.mult, ALU.add))
        for i, out in enumerate((k.rs[1], k.rs[0], k.rstd)):
            r = k.rs[i % 2]
            link(v.tensor_tensor(k.rsq[:, :], r[:, :], r[:, :], ALU.mult))
            link(v.scalar_tensor_tensor(out=k.rvv[:, :], in0=k.rsq[:, :], scalar=-0.5, in1=k.ve[:, :],
                                        op0=ALU.mult, op1=ALU.mult))
            link(v.scalar_tensor_tensor(out=out[:, :], in0=k.rvv[:, :], scalar=1.5, in1=r[:, :],
                                        op0=ALU.add, op1=ALU.mult))
        v.scalar_tensor_tensor(out=k.nmr[:, :], in0=k.mv[:, :, 0], scalar=-1.0, in1=k.rstd[:, :],
                               op0=ALU.mult, op1=ALU.mult)


def gates(k, pool, done):
    sign2, twice, mag, low = (k.O[:, B * i:B * i + B, :] for i in range(4))
    steps = [0]

    def link(ins):
        ins.then_inc(done, 1)
        steps[0] += 1
        pool.wait_ge(done, steps[0])

    for g in (k.BR[:, :, 0, :], k.gb[:, :, :]):
        link(pool.tensor_scalar(sign2, g, 0.0, 2.0, ALU.is_ge, ALU.mult))
        link(pool.tensor_tensor(twice, sign2, g, ALU.mult))
        link(pool.tensor_tensor(mag, twice, g, ALU.subtract))
        link(pool.tensor_scalar(low, mag, 0.25, None, ALU.max))
        link(pool.tensor_tensor(mag, sign2, low, ALU.mult))
        link(pool.tensor_tensor(g, mag, low, ALU.subtract))
    pool.tensor_scalar(k.BR[:, :, 2, :], k.BR[:, :, 2, :], 1.0, None, ALU.add)


def normalised(act, k, out, src, b, done, tiles=range(TB)):
    for t in tiles:
        tile = b * TB + t
        last = act.activation(out[:, t, :], src[:, bass.ds(tile, 1), :].rearrange("p o c -> p (o c)"),
                              ACT.Identity, bias=k.nmr[:, bass.ds(tile, 1)], scale=k.rstd[:, bass.ds(tile, 1)])
    last.then_inc(done, 1)


def norm_and_project(nc, k, src, wq, wk, wv, bqk, bv, scale_of, shift_of, banks, tag, with_gates=False):
    with ExitStack() as ctx:
        def sb(name, shape, dt=F32):
            return ctx.enter_context(nc.sbuf_tensor(f"{tag}_{name}", shape, dt))

        def sem(name):
            return ctx.enter_context(nc.semaphore(f"{tag}_{name}"))

        XN = sb("XN", [P, 2, TB, C])
        HT = sb("HT", [P, 2, T])
        RE = sb("RE", [P, 2, 2, T])
        xn_ok = sem("xn_ok")
        xo_ok = sem("xo_ok")
        tr_ps = sem("tr_ps")
        ht_ok = sem("ht_ok")
        qk_ps = sem("qk_ps")
        v_ps = sem("v_ps")
        s1_ok = sem("s1_ok")
        re_ok = sem("re_ok")
        s2_ok = sem("s2_ok")
        s3_ok = sem("s3_ok")
        v_ok = sem("v_ok")
        block = ctx.enter_context(nc.Block())

        def bank(u, j):
            return banks[4 * u + j]

        def is_last(b):
            return type(b) is int and b == B - 1

        if with_gates:
            gate_ok = sem("gate_ok")

            @block.gpsimd
            def _(pool):
                gates(k, pool, gate_ok)

        @block.sync
        def _(sp):
            for b in range(2):
                sp.wait_ge(s3_ok, 2 * b + 2)
                for half in range(2):
                    load_score_rows(sp, k, b, b, half)

        @block.vector
        def _(dve):
            def normalise(b, u):
                if later(b):
                    dve.wait_ge(tr_ps, b - 1)
                for t in range(TB // 2, TB):
                    tile = b * TB + t
                    last = nc.vector.tensor_scalar(
                        XN[:, u, t, :], src[:, bass.ds(tile, 1), :], k.rstd[:, bass.ds(tile, 1)],
                        k.nmr[:, bass.ds(tile, 1)], ALU.mult, ALU.add)
                last.then_inc(xo_ok, 1)

            def step(b, u):
                if not is_last(b):
                    normalise(b + 1, 1 - u)
                for side in range(2):
                    dve.wait_ge(s1_ok, 2 * b + side + 1)
                    nc.vector.scalar_tensor_tensor(
                        out=RE[:, u, side, :], in0=bank(u, 1 + side)[:, :], scalar=bqk[:, side:side + 1],
                        in1=k.QKS[:, 3 * side, bass.ds(b * T, T)], op0=ALU.add,
                        op1=ALU.subtract).then_inc(re_ok, 1)
                dve.wait_ge(v_ps, b + 1)
                nc.vector.tensor_tensor(
                    k.V[:, bass.ds(b * TB, TB), :], bank(u, 3)[:, :].rearrange("p (t c) -> p t c", t=TB),
                    bv[:, :].unsqueeze(1).broadcast_to([P, TB, C]), ALU.add).then_inc(v_ok, 1)
                for side in range(2):
                    dve.wait_ge(s2_ok, 2 * b + side + 1)
                    nc.vector.tensor_tensor(
                        k.QKS[:, 3 * side + 2, bass.ds(b * T, T)], RE[:, u, side, :],
                        k.QKS[:, 3 * side + 1, bass.ds(b * T, T)], ALU.subtract).then_inc(s3_ok, 1)

            normalise(0, 0)
            in_turns(dve, step)

        @block.tensor
        def _(pe):
            def turn(b, u):
                pe.wait_ge(xn_ok, b + 1)
                pe.wait_ge(xo_ok, b + 1)
                if later(b):
                    pe.wait_ge(ht_ok, b - 1)
                for t in range(TB):
                    mm = pe.transpose(bank(u, 0)[:, t * P:t * P + P], XN[:, u, t, :], k.ident[:, :])
                mm.then_inc(tr_ps, 1)

            def step(b, u):
                pe.wait_ge(ht_ok, b + 1)
                if later(b):
                    pe.wait_ge(re_ok, 2 * (b - 1))
                pe.matmul(bank(u, 1)[:, :], wq[:, :], HT[:, u, :], start=True, stop=True).then_inc(qk_ps, 1)
                pe.matmul(bank(u, 2)[:, :], wk[:, :], HT[:, u, :], start=True, stop=True).then_inc(qk_ps, 1)
                if not is_last(b):
                    turn(b + 1, 1 - u)
                if later(b):
                    pe.wait_ge(v_ok, b - 1)
                for t in range(TB):
                    mm = pe.matmul(bank(u, 3)[:, t * P:t * P + P], HT[:, u, t * P:t * P + P], wv[:, :],
                                   start=True, stop=True)
                mm.then_inc(v_ps, 1)

            turn(0, 0)
            in_turns(pe, step)

        @block.scalar
        def _(act):
            def turned(b, u):
                act.wait_ge(tr_ps, b + 1)
                if later(b):
                    act.wait_ge(v_ps, b - 1)
                act.activation(HT[:, u, :], bank(u, 0)[:, :], ACT.Identity, bias=shift_of(b),
                               scale=scale_of(b)).then_inc(ht_ok, 1)

            def normalise(b, u):
                if later(b):
                    act.wait_ge(tr_ps, b - 1)
                normalised(act, k, XN[:, u], src, b, xn_ok, range(TB // 2))

            def step(b, u):
                if not is_last(b):
                    normalise(b + 1, 1 - u)
                for side in range(2):
                    act.wait_ge(qk_ps, 2 * b + side + 1)
                    act.activation(k.QKS[:, 3 * side, bass.ds(b * T, T)], bank(u, 1 + side)[:, :],
                                   ACT.Identity, bias=bqk[:, side:side + 1]).then_inc(s1_ok, 1)
                if not is_last(b):
                    turned(b + 1, 1 - u)
                for side in range(2):
                    act.wait_ge(re_ok, 2 * b + side + 1)
                    act.activation(k.QKS[:, 3 * side + 1, bass.ds(b * T, T)], RE[:, u, side, :],
                                   ACT.Copy).then_inc(s2_ok, 1)

            normalise(0, 0)
            turned(0, 0)
            in_turns(act, step)


def wait_apart(eng, sem, value, ready=None):
    value = value if type(value) is int else eng.to_reg(value)
    if ready is not None:
        eng.wait_ge(*ready)
    eng.wait_ge(sem, value)


def attention(nc, k, causal, pairs_s, banks_t, bank_o, bank_m, spare, tag):
    sems = []
    with ExitStack() as ctx:
        def sb(name, shape, dt=F32):
            return ctx.enter_context(nc.sbuf_tensor(f"{tag}_{name}", shape, dt))

        def sem(name):
            sems.append(nc.alloc_semaphore(name=f"{tag}_{name}"))
            return sems[-1]

        ST, VA = k.ST, k.VA
        PT = ([spare[:, 16:32, :].rearrange("p (h t) c -> p h (t c)", h=HG)] +
              [sb(f"PT{kt}", [P, HG, T - kt * P]) for kt in range(1, TB)] if causal else
              [sb(f"PT{j}", [P, HG, T]) for j in range(2)])
        NB = len(PT)
        LAG = NB // 2
        MX = sb("MX", [P, 2, TB, 2, HG])
        MR = sb("MR", [P, 2, TB, 2, HG])
        M3 = sb("M3", [P, 2, TB, 2, 3, HG], BF16)
        MT = sb("MT", [6 * HG, 2, T], BF16)
        OT = spare[:, 0:8, :].rearrange("p (g t) c -> p g (t c)", g=2)
        RD = sb("RD", [P, 2, TB, HG])
        JK = (spare[:, 8:16, :].rearrange("p t c -> p (t c)").bitcast(BF16).rearrange(
            "p (a b t) -> p a b t", a=2, b=2) if causal else None)

        vau = sem("vau")
        s_ps = sem("s_ps")
        red = sem("red")
        spl = sem("spl")
        m_ps = sem("m_ps")
        m_ev = sem("m_ev")
        m_row = [sem(f"m_row{h}") for h in range(2)]
        t_ps = sem("t_ps")
        ex = sem("ex")
        msk = sem("msk")
        o_pe = sem("o_pe")
        o_ev = sem("o_ev")
        o_tr = sem("o_tr")
        o_rc = sem("o_rc")
        o_nm = sem("o_nm")
        block = ctx.enter_context(nc.Block())

        STEPS = B + 1

        def width(kt):
            return T - kt * P if causal else T

        def steps(eng, step):
            step(0, 0)
            step(1, 1)
            with eng.Fori(2, B - 1, 2) as n:
                step(n, 0)
                step(n + 1, 1)
            step(B, B % 2)

        def stage(n):
            return not (type(n) is int and n == B), not (type(n) is int and n == 0)

        def sums_of(n, u, g):
            if g == NG - 1:
                return (n, u, 0) if stage(n)[0] else None
            return (n - 1, 1 - u, g + 1) if stage(n)[1] else None

        def before(m, v, h):
            if h:
                return m, v, h - 1
            return (m - 1, 1 - v, NG - 1) if stage(m)[1] else None

        @block.sync
        def _(sp):
            def maxima_rows(n, u, half):
                sp.wait_ge(m_ev, 2 * n + half + 1)
                for par in range(2):
                    sp.dma_start(ST[u][64 * par + M_ROW:64 * par + KT_ROWS, HG * half:HG * half + HG, 0, :],
                                 MT[3 * HG * par:3 * HG * par + 3 * HG, half, :]).then_inc(m_row[half], 16)

            def step(n, u):
                maxima, behind = stage(n)
                if behind:
                    maxima_rows(n - 1, 1 - u, 1)
                more = not (type(n) is int and n >= B - 1)
                if maxima:
                    if more and behind:
                        sp.wait_ge(t_ps, (n - 1) * UN * HG + UN * HG // 2)
                        load_score_rows(sp, k, n + 1, 1 - u, 0)
                    maxima_rows(n, u, 0)
                    if more and behind:
                        sp.wait_ge(t_ps, n * UN * HG)
                        load_score_rows(sp, k, n + 1, 1 - u, 1)

            step(0, 0)
            step(1, 1)
            with sp.Fori(2, B - 3, 2) as n:
                step(n, 0)
                step(n + 1, 1)
            step(B - 2, 0)
            step(B - 1, 1)
            step(B, 0)

        @block.tensor
        def _(pe):
            def scores_max(n, u, g, qt, pair):
                if not (type(n) is int and n == 0 and g == 0 and qt == TB - 1):
                    pe.wait_ge(red, (n * UN + g * TB + TB - 1 - qt) * 2 + pair - 1)
                w = (qt + 1) * P if causal else T
                p = 2 * g + pair
                for par in range(2):
                    r = 64 * par
                    mm = pe.matmul(pairs_s[pair][:, par, 0:w], ST[u][r:r + M_ROW, p, 0, qt * P:qt * P + P],
                                   ST[u][r:r + M_ROW, p, 1, 0:w], start=True, stop=True)
                mm.then_inc(s_ps, 1)

            def scores_exp(n, u, g, kt, pair):
                w = width(kt)
                p = 2 * g + pair
                for par in range(2):
                    at = (g * TB + kt) * HG + 2 * pair + par
                    if not (type(n) is int and n == 0 and at < 2):
                        pe.wait_ge(ex, n * UN * HG + at - 1)
                    r = 64 * par
                    pe.matmul(banks_t[par][:, 0:w], ST[u][r:r + KT_ROWS, p, 1, kt * P:kt * P + P],
                              ST[u][r:r + KT_ROWS, p, 0, T - w:T], start=True, stop=True).then_inc(t_ps, 1)

            def add_sums(n, u, g, kt):
                w = width(kt)
                unit = n * UN + g * TB + kt
                if causal:
                    pe.wait_ge(msk, unit + 1)
                else:
                    pe.wait_ge(ex, (unit + 1) * HG)
                if kt == 0:
                    if g == 0:
                        pe.wait_ge(vau, n + 1)
                    if not (type(n) is int and n == 0 and g == 0):
                        pe.wait_ge(o_ev, n * NG + g)
                for i in range(HG):
                    mm = pe.matmul(bank_o[32 * i:32 * i + 32, T - w:T], VA[:, u, kt, head_of(g, i), :],
                                   PT[kt % NB][:, i, 0:w], start=(kt == 0), stop=(kt == TB - 1))
                mm.then_inc(o_pe, 1)

            def turn_sums(n, g, halves):
                pe.wait_ge(o_ev, n * NG + g + 1)
                if not (type(n) is int and n == 0 and g == 0):
                    pe.wait_ge(o_nm, n * NG + g)
                pe.wait_ge(m_ev, halves)
                for qt in range(TB):
                    mm = pe.transpose(bank_m[:, qt * P:qt * P + P], OT[:, g % 2, qt * P:qt * P + P],
                                      k.ident[:, :])
                mm.then_inc(o_tr, 1)

            def turn_maxima(n, half, groups):
                pe.wait_ge(spl, (2 * n + half) * 4 + 4)
                if not (type(groups) is int and groups == 0):
                    pe.wait_ge(o_nm, groups)
                if not (type(n) is int and n == 0 and half == 0):
                    pe.wait_ge(m_ev, 2 * n + half)
                out = bank_m[0:6 * HG, :].bitcast(BF16)
                for qt in range(TB):
                    mm = pe.transpose(out[:, qt * P:qt * P + P],
                                      M3[:, half, qt].rearrange("p a s h -> p (a s h)"), k.identb[:, :])
                mm.then_inc(m_ps, 1)

            def turn_latest_maxima(n, g):
                maxima, behind = stage(n)
                if g == 0 and behind:
                    turn_maxima(n - 1, 1, (n - 1) * NG)
                if g == 2 and maxima:
                    turn_maxima(n, 0, (n - 1) * NG + 2 if behind else 0)

            def step(n, u):
                maxima, behind = stage(n)
                for g in range(NG):
                    now = sums_of(n, u, g)
                    last_group = before(*now) if now else None
                    for kt in range(TB):
                        if maxima and g % 2 == 0 and kt == 0:
                            pe.wait_ge(k.stk[u][g // 2], n * (N_HALF // 2) + N_HALF - u * (N_HALF // 2))
                        if now:
                            m, v, h = now
                            if h % 2 == 0 and kt == 0:
                                pe.wait_ge(m_row[h // 2], (m + 1) * 32)
                            scores_exp(m, v, h, kt, 0)
                        if maxima and causal:
                            scores_max(n, u, g, TB - 1 - kt, 0)
                        if now and kt >= LAG:
                            add_sums(m, v, h, kt - LAG)
                        elif last_group:
                            add_sums(*last_group, TB + kt - LAG)
                        if kt == 1 and not causal:
                            turn_latest_maxima(n, g)
                        if now:
                            scores_exp(m, v, h, kt, 1)
                        if maxima:
                            if not causal:
                                scores_max(n, u, g, TB - 1 - kt, 0)
                            scores_max(n, u, g, TB - 1 - kt, 1)
                        if kt == 1 and causal:
                            turn_latest_maxima(n, g)
                        if kt == (LAG + 1 if causal else LAG) and last_group:
                            turn_sums(last_group[0], last_group[2], 2 * n + 1 if g >= 2 and maxima else 2 * n)

            steps(pe, step)
            for kt in range(TB - LAG, TB):
                add_sums(B - 1, (B - 1) % 2, NG - 1, kt)
            turn_sums(B - 1, NG - 1, 2 * B)

        @block.scalar
        def _(act):
            def keep_sums(n, g):
                act.wait_ge(o_pe, (n * NG + g + 1) * TB)
                if g >= 2:
                    act.wait_ge(o_tr, n * NG + g - 1)
                elif later(n, 1):
                    act.wait_ge(o_tr, n * NG + g - 1)
                act.activation(OT[:, g % 2, :], bank_o[:, :], ACT.Copy).then_inc(o_ev, 1)

            def keep_maxima(n, half):
                act.wait_ge(m_ps, 2 * n + half + 1)
                if later(n, 1):
                    act.wait_ge(m_row[half], n * 32)
                act.activation(MT[:, half, :], bank_m[0:6 * HG, :].bitcast(BF16)[:, 0:T],
                               ACT.Copy).then_inc(m_ev, 1)

            def keep_latest_maxima(n, g):
                maxima, behind = stage(n)
                if g == 0 and behind:
                    keep_maxima(n - 1, 1)
                if g == 2 and maxima:
                    keep_maxima(n, 0)

            def step(n, u):
                for g in range(NG):
                    now = sums_of(n, u, g)
                    last_group = before(*now) if now else None
                    for kt in range(TB):
                        if now:
                            m, _, h = now
                            w = width(kt)
                            unit = m * UN + h * TB + kt
                            for i in range(HG):
                                if i == HG // 2 and kt == 1 and not causal:
                                    keep_latest_maxima(n, g)
                                act.wait_ge(t_ps, unit * HG + i + 1)
                                if i == 0 and later(unit, NB):
                                    act.wait_ge(o_pe, unit - NB + 1)
                                act.activation(PT[kt % NB][:, i, 0:w], banks_t[i % 2][:, 0:w], ACT.Exp,
                                               scale=SCALE).then_inc(ex, 1)
                        if kt == LAG - 1 and last_group:
                            keep_sums(last_group[0], last_group[2])
                        if kt == 1 and (causal or not now):
                            keep_latest_maxima(n, g)

            steps(act, step)
            keep_sums(B - 1, NG - 1)

        @block.vector
        def _(dve):
            def output(n, g):
                dve.wait_ge(o_tr, n * NG + g + 1)
                t = bank_m[:, :].rearrange("p (q i c) -> p q i c", q=TB, i=HG)
                nc.vector.reciprocal(RD[:, g % 2], t[:, :, :, D]).then_inc(o_rc, 1)
                dve.wait_ge(o_rc, n * NG + g + 1)
                out = k.O[:, bass.ds(n * TB, TB), g * 32:g * 32 + 32].rearrange("p q (i d) -> p q i d", i=HG)
                nc.vector.tensor_tensor(out, t[:, :, :, 0:D],
                                        RD[:, g % 2].unsqueeze(3).broadcast_to([P, TB, HG, D]),
                                        ALU.mult).then_inc(o_nm, 1)

            def step(n, u):
                maxima, behind = stage(n)
                for g in range(NG):
                    now = sums_of(n, u, g)
                    last_group = before(*now) if now else None
                    for kt in range(TB):
                        qt = TB - 1 - kt
                        for pair in range(2):
                            if not maxima:
                                continue
                            if kt == 0 and pair == 0 and g % 2 == 0 and behind:
                                dve.wait_ge(spl, (2 * (n - 1) + g // 2) * 4 + 4)
                            at = (n * UN + g * TB + kt) * 2 + pair
                            wait_apart(dve, s_ps, at + 1, (s_ps, 1))
                            mx = MX[:, g // 2, qt, :, 2 * (g % 2) + pair]
                            if causal:
                                w = (qt + 1) * P
                                for par in range(2):
                                    last = nc.vector.tensor_tensor_reduce(
                                        out=JK[:, pair, par, 0:w], in0=pairs_s[pair][:, par, 0:w], in1=k.cmask[:, T - w:T],
                                        scale=1.0, scalar=-BIG, op0=ALU.add, op1=ALU.max,
                                        accum_out=mx[:, par:par + 1])
                            else:
                                last = nc.vector.tensor_reduce(mx, pairs_s[pair][:, :, :], AX.X, ALU.max)
                            last.then_inc(red, 1)
                        if kt == LAG + 1 and last_group:
                            output(last_group[0], last_group[2])

            steps(dve, step)
            output(B - 1, NG - 1)

        @block.gpsimd
        def _(pool):
            def stage_v(n, u):
                if later(n):
                    wait_apart(pool, o_pe, (n - 1) * UN, (vau, 1))
                pool.tensor_copy(VA[:, u, :, :, 0:D].rearrange("p t h d -> p (t h) d"),
                                 k.V[:, bass.ds(n * TB, TB), :].rearrange("p t (h d) -> p (t h) d", d=D)
                                 ).then_inc(vau, 1)

            def split_maxima(n, half):
                wait_apart(pool, red, (2 * n + half + 1) * UN, (vau, 1))
                if later(n, 1):
                    wait_apart(pool, m_ps, 2 * n + half - 1, (vau, 1))
                at = (2 * n + half) * 4
                m, r = MX[:, half], MR[:, half]
                part = [M3[:, half, :, :, s, :] for s in range(3)]
                pool.tensor_copy(part[0], m).then_inc(spl, 1)
                wait_apart(pool, spl, at + 1, (vau, 1))
                pool.tensor_tensor(r, m, part[0], ALU.subtract).then_inc(spl, 1)
                wait_apart(pool, spl, at + 2, (vau, 1))
                pool.tensor_copy(part[1], r).then_inc(spl, 1)
                wait_apart(pool, spl, at + 3, (vau, 1))
                pool.tensor_tensor(part[2], r, part[1], ALU.subtract).then_inc(spl, 1)

            def step(n, u):
                maxima, _ = stage(n)
                for g in range(NG):
                    now = sums_of(n, u, g)
                    for kt in range(TB):
                        if g == 2 and kt == 0 and maxima:
                            split_maxima(n, 0)
                        if causal and now:
                            unit = now[0] * UN + now[2] * TB + kt
                            wait_apart(pool, ex, (unit + 1) * HG, (vau, 1))
                            dg = PT[kt % NB][:, :, 0:P]
                            pool.affine_select(out=dg, in_=dg, compare_op=ALU.is_ge, fill=0.0, base=0,
                                               pattern=[[0, HG], [1, P]], channel_multiplier=-1).then_inc(msk, 1)
                        if g == 0 and kt == 2 and maxima:
                            stage_v(n, u)
                if maxima:
                    split_maxima(n, 1)

            steps(pool, step)
    nc.clear_and_free_semaphores(sems)
    nc.all_engine_barrier()


def out_project(nc, k, wo, banks, tag, add_rows, into, gate):
    with ExitStack() as ctx:
        def sb(name, shape, dt=F32):
            return ctx.enter_context(nc.sbuf_tensor(f"{tag}_{name}", shape, dt))

        def sem(name):
            return ctx.enter_context(nc.semaphore(f"{tag}_{name}"))

        OB = sb("OB", [P, 2, TB, C])
        OC = sb("OC", [P, 2, T])
        YG = sb("YG", [P, 2, TB, C])
        ob_ok = sem("ob_ok")
        tr_ps = sem("tr_ps")
        oc_ok = sem("oc_ok")
        y_ps = sem("y_ps")
        yg_ok = sem("yg_ok")
        in_ok = sem("in_ok")
        into_stats = Stats(nc, k, into, sem)
        block = ctx.enter_context(nc.Block())

        @block.gpsimd
        def _(pool):
            def add(b, u):
                wait_apart(pool, yg_ok, b + 1, (yg_ok, 1))
                dst = into[:, bass.ds(b * TB, TB), :]
                pool.tensor_tensor(dst, dst, YG[:, u], ALU.add).then_inc(in_ok, 1)

            in_pairs(pool, add)

        @block.tensor
        def _(pe):
            def turn(b, u):
                pe.wait_ge(ob_ok, b + 1)
                if later(b):
                    pe.wait_ge(oc_ok, b - 1)
                for t in range(TB):
                    mm = pe.transpose(banks[2 * u][:, t * P:t * P + P], OB[:, u, t, :], k.ident[:, :])
                mm.then_inc(tr_ps, 1)

            def project(b, u):
                if not (type(b) is int and b == B - 1):
                    turn(b + 1, 1 - u)
                pe.wait_ge(oc_ok, b + 1)
                if later(b):
                    pe.wait_ge(yg_ok, b - 1)
                for t in range(TB):
                    mm = pe.matmul(banks[2 * u + 1][:, t * P:t * P + P], OC[:, u, t * P:t * P + P],
                                   wo[:, :], start=True, stop=True)
                mm.then_inc(y_ps, 1)

            turn(0, 0)
            in_turns(pe, project)

        @block.scalar
        def _(act):
            def fill(b, u):
                if later(b):
                    act.wait_ge(tr_ps, b - 1)
                act.activation(OB[:, u, :, :], k.O[:, bass.ds(b * TB, TB), :], ACT.Copy).then_inc(ob_ok, 1)

            def turned(b, u):
                if not (type(b) is int and b == B - 1):
                    fill(b + 1, 1 - u)
                act.wait_ge(tr_ps, b + 1)
                if later(b):
                    act.wait_ge(y_ps, b - 1)
                act.activation(OC[:, u, :], banks[2 * u][:, :], ACT.Copy).then_inc(oc_ok, 1)

            fill(0, 0)
            in_turns(act, turned)

        @block.vector
        def _(dve):
            def apply(b, u):
                dve.wait_ge(y_ps, b + 1)
                if later(b):
                    dve.wait_ge(in_ok, b - 1)
                y = banks[2 * u + 1][:, :].rearrange("p (t c) -> p t c", t=TB)
                if gate is not None:
                    row, op = gate[:, bass.ds(b, 1), :], ALU.mult
                else:
                    row, op = add_rows[:, :].unsqueeze(1), ALU.add
                nc.vector.tensor_tensor(YG[:, u], y, row.broadcast_to([P, TB, C]), op).then_inc(yg_ok, 1)
                if later(b, 1):
                    dve.wait_ge(in_ok, b)
                    into_stats.rows(dve, b - 1)

            in_pairs(dve, apply)
            dve.wait_ge(in_ok, B)
            into_stats.rows(dve, B - 1)
            into_stats.finish(dve)


def modulate(nc, k, src, dst, mult, add, tag):
    with ExitStack() as ctx:
        def sem(name):
            return ctx.enter_context(nc.semaphore(f"{tag}_{name}"))

        XN = ctx.enter_context(nc.sbuf_tensor(f"{tag}_XN", [P, 2, TB, C], F32))
        XM = ctx.enter_context(nc.sbuf_tensor(f"{tag}_XM", [P, 2, TB, C], F32))
        xn_ok, xm_ok, out_ok = sem("xn_ok"), sem("xm_ok"), sem("out_ok")
        dst_stats = Stats(nc, k, dst, sem)
        block = ctx.enter_context(nc.Block())

        @block.scalar
        def _(act):
            def normalise(b, u):
                if later(b):
                    act.wait_ge(xm_ok, b - 1)
                normalised(act, k, XN[:, u], src, b, xn_ok)

            in_pairs(act, normalise)

        @block.vector
        def _(dve):
            def scale(b, u):
                dve.wait_ge(xn_ok, b + 1)
                if later(b):
                    dve.wait_ge(out_ok, b - 1)
                nc.vector.tensor_tensor(XM[:, u], XN[:, u], mult(b).broadcast_to([P, TB, C]),
                                        ALU.mult).then_inc(xm_ok, 1)
                if later(b, 1):
                    dve.wait_ge(out_ok, b)
                    dst_stats.rows(dve, b - 1)

            in_pairs(dve, scale)
            dve.wait_ge(out_ok, B)
            dst_stats.rows(dve, B - 1)
            dst_stats.finish(dve)

        @block.gpsimd
        def _(pool):
            with pool.Fori(0, B - 1, 2) as b0:
                for u in range(2):
                    b = b0 + u
                    wait_apart(pool, xm_ok, b + 1)
                    pool.tensor_tensor(dst[:, bass.ds(b * TB, TB), :], XM[:, u],
                                       add(b).broadcast_to([P, TB, C]), ALU.add).then_inc(out_ok, 1)


def gate(nc, k, a, banks):
    NL = E + 2
    with ExitStack() as ctx:
        def sb(name, shape, dt=F32):
            return ctx.enter_context(nc.sbuf_tensor(f"gr_{name}", shape, dt))

        def sem(name):
            return ctx.enter_context(nc.semaphore(f"gr_{name}"))

        XN = sb("XN", [P, 2, TB, C])
        XM = sb("XM", [P, 2, TB, C])
        OB = sb("OB", [P, 2, TB, C])
        XB = sb("XB", [P, 2, T])
        fill = sb("fill", [P, NX, C + 1])
        z_in = sem("z_in")
        z_ok = sem("z_ok")
        xn_ok = sem("xn_ok")
        xm_ok = sem("xm_ok")
        xt_ok = sem("xt_ok")
        kept = sem("kept")
        tr_ps = sem("tr_ps")
        xc_ok = sem("xc_ok")
        xk_ok = sem("xk_ok")
        lg_ps = sem("lg_ps")
        lg_ok = sem("lg_ok")
        block = ctx.enter_context(nc.Block())

        def is_last(b):
            return type(b) is int and b == B - 1

        @block.sync
        def _(sp):
            sp.dma_start(k.rw1[:, :], a["L0_ffn_rW1"]).then_inc(k.rw_in, 16)
            sp.dma_start(k.rw2[:, :, :], a["L0_ffn_rW2"].rearrange("(t f) d -> f t d", f=P)).then_inc(k.rw_in, 16)
            sp.wait_ge(z_ok, 2)
            sp.dma_start(k.XS.rearrange("(t p) c -> p t c", p=P), fill[:, :, :]).then_inc(z_in, 16)
            sp.dma_start(k.EB2[:, :, :], a["L0_ffn_b2"].partition_broadcast(P)).then_inc(k.ew_in, 16)
            for e in range(E):
                sp.dma_start(k.W1[:, e, :], a["L0_ffn_W1"][e]).then_inc(k.ew_in, 16)
                sp.dma_start(k.W2[:, e, :, :], a["L0_ffn_W2"][e].rearrange("(t f) d -> f t d", f=P)
                             ).then_inc(k.ew_in, 16)
            sp.wait_ge(z_in, 16)

        @block.gpsimd
        def _(pool):
            pool.memset(fill[:, :, 0:C], 0.0).then_inc(z_ok, 1)
            pool.iota(fill[:, :, C:C + 1].bitcast(I32), pattern=[[P, NX], [1, 1]], base=NT * P,
                      channel_multiplier=1).then_inc(z_ok, 1)
            pool.iota(k.XR[:, :, C:C + 1].bitcast(I32), pattern=[[P, NT], [1, 1]], base=0, channel_multiplier=1)
            with pool.Fori(0, B - 1, 2) as b0:
                for u in range(2):
                    b = b0 + u
                    wait_apart(pool, xt_ok, b + 1, (z_ok, 2))
                    pool.tensor_copy(k.XR[:, bass.ds(b * TB, TB), 0:C], OB[:, u]).then_inc(kept, 1)

        @block.vector
        def _(dve):
            def scale_shift(b, u):
                dve.wait_ge(xn_ok, b + 1)
                nc.vector.tensor_tensor(XM[:, u], XN[:, u], k.g2_bc[:, :].unsqueeze(1).broadcast_to([P, TB, C]),
                                        ALU.mult).then_inc(xm_ok, 1)
                dve.wait_ge(xm_ok, b + 1)
                if later(b):
                    dve.wait_ge(tr_ps, b - 1)
                    dve.wait_ge(kept, b - 1)
                nc.vector.tensor_tensor(OB[:, u], XM[:, u],
                                        k.b2_bc[:, :].unsqueeze(1).broadcast_to([P, TB, C]),
                                        ALU.add).then_inc(xt_ok, 1)

            def logits(b, u):
                dve.wait_ge(lg_ps, b + 1)
                nc.vector.tensor_tensor(
                    k.LG[:, bass.ds(b * TB, TB), :], banks[2 + u][:, 0:TB * NL].rearrange("p (t e) -> p t e", t=TB),
                    k.cb[:, :].unsqueeze(1).broadcast_to([P, TB, NL]), ALU.add).then_inc(lg_ok, 1)

            def step(b, u):
                if not is_last(b):
                    scale_shift(b + 1, 1 - u)
                dve.wait_ge(xc_ok, b + 1)
                nc.vector.tensor_copy(k.XC[:, bass.ds(b * T, T)], XB[:, u, :]).then_inc(xk_ok, 1)
                if later(b, 1):
                    logits(b - 1, 1 - u)

            scale_shift(0, 0)
            in_turns(dve, step)
            logits(B - 1, (B - 1) % 2)

        @block.scalar
        def _(act):
            def normalise(b, u):
                if later(b):
                    act.wait_ge(xm_ok, b - 1)
                normalised(act, k, XN[:, u], k.H2, b, xn_ok)

            def turned(b, u):
                act.wait_ge(tr_ps, b + 1)
                if later(b):
                    act.wait_ge(lg_ps, b - 1)
                    act.wait_ge(xk_ok, b - 1)
                act.activation(XB[:, u, :], banks[u], ACT.Copy).then_inc(xc_ok, 1)
                if not (type(b) is int and b >= B - 2):
                    normalise(b + 2, u)

            normalise(0, 0)
            normalise(1, 1)
            in_turns(act, turned)

        @block.tensor
        def _(pe):
            def turn(b, u):
                pe.wait_ge(xt_ok, b + 1)
                if later(b):
                    pe.wait_ge(xc_ok, b - 1)
                for t in range(TB):
                    mm = pe.transpose(banks[u][:, t * P:t * P + P], OB[:, u, t, :], k.ident[:, :])
                mm.then_inc(tr_ps, 1)

            def step(b, u):
                if not is_last(b):
                    turn(b + 1, 1 - u)
                pe.wait_ge(xc_ok, b + 1)
                if later(b):
                    pe.wait_ge(lg_ok, b - 1)
                for t in range(TB):
                    mm = pe.matmul(banks[2 + u][:, t * NL:t * NL + NL], XB[:, u, t * P:t * P + P], k.gw[:, :],
                                   start=True, stop=True)
                mm.then_inc(lg_ps, 1)

            turn(0, 0)
            in_turns(pe, step)


class Residual:

    def __init__(self, nc, k, banks, sem, GE, first, count):
        self.nc, self.k, self.banks, self.GE = nc, k, banks, GE
        self.first, self.count = first, count
        self.up_ps = sem("up_ps")
        self.ge_ok = sem("ge_ok")
        self.dn_ps = sem("dn_ps")
        self.rm_ok = sem("rm_ok")
        self.g1_ok = sem("g1_ok")
        self.gb_ok = sem("gb_ok")
        self.x_ok = sem("x_ok")

    def up(self, pe, m, u):
        k = self.k
        for ft in range(FT):
            if later(m, 1) or ft >= 2:
                pe.wait_ge(self.ge_ok, m * FT + ft - 1)
            pe.matmul(self.banks[2 + ft % 2], k.rw1[:, ft * P:ft * P + P],
                      k.XC[:, bass.ds((m + self.first) * T, T)], start=True, stop=True).then_inc(self.up_ps, 1)

    def down(self, pe, m, u):
        pe.wait_ge(self.ge_ok, m * FT + FT)
        if later(m):
            pe.wait_ge(self.rm_ok, m - 1)
        for t in range(TB):
            for ft in range(FT):
                mm = pe.matmul(self.banks[4 + u][:, t * P:t * P + P], self.GE[:, u, ft, t * P:t * P + P],
                               self.k.rw2[:, ft, :], start=(ft == 0), stop=(ft == FT - 1))
        mm.then_inc(self.dn_ps, 1)

    def gelus(self, act):
        def hidden(m, u):
            for ft in range(FT):
                act.wait_ge(self.up_ps, m * FT + ft + 1)
                act.activation(self.GE[:, u, ft, :], self.banks[2 + ft % 2], ACT.Gelu,
                               bias=self.k.rb1T[:, ft:ft + 1]).then_inc(self.ge_ok, 1)

        in_pairs(act, hidden, self.count)

    def add(self, dve, m, u):
        k = self.k
        dve.wait_ge(self.dn_ps, m + 1)
        self.nc.vector.tensor_tensor(
            k.RM[:, bass.ds((m + self.first) * TB, TB), :],
            self.banks[4 + u].rearrange("p (t c) -> p t c", t=TB),
            k.rb2_bc[:, :].unsqueeze(1).broadcast_to([P, TB, C]), ALU.add).then_inc(self.rm_ok, 1)


    def blend(self, dve, m, u):
        k, v = self.k, self.nc.vector
        b = m + self.first
        dve.wait_ge(self.rm_ok, m + 1)
        for t in range(TB):
            tile = b * TB + t
            rm = k.RM[:, bass.ds(tile, 1), :]
            last = v.scalar_tensor_tensor(out=rm, in0=rm, scalar=k.G1[:, bass.ds(tile, 1)],
                                          in1=k.H2[:, bass.ds(tile, 1), :], op0=ALU.mult, op1=ALU.add)
        last.then_inc(self.g1_ok, 1)
        dve.wait_ge(self.g1_ok, m + 1)
        rm, x = k.RM[:, bass.ds(b * TB, TB), :], k.X[:, bass.ds(b * TB, TB), :]
        v.tensor_tensor(rm, rm, k.gb[:, bass.ds(b, 1), :].broadcast_to([P, TB, C]), ALU.mult).then_inc(self.gb_ok, 1)
        dve.wait_ge(self.gb_ok, m + 1)
        v.tensor_tensor(x, x, rm, ALU.add).then_inc(self.x_ok, 1)


def route(nc, k, banks):
    with ExitStack() as ctx:
        def sb(name, shape, dt=F32):
            return ctx.enter_context(nc.sbuf_tensor(f"rt_{name}", shape, dt))

        def sem(name):
            return ctx.enter_context(nc.semaphore(f"rt_{name}"))

        LM = sb("LM", [P, NT])
        DF = sb("DF", [P, NT, E])
        EX = sb("EX", [P, NT, E])
        SE = sb("SE", [P, NT])
        GV = sb("GV", [P, NT])
        CM = sb("CM", [P, NT])
        CD = sb("CD", [P, NT, 2])
        CE = sb("CE", [P, NT, 2])
        CS = sb("CS", [P, NT])
        CR = sb("CR", [P, NT])
        GC = sb("GC", [P, NT])
        EQ = sb("EQ", [P, NT, E])
        RV = sb("RV", [P, NT, E])
        RW = sb("RW", [P, NT, E])
        RM_ = sb("RM", [P, NT])
        OH = sb("OH", [P, NT, E])
        OHB = sb("OHB", [P, NT, E], BF16)
        tri = sb("tri", [P, P], BF16)
        ones = sb("ones", [P, P], BF16)
        one_row = sb("one_row", [P, NT])
        TT = sb("TT", [P, E, NT])
        TI = sb("TI", [P, E, NT])
        TX = sb("TX", [P, E, NT])
        NE = sb("NE", [P, E])
        NI = sb("NI", [P, E], I32)
        NS = sb("NS", [P, E], I32)
        NP = sb("NP", [P, E])
        EN = sb("EN", [P, E])
        OF = sb("OF", [P, E])
        BS = sb("BS", [P, E, NT])
        WB = sb("WB", [P, NT, E])
        WO = sb("WO", [P, NT, E])
        DS = sb("DS", [P, NT])
        JV = sb("JV", [P, NX])
        TE0 = sb("TE0", [P, NX])
        TE1 = sb("TE1", [P, NX])
        c_ok = sem("c_ok")
        dv = sem("dv")
        d_ok = sem("d_ok")
        e_ok = sem("e_ok")
        oh_ok = sem("oh_ok")
        cn_ps = sem("cn_ps")
        di_ok = sem("di_ok")
        sc_in = sem("sc_in")
        res = Residual(nc, k, banks, sem, sb("GE", [P, 2, FT, T]), 0, RES_BESIDE_ROUTE)
        block = ctx.enter_context(nc.Block())

        @block.gpsimd
        def _(pool):
            pool.memset(tri[:, :], 1.0).then_inc(c_ok, 1)
            pool.memset(ones[:, :], 1.0).then_inc(c_ok, 1)
            pool.memset(one_row[:, :], 1.0).then_inc(c_ok, 1)
            pool.memset(TE0[:, :], 0.0).then_inc(c_ok, 1)
            pool.wait_ge(c_ok, 4)
            pool.affine_select(out=tri[:, :], in_=tri[:, :], compare_op=ALU.is_gt, fill=0.0, base=0,
                               pattern=[[1, P]], channel_multiplier=-1).then_inc(c_ok, 1)
            pool.iota(RV[:, :, :], pattern=[[0, NT], [-1, E]], base=E, channel_multiplier=0,
                      allow_small_or_imprecise_dtypes=True).then_inc(c_ok, 1)
            pool.iota(JV[:, :], pattern=[[P, NX]], base=0, channel_multiplier=0,
                      allow_small_or_imprecise_dtypes=True).then_inc(c_ok, 1)
            pool.wait_ge(di_ok, 1)
            for t in range(NT):
                pool.indirect_dma_start(out=k.XS, out_offset=bass.IndirectOffsetOnAxis(ap=k.DI[:, t:t + 1], axis=0),
                                        in_=k.XR[:, t, :], in_offset=None).then_inc(sc_in, 16)
            pool.wait_ge(sc_in, 16 * NT)

        @block.scalar
        def _(act):
            act.wait_ge(d_ok, 2)
            act.activation(EX[:, :, :], DF[:, :, :], ACT.Exp)
            act.activation(CE[:, :, :], CD[:, :, :], ACT.Exp).then_inc(e_ok, 1)
            res.gelus(act)

        @block.tensor
        def _(pe):
            pe.wait_ge(k.rw_in, 32)
            res.up(pe, 0, 0)
            pe.wait_ge(c_ok, 7)
            pe.wait_ge(oh_ok, 1)
            oh = OHB[:, :, :].rearrange("p t e -> p (t e)")
            pe.matmul(banks[0][:, 0:NT * E], tri[:, :], oh, start=True, stop=True)
            pe.matmul(banks[1][:, 0:NT * E], ones[:, :], oh, start=True, stop=True).then_inc(cn_ps, 1)
            res.up(pe, 1, 1)
            res.down(pe, 0, 0)
            with pe.Fori(2, res.count - 1, 2) as m:
                for u in range(2):
                    res.up(pe, m + u, u)
                    res.down(pe, m + u - 1, 1 - u)
            res.down(pe, res.count - 1, 1)

        @block.vector
        def _(dve):
            v = nc.vector
            steps = [0]

            def link(ins):
                ins.then_inc(dv, 1)
                steps[0] += 1
                dve.wait_ge(dv, steps[0])

            def over(x, n):
                return x.unsqueeze(2).broadcast_to([P, NT, n])

            dve.wait_ge(c_ok, 7)
            lg, lc = k.LG[:, :, 0:E], k.LG[:, :, E:E + 2]
            v.tensor_reduce(CM[:, :], lc, AX.X, ALU.max)
            link(v.tensor_reduce(LM[:, :], lg, AX.X, ALU.max))
            v.tensor_tensor(DF[:, :, :], lg, over(LM[:, :], E), ALU.subtract).then_inc(d_ok, 1)
            v.tensor_tensor(CD[:, :, :], lc, over(CM[:, :], 2), ALU.subtract).then_inc(d_ok, 1)
            link(v.tensor_tensor(EQ[:, :, :], lg, over(LM[:, :], E), ALU.is_equal))
            link(v.tensor_tensor(RW[:, :, :], EQ[:, :, :], RV[:, :, :], ALU.mult))
            link(v.tensor_reduce(RM_[:, :], RW[:, :, :], AX.X, ALU.max))
            v.tensor_tensor(OHB[:, :, :], RW[:, :, :], over(RM_[:, :], E), ALU.is_equal).then_inc(oh_ok, 1)
            v.tensor_tensor(OH[:, :, :], RW[:, :, :], over(RM_[:, :], E), ALU.is_equal)
            dve.wait_ge(e_ok, 1)
            v.tensor_reduce(CS[:, :], CE[:, :, :], AX.X, ALU.add)
            link(v.tensor_reduce(SE[:, :], EX[:, :, :], AX.X, ALU.add))
            v.reciprocal(CR[:, :], CS[:, :])
            link(v.reciprocal(GV[:, :], SE[:, :]))
            v.tensor_tensor(k.G1[:, :], CE[:, :, 1], CR[:, :], ALU.mult)
            link(v.tensor_tensor(GC[:, :], CE[:, :, 0], CR[:, :], ALU.mult))
            v.tensor_tensor(k.G0[:, :], GC[:, :], GV[:, :], ALU.mult)
            dve.wait_ge(cn_ps, 1)
            link(v.tensor_copy(TT[:, :, :], banks[1][:, 0:NT * E].rearrange("p (t e) -> p e t", e=E)))
            for e in range(E):
                ins = v.tensor_tensor_scan(TI[:, e, :], one_row[:, :], TT[:, e, :], 0.0, ALU.mult, ALU.add)
            link(ins)
            v.tensor_tensor(TX[:, :, :], TI[:, :, :], TT[:, :, :], ALU.subtract)
            link(v.tensor_scalar(NE[:, :], TI[:, :, NT - 1], float(P - 1), None, ALU.add))
            link(v.tensor_copy(NI[:, :], NE[:, :]))
            link(v.tensor_scalar(NS[:, :], NI[:, :], 7, 7, ALU.logical_shift_right, ALU.logical_shift_left))
            link(v.tensor_copy(NP[:, :], NS[:, :]))
            link(v.tensor_tensor_scan(EN[:, :], one_row[:, 0:E], NP[:, :], 0.0, ALU.mult, ALU.add))
            link(v.tensor_tensor(OF[:, :], EN[:, :], NP[:, :], ALU.subtract))
            link(v.tensor_tensor(BS[:, :, :], TX[:, :, :],
                                 OF[:, :].unsqueeze(2).broadcast_to([P, E, NT]), ALU.add))
            link(v.tensor_tensor(WB[:, :, :], banks[0][:, 0:NT * E].rearrange("p (t e) -> p t e", e=E),
                                 BS[:, :, :].rearrange("p e t -> p t e"), ALU.add))
            link(v.tensor_tensor(WO[:, :, :], WB[:, :, :], OH[:, :, :], ALU.mult))
            link(v.tensor_reduce(DS[:, :], WO[:, :, :], AX.X, ALU.add))
            v.tensor_copy(k.DI[:, :], DS[:, :]).then_inc(di_ok, 1)
            t0, t1 = TE0, TE1
            for e in range(E - 1):
                link(v.scalar_tensor_tensor(out=t1[:, :], in0=JV[:, :], scalar=EN[:, e:e + 1], in1=t0[:, :],
                                            op0=ALU.is_ge, op1=ALU.add))
                t0, t1 = t1, t0
            v.tensor_copy(k.TE[:, :], t0[:, :])

            def finish(m, u):
                res.add(dve, m, u)
                res.blend(dve, m, u)

            in_pairs(dve, finish, res.count)


def experts(nc, k, a, banks):
    U = 4
    with ExitStack() as ctx:
        def sb(name, shape, dt=F32):
            return ctx.enter_context(nc.sbuf_tensor(f"ex_{name}", shape, dt))

        def sem(name):
            return ctx.enter_context(nc.semaphore(f"ex_{name}"))

        WS = sb("WS", [P, 2, F])
        XT = sb("XT", [P, U, C + 1])
        IX = sb("IX", [P, U], mybir.dt.uint32)
        XC = sb("XC", [P, 2, P])
        HB = sb("HB", [P, 2, FT, P])
        GE = sb("GE", [P, 2, FT, P])
        YT = sb("YT", [P, U, C])
        x_in = [sem(f"x_in{i}") for i in range(U)]
        tr_ps = sem("tr_ps")
        xc_ok = sem("xc_ok")
        ix_ok = sem("ix_ok")
        up_ps = sem("up_ps")
        hb_ok = sem("hb_ok")
        ge_ok = sem("ge_ok")
        dn_ps = sem("dn_ps")
        y_ok = sem("y_ok")
        y_out = [sem(f"y_out{i}") for i in range(U)]
        block = ctx.enter_context(nc.Block())

        def expert_of(eng, j):
            return eng.value_load(k.TE[0:1, bass.ds(j, 1)], min_val=0, max_val=E - 1)

        def in_fours(eng, body):
            for j in range(U):
                body(j, j)
            with eng.Fori(U, NX - 2 * U + 1, U) as j0:
                for i in range(U):
                    body(j0 + i, i)
            for j in range(NX - U, NX):
                body(j, j % U)

        def is_last(j):
            return type(j) is int and j == NX - 1

        @block.sync
        def _(sp):
            def load(j, i):
                if later(j, U):
                    sp.wait_ge(tr_ps, j - U + 1)
                    sp.wait_ge(ix_ok, j - U + 1)
                sp.dma_start(XT[:, i, :], k.XS[bass.ds(j * P, P), :]).then_inc(x_in[i], 16)

            in_fours(sp, load)

        @block.tensor
        def _(pe):
            def turn(j, i):
                pe.wait_ge(x_in[i], j * (16 // U) + 16 - i * (16 // U))
                pe.transpose(banks[i % 2][:, 0:P], XT[:, i, 0:C], k.ident[:, :]).then_inc(tr_ps, 1)

            def down(j, u):
                e = expert_of(pe, j)
                pe.wait_ge(ge_ok, j + 1)
                if later(j):
                    pe.wait_ge(y_ok, j - 1)
                for ft in range(FT):
                    mm = pe.matmul(banks[4 + u][:, 0:C], GE[:, u, ft, :],
                                   k.W2[:, bass.ds(e, 1), ft, :].rearrange("p o c -> p (o c)"),
                                   start=(ft == 0), stop=(ft == FT - 1))
                mm.then_inc(dn_ps, 1)

            def step(j, i):
                u = i % 2
                pe.wait_ge(xc_ok, j + 1)
                if later(j):
                    pe.wait_ge(hb_ok, j - 1)
                for ft in range(FT):
                    mm = pe.matmul(banks[2 + u][:, ft * P:ft * P + P], WS[:, u, ft * P:ft * P + P], XC[:, u, :],
                                   start=True, stop=True)
                mm.then_inc(up_ps, 1)
                if not is_last(j):
                    turn(j + 1, (i + 1) % U)
                if later(j, 1):
                    down(j - 1, 1 - u)

            turn(0, 0)
            pe.wait_ge(k.ew_in, 16 * (2 * E + 1))
            in_fours(pe, step)
            down(NX - 1, (NX - 1) % 2)

        @block.scalar
        def _(act):
            def staged(j, u):
                e = expert_of(act, j)
                if later(j):
                    act.wait_ge(up_ps, j - 1)
                act.activation(WS[:, u, :], k.W1[:, bass.ds(e, 1), :].rearrange("p o f -> p (o f)"), ACT.Copy)
                act.wait_ge(tr_ps, j + 1)
                act.activation(XC[:, u, :], banks[u][:, 0:P], ACT.Copy).then_inc(xc_ok, 1)

            def step(j, i):
                u = i % 2
                if not is_last(j):
                    staged(j + 1, 1 - u)
                act.wait_ge(hb_ok, j + 1)
                act.activation(GE[:, u], HB[:, u], ACT.Gelu).then_inc(ge_ok, 1)

            act.wait_ge(k.ew_in, 16 * (2 * E + 1))
            staged(0, 0)
            in_fours(act, step)

        @block.vector
        def _(dve):
            def output(j, i):
                e = expert_of(dve, j)
                dve.wait_ge(dn_ps, j + 1)
                nc.vector.tensor_tensor(YT[:, i, :], banks[4 + i % 2][:, 0:C],
                                        k.EB2[:, bass.ds(e, 1), :].rearrange("p o c -> p (o c)"),
                                        ALU.add).then_inc(y_ok, 1)

            def step(j, i):
                e = expert_of(dve, j)
                dve.wait_ge(x_in[i], j * (16 // U) + 16 - i * (16 // U))
                if later(j, U):
                    dve.wait_ge(y_out[i], j * (16 // U) - i * (16 // U))
                nc.vector.tensor_copy(IX[:, i:i + 1], XT[:, i, C:C + 1].bitcast(mybir.dt.uint32)).then_inc(ix_ok, 1)
                dve.wait_ge(up_ps, j + 1)
                nc.vector.tensor_tensor(HB[:, i % 2], banks[2 + i % 2].rearrange("p (t n) -> p t n", t=FT),
                                        k.eb1T[:, bass.ds(e * FT, FT)].unsqueeze(2).broadcast_to([P, FT, P]),
                                        ALU.add).then_inc(hb_ok, 1)
                if later(j, 1):
                    output(j - 1, (i - 1) % U)

            dve.wait_ge(k.ew_in, 16 * (2 * E + 1))
            in_fours(dve, step)
            output(NX - 1, (NX - 1) % U)

        @block.gpsimd
        def _(pool):
            with pool.Fori(0, NX - U + 1, U) as j0:
                for i in range(U):
                    j = j0 + i
                    wait_apart(pool, y_ok, j + 1, (y_ok, 1))
                    pool.indirect_dma_start(out=k.YS, out_offset=bass.IndirectOffsetOnAxis(ap=IX[:, i:i + 1], axis=0),
                                            in_=YT[:, i, :], in_offset=None).then_inc(y_out[i], 16)
            for i in range(U):
                pool.wait_ge(y_out[i], 16 * NX // U)


def combine(nc, k, banks, out):
    with ExitStack() as ctx:
        def sb(name, shape, dt=F32):
            return ctx.enter_context(nc.sbuf_tensor(f"cb_{name}", shape, dt))

        def sem(name):
            return ctx.enter_context(nc.semaphore(f"cb_{name}"))

        Y = sb("Y", [P, B, TB, C])
        GY = sb("GY", [P, 2, TB, C])
        y_in = [sem(f"y_in{b}") for b in range(B)]
        gy_ok, r_ok, r_out = sem("gy_ok"), sem("r_ok"), sem("r_out")
        res = Residual(nc, k, banks, sem, sb("GE", [P, 2, FT, T]), RES_BESIDE_ROUTE, B - RES_BESIDE_ROUTE)
        block = ctx.enter_context(nc.Block())

        @block.scalar
        def _(act):
            res.gelus(act)

        @block.tensor
        def _(pe):
            res.up(pe, 0, 0)
            res.up(pe, 1, 1)
            res.down(pe, 0, 0)
            res.down(pe, 1, 1)

        @block.vector
        def _(dve):
            v = nc.vector
            for b in range(B):
                u = b % 2
                m = b - res.first
                if m >= 0:
                    res.add(dve, m, u)
                    res.blend(dve, m, u)
                    dve.wait_ge(res.x_ok, m + 1)
                if b >= 2:
                    dve.wait_ge(r_ok, b - 1)
                dve.wait_ge(y_in[b], 16)
                for t in range(TB):
                    n = b * TB + t
                    last = v.scalar_tensor_tensor(out=GY[:, u, t, :], in0=Y[:, b, t, :], scalar=k.G0[:, n:n + 1],
                                                  in1=k.gb[:, b, :], op0=ALU.mult, op1=ALU.mult)
                last.then_inc(gy_ok, 1)
                dve.wait_ge(gy_ok, b + 1)
                x = k.X[:, b * TB:b * TB + TB, :]
                v.tensor_tensor(x, GY[:, u], x, ALU.add).then_inc(r_ok, 1)

        @block.sync
        def _(sp):
            y = k.YS[0:NT * P, :].rearrange("(b t p) c -> b p t c", t=TB, p=P)
            for b in range(B):
                sp.dma_start(Y[:, b], y[b]).then_inc(y_in[b], 16)
            o = out.rearrange("b (t p) c -> b p t c", p=P)
            for b in range(B):
                sp.wait_ge(r_ok, b + 1)
                sp.dma_start(o[b], k.X[:, b * TB:b * TB + TB, :]).then_inc(r_out, 16)
            sp.wait_ge(r_out, 16 * B)


def build(nc, a, out):
    k = Tensors()
    k.XS = nc.dram_tensor("sorted_tokens", [NX * P, C + 1], F32).ap()
    k.YS = nc.dram_tensor("expert_outputs", [(NT + NX) * P, C], F32).ap()
    with ExitStack() as ctx:
        def sb(name, shape, dt=F32):
            return ctx.enter_context(nc.sbuf_tensor(name, shape, dt))

        pairs_s = [ctx.enter_context(nc.psum_tensor(f"pair_s{i}", [P, 2, T], F32)) for i in range(2)]
        singles = [ctx.enter_context(nc.psum_tensor(f"bank{i}", [P, T], F32)) for i in range(4)]
        banks = [pairs_s[0][:, 0, :], pairs_s[0][:, 1, :], pairs_s[1][:, 0, :], pairs_s[1][:, 1, :]] + \
                [s[:, :] for s in singles]

        k.X = sb("X", [P, NT, C])
        k.O = sb("O", [P, NT, C])
        k.H2 = sb("H2", [P, NT, C])
        k.gb = sb("gb", [P, B, C])
        k.ident = sb("ident", [P, P])
        k.identb = sb("identb", [P, P], BF16)
        k.cmask = sb("cmask", [P, T])
        k.sac = sb("sac", [P, B])
        k.cac = sb("cac", [P, B])
        k.wq1 = sb("wq1", [P, C])
        k.wk1 = sb("wk1", [P, C])
        k.wv1 = sb("wv1", [P, C])
        k.wo1 = sb("wo1", [P, C])
        k.wq2 = sb("wq2", [P, C])
        k.wk2 = sb("wk2", [P, C])
        k.wv2 = sb("wv2", [P, C])
        k.wo2 = sb("wo2", [P, C])
        k.bv2 = sb("bv2", [P, C])
        k.bo_bc = sb("bo_bc", [P, C])
        k.g2_bc = sb("g2_bc", [P, C])
        k.b2_bc = sb("b2_bc", [P, C])
        k.rb2_bc = sb("rb2_bc", [P, C])
        k.bqk2 = sb("bqk2", [P, 2])
        k.zcol = sb("zcol", [P, 2])
        k.ln1c = sb("ln1c", [P, 2])
        k.eb1T = sb("eb1T", [P, E * FT])
        k.rb1T = sb("rb1T", [P, FT])
        k.gw = sb("gw", [P, E + 2])
        k.cb = sb("cb", [P, E + 2])
        k.rstd = sb("rstd", [P, NT])
        k.nmr = sb("nmr", [P, NT])
        k.six = sb("six", [P, NT, 6])
        k.mv = sb("mv", [P, NT, 2])
        k.ve = sb("ve", [P, NT])
        k.rs = [sb(f"rs{i}", [P, NT]) for i in range(2)]
        k.rsq = sb("rsq", [P, NT])
        k.rvv = sb("rvv", [P, NT])

        with ExitStack() as first:
            def first_sb(name, shape, dt=F32):
                return first.enter_context(nc.sbuf_tensor(name, shape, dt))

            k.BR = first_sb("BR", [P, B, 3, C])
            k.QKS = first_sb("QKS", [P, 6, B * T], BF16)
            k.V = first_sb("V", [P, NT, C])
            k.ST = [first_sb(f"ST{u}", [P, H // 2, 2, T], BF16) for u in range(2)]
            k.VA = first_sb("VA", [P, 2, TB, H, 32])

            load_and_tables(nc, k, a, banks)
            k.stk = [[nc.alloc_semaphore(name=f"rows1_{u}{h}") for h in range(2)] for u in range(2)]
            norm_and_project(nc, k, k.X, k.wq1, k.wk1, k.wv1, k.zcol, k.zcol[:, 0:1].broadcast_to([P, C]),
                             lambda b: k.cac[:, bass.ds(b, 1)], lambda b: k.sac[:, bass.ds(b, 1)],
                             banks, "np1", with_gates=True)
            attention(nc, k, True, pairs_s, banks[4:6], banks[6], banks[7], k.H2, "at1")
            out_project(nc, k, k.wo1, banks, "op1", None, k.X, k.BR[:, :, 0, :])
            modulate(nc, k, k.X, k.H2, lambda b: k.BR[:, bass.ds(b, 1), 2, :],
                     lambda b: k.BR[:, bass.ds(b, 1), 1, :], "mo2")
            k.stk = [[nc.alloc_semaphore(name=f"rows2_{u}{h}") for h in range(2)] for u in range(2)]
            norm_and_project(nc, k, k.H2, k.wq2, k.wk2, k.wv2, k.bqk2, k.bv2,
                             lambda b: k.ln1c[:, 0:1], lambda b: k.ln1c[:, 1:2], banks, "np2")
            attention(nc, k, False, pairs_s, banks[4:6], banks[6], banks[7],
                      k.BR.rearrange("p b j c -> p (b j) c"), "at2")
        out_project(nc, k, k.wo2, banks, "op2", k.bo_bc, k.H2, None)
        k.RM = sb("RM", [P, NT, C])
        k.LG = sb("LG", [P, NT, E + 2])
        k.G0 = sb("G0", [P, NT])
        k.G1 = sb("G1", [P, NT])
        k.W1 = sb("W1", [P, E, F])
        k.W2 = sb("W2", [P, E, FT, C])
        k.EB2 = sb("EB2", [P, E, C])
        k.DI = sb("DI", [P, NT], mybir.dt.uint32)
        k.TE = sb("TE", [P, NX], I32)
        k.XR = sb("XR", [P, NT, C + 1])
        k.XC = sb("XC", [P, B * T])
        k.rw1 = sb("rw1", [P, F])
        k.rw2 = sb("rw2", [P, FT, C])
        k.rw_in = nc.alloc_semaphore(name="rw_in")
        k.ew_in = nc.alloc_semaphore(name="ew_in")
        gate(nc, k, a, banks)
        route(nc, k, banks)
        experts(nc, k, a, banks)
        combine(nc, k, banks, out)


_OUTS = [((B, T, C), "float32")]


def kernel(**inputs):
    import numpy as _np
    import concourse.bacc as _bacc
    from concourse import mybir as _mybir
    from concourse.bass_utils import run_bass_kernel_spmd as _run

    nc = _bacc.Bacc("TRN2", target_bir_lowering=False, num_devices=1)
    arrays, args = {}, {}
    for name in inputs:
        arr = _np.ascontiguousarray(inputs[name])
        arrays[f"in_{name}"] = arr
        args[name] = nc.dram_tensor(f"in_{name}", arr.shape, _mybir.dt.from_np(arr.dtype),
                                    kind="ExternalInput").ap()
    shape, dtype = _OUTS[0]
    out = nc.dram_tensor("out_0", shape, _mybir.dt.from_np(_np.dtype(dtype)), kind="ExternalOutput").ap()
    build(nc, args, out)
    r = _run(nc, [arrays], core_ids=[0])
    return r.results[0]["out_0"]
```
